# Optimizing a Trainium2 kernel written in Bass

```python
import numpy as np
import jax
import jax.numpy as jnp

def _softmax(x, axis=-1):
    return jax.nn.softmax(x, axis=axis)

def _gelu(x):
    return jax.nn.gelu(x, approximate=True)

def _silu(x):
    return jax.nn.silu(x)

def _sigmoid(x):
    return jax.nn.sigmoid(x)

def _layernorm(x, axis=-1, eps=1e-05):
    m = jnp.mean(x, axis=axis, keepdims=True)
    v = jnp.var(x, axis=axis, keepdims=True)
    return (x - m) / jnp.sqrt(v + eps)

def _scatter_add(tgt, idx, src, axis=0):
    return tgt.at[idx].add(src)

def _segment_sum(src, seg, n):
    return jax.ops.segment_sum(src, seg, n)
kernel_name = 'mk_decoder_postln_d1_seqx_r8_1cfecf'

def setup_inputs(seed: int=0):
    np.random.seed(seed)
    _w = jnp.asarray

    def _rec_inputs():
        import jax
        import jax.numpy as jnp
        _rk = jax.random.key(seed)
        x = -0.0002928 + 1 * jax.random.normal(jax.random.fold_in(_rk, 1), (32, 128, 128), jnp.float32)
        _lenS = 128 - jax.random.randint(jax.random.fold_in(_rk, 7), (32,), 0, max(1, 128 // 4) + 1, jnp.int32)
        _lenS2 = 77 - jax.random.randint(jax.random.fold_in(_rk, 8), (32,), 0, max(1, 77 // 4) + 1, jnp.int32)
        _ctx_1024P = jax.random.normal(jax.random.fold_in(_rk, 11), (32, 16, 128), jnp.float32)
        _ctx_1024c = jax.random.dirichlet(jax.random.fold_in(_rk, 511), 0.3 * jnp.ones((16,), jnp.float32), (32, 77))
        _ctx_1024t = jnp.einsum('bsk,bkd->bsd', _ctx_1024c, _ctx_1024P)
        _ctx_1024t = _ctx_1024t * jax.lax.rsqrt(jnp.mean(jnp.square(_ctx_1024t)) + 1e-12) * 0.953939
        ctx_1024 = -1.39393e-06 + 0.999914 * (_ctx_1024t + 0.3 * jax.random.normal(jax.random.fold_in(_rk, 611), (32, 77, 128), jnp.float32))
        fside_BxSxS2_0 = jax.random.uniform(jax.random.fold_in(_rk, 12), (32, 128, 77), jnp.float32, 0.0, 1)
        _validS = jnp.arange(128)[None, :] < _lenS[:, None]
        _validS2 = jnp.arange(77)[None, :] < _lenS2[:, None]
        _causal = jnp.tril(jnp.ones((128, 128), dtype=bool))
        mask_BxSxS2_ik1 = jnp.where(jnp.broadcast_to(_validS2[:, None, :], (32, 128, 77)), 1, 0).astype(jnp.int32)
        return (x, ctx_1024, fside_BxSxS2_0, mask_BxSxS2_ik1)
    x, ctx_1024, fside_BxSxS2_0, mask_BxSxS2_ik1 = _rec_inputs()

    def _L0_attn_setup():
        import jax, jax.numpy as jnp
        import numpy as np
        B, N, E, H = (2, 256, 128, 8)
        HID = 128
        D = HID // H
        EPS = 1e-08

        def rms_norm(x, scale):
            rms = jnp.linalg.norm(x, axis=-1, keepdims=True) * x.shape[-1] ** (-0.5)
            return scale * (x / (rms + EPS))
        key = jax.random.key(seed)
        ks = jax.random.split(key, 12)
        s = 0.02
        return {'x': jax.random.normal(ks[0], (B, N, E), jnp.float32), 'Wq': jax.random.normal(ks[1], (HID, E), jnp.float32) * s, 'bq': jnp.zeros((HID,), jnp.float32), 'Wk': jax.random.normal(ks[2], (HID, E), jnp.float32) * s, 'bk': jnp.zeros((HID,), jnp.float32), 'Wv': jax.random.normal(ks[3], (HID, E), jnp.float32) * s, 'bv': jnp.zeros((HID,), jnp.float32), 'Wu': jax.random.normal(ks[4], (HID, E), jnp.float32) * s, 'bu': jnp.zeros((HID,), jnp.float32), 'Wo': jax.random.normal(ks[5], (E, HID), jnp.float32) * s, 'bo': jnp.zeros((E,), jnp.float32), 'scale': jnp.ones((HID,), jnp.float32)}
    _L0_attn_all = _L0_attn_setup()
    _L0_attn_in = {k: v for k, v in _L0_attn_all.items() if k in ('Wq', 'bq', 'Wk', 'bk', 'Wv', 'bv', 'Wu', 'bu', 'Wo', 'bo', 'scale')}
    del _L0_attn_all

    def _L0_xattn_setup():
        import jax, jax.numpy as jnp
        import numpy as np
        NUM_HEADS = 16
        HIDDEN = 128
        B, S = (2, 256)

        def _split_heads(x, H):
            b, s, d = x.shape
            return x.reshape(b, s, H, d // H).transpose(0, 2, 1, 3)
        key = jax.random.key(seed)
        ks = jax.random.split(key, 14)
        D = HIDDEN
        scale = 1.0 / np.sqrt(D)
        inp = {'query': jax.random.normal(ks[0], (B, S, D), jnp.float32), 'key_in': jax.random.normal(ks[1], (B, S, D), jnp.float32), 'value': jax.random.normal(ks[2], (B, S, D), jnp.float32), 'group_prob': jax.random.uniform(ks[3], (B, S, S), jnp.float32), 'mask': jax.random.randint(ks[4], (B, S, S), 0, 2, jnp.int32), 'wq_k': jax.random.normal(ks[5], (D, D), jnp.float32) * scale, 'wq_b': jnp.zeros((D,), jnp.float32), 'wk_k': jax.random.normal(ks[6], (D, D), jnp.float32) * scale, 'wk_b': jnp.zeros((D,), jnp.float32), 'wv_k': jax.random.normal(ks[7], (D, D), jnp.float32) * scale, 'wv_b': jnp.zeros((D,), jnp.float32), 'wo_k': jax.random.normal(ks[8], (D, D), jnp.float32) * scale, 'wo_b': jnp.zeros((D,), jnp.float32)}
        return inp
    _L0_xattn_all = _L0_xattn_setup()
    _L0_xattn_in = {k: v for k, v in _L0_xattn_all.items() if k in ('wq_k', 'wq_b', 'wk_k', 'wk_b', 'wv_k', 'wv_b', 'wo_k', 'wo_b')}
    del _L0_xattn_all

    def _L0_ffn_setup():
        import jax, jax.numpy as jnp
        import numpy as np
        DIM = 128
        EXPERT_DIM = 64
        N_EXPERTS = 16
        TOPK = 2
        SHARED_HIDDEN = EXPERT_DIM * TOPK
        B, T = (4, 128)

        def _moe_forward(x, router_w, router_bias, up_proj, gate_proj, down_proj, sh_gate, sh_up, sh_down):
            Bb, Tt, D = x.shape
            flat = x.reshape(Bb * Tt, D)
            N = flat.shape[0]
            logits = flat @ router_w.T
            topk_scores, topk_idx = jax.lax.top_k(logits + router_bias, TOPK)
            topk_scores = jax.nn.softmax(topk_scores, axis=-1)
            combine = jnp.zeros((N, N_EXPERTS), flat.dtype)
            combine = combine.at[jnp.arange(N)[:, None], topk_idx].add(topk_scores)
            up_all = jnp.einsum('nd,kde->nke', flat, up_proj)
            gate_all = jnp.einsum('nd,kde->nke', flat, gate_proj)
            hidden = jax.nn.silu(gate_all) * up_all
            down_all = jnp.einsum('nke,ked->nkd', hidden, down_proj)
            out = jnp.einsum('nk,nkd->nd', combine, down_all)
            sh_hidden = jax.nn.silu(flat @ sh_gate.T) * (flat @ sh_up.T)
            out = out + sh_hidden @ sh_down.T
            return out.reshape(Bb, Tt, D)
        key = jax.random.key(seed)
        ks = jax.random.split(key, 9)
        std = 0.02
        return {'x': jax.random.normal(ks[0], (B, T, DIM), jnp.float32), 'router_w': jax.random.normal(ks[1], (N_EXPERTS, DIM), jnp.float32) * std, 'router_bias': jnp.zeros((N_EXPERTS,), jnp.float32), 'up_proj': jax.random.normal(ks[2], (N_EXPERTS, DIM, EXPERT_DIM), jnp.float32) * std, 'gate_proj': jax.random.normal(ks[3], (N_EXPERTS, DIM, EXPERT_DIM), jnp.float32) * std, 'down_proj': jax.random.normal(ks[4], (N_EXPERTS, EXPERT_DIM, DIM), jnp.float32) * std, 'sh_gate': jax.random.normal(ks[5], (SHARED_HIDDEN, DIM), jnp.float32) * std, 'sh_up': jax.random.normal(ks[6], (SHARED_HIDDEN, DIM), jnp.float32) * std, 'sh_down': jax.random.normal(ks[7], (DIM, SHARED_HIDDEN), jnp.float32) * std}
    _L0_ffn_all = _L0_ffn_setup()
    _L0_ffn_in = {k: v for k, v in _L0_ffn_all.items() if k in ('router_w', 'router_bias', 'up_proj', 'gate_proj', 'down_proj', 'sh_gate', 'sh_up', 'sh_down')}
    del _L0_ffn_all
    return {'x': x, 'ctx_1024': ctx_1024, 'fside_BxSxS2_0': fside_BxSxS2_0, 'mask_BxSxS2_ik1': mask_BxSxS2_ik1, 'L0_attn_Wq': _L0_attn_in['Wq'], 'L0_attn_bq': _L0_attn_in['bq'], 'L0_attn_Wk': _L0_attn_in['Wk'], 'L0_attn_bk': _L0_attn_in['bk'], 'L0_attn_Wv': _L0_attn_in['Wv'], 'L0_attn_bv': _L0_attn_in['bv'], 'L0_attn_Wu': _L0_attn_in['Wu'], 'L0_attn_bu': _L0_attn_in['bu'], 'L0_attn_Wo': _L0_attn_in['Wo'], 'L0_attn_bo': _L0_attn_in['bo'], 'L0_attn_scale': _L0_attn_in['scale'], 'L0_xattn_wq_k': _L0_xattn_in['wq_k'], 'L0_xattn_wq_b': _L0_xattn_in['wq_b'], 'L0_xattn_wk_k': _L0_xattn_in['wk_k'], 'L0_xattn_wk_b': _L0_xattn_in['wk_b'], 'L0_xattn_wv_k': _L0_xattn_in['wv_k'], 'L0_xattn_wv_b': _L0_xattn_in['wv_b'], 'L0_xattn_wo_k': _L0_xattn_in['wo_k'], 'L0_xattn_wo_b': _L0_xattn_in['wo_b'], 'L0_ffn_router_w': _L0_ffn_in['router_w'], 'L0_ffn_router_bias': _L0_ffn_in['router_bias'], 'L0_ffn_up_proj': _L0_ffn_in['up_proj'], 'L0_ffn_gate_proj': _L0_ffn_in['gate_proj'], 'L0_ffn_down_proj': _L0_ffn_in['down_proj'], 'L0_ffn_sh_gate': _L0_ffn_in['sh_gate'], 'L0_ffn_sh_up': _L0_ffn_in['sh_up'], 'L0_ffn_sh_down': _L0_ffn_in['sh_down']}

def reference(x, ctx_1024, fside_BxSxS2_0, mask_BxSxS2_ik1, L0_attn_Wq, L0_attn_bq, L0_attn_Wk, L0_attn_bk, L0_attn_Wv, L0_attn_bv, L0_attn_Wu, L0_attn_bu, L0_attn_Wo, L0_attn_bo, L0_attn_scale, L0_xattn_wq_k, L0_xattn_wq_b, L0_xattn_wk_k, L0_xattn_wk_b, L0_xattn_wv_k, L0_xattn_wv_b, L0_xattn_wo_k, L0_xattn_wo_b, L0_ffn_router_w, L0_ffn_router_bias, L0_ffn_up_proj, L0_ffn_gate_proj, L0_ffn_down_proj, L0_ffn_sh_gate, L0_ffn_sh_up, L0_ffn_sh_down):
    import jax
    import jax.numpy as jnp

    def _L0_attn_ref(x, Wq, bq, Wk, bk, Wv, bv, Wu, bu, Wo, bo, scale):
        import jax, jax.numpy as jnp
        import numpy as np
        B, N, E, H = (2, 256, 128, 8)
        HID = 128
        D = HID // H
        EPS = 1e-08

        def rms_norm(x, scale):
            rms = jnp.linalg.norm(x, axis=-1, keepdims=True) * x.shape[-1] ** (-0.5)
            return scale * (x / (rms + EPS))
        n = x.shape[-2]
        q = x @ Wq.T + bq
        u = x @ Wu.T + bu
        k = x @ Wk.T + bk
        v = x @ Wv.T + bv
        u = jax.nn.silu(u)
        v = jax.nn.silu(v)
        to_heads = lambda t: t.reshape(*t.shape[:-1], H, D).swapaxes(-3, -2)
        q, k, v = map(to_heads, (q, k, v))
        q = jax.nn.elu(q)
        k = jax.nn.elu(k)
        mask = jnp.tril(jnp.ones((n, n), q.dtype))
        energy = jnp.einsum('bhnd,bhmd->bhnm', q, k) * mask
        out = jnp.einsum('bhnm,bhmd->bhnd', energy, v)
        out = out.swapaxes(-3, -2).reshape(*x.shape[:-1], HID)
        out = rms_norm(out, scale)
        out = u * out
        return out @ Wo.T + bo

    def _L0_xattn_ref(query, key_in, value, group_prob, mask, wq_k, wq_b, wk_k, wk_b, wv_k, wv_b, wo_k, wo_b):
        import jax, jax.numpy as jnp
        import numpy as np
        NUM_HEADS = 16
        HIDDEN = 128
        B, S = (2, 256)

        def _split_heads(x, H):
            b, s, d = x.shape
            return x.reshape(b, s, H, d // H).transpose(0, 2, 1, 3)
        H = NUM_HEADS
        dh = query.shape[-1] // H
        q = _split_heads(query @ wq_k + wq_b, H)
        k = _split_heads(key_in @ wk_k + wk_b, H)
        v = _split_heads(value @ wv_k + wv_b, H)
        logits = jnp.einsum('bhqd,bhkd->bhqk', q, k) / jnp.sqrt(jnp.asarray(dh, q.dtype))
        neg = (1.0 - mask.astype(q.dtype)) * -1000000000.0
        logits = logits + neg[:, None, :, :]
        attn = jax.nn.softmax(logits, axis=-1)
        attn = attn * group_prob[:, None, :, :]
        out = jnp.einsum('bhqk,bhkd->bhqd', attn, v)
        out = out.transpose(0, 2, 1, 3).reshape(query.shape[0], -1, H * dh)
        return out @ wo_k + wo_b

    def _L0_ffn_ref(x, router_w, router_bias, up_proj, gate_proj, down_proj, sh_gate, sh_up, sh_down):
        import jax, jax.numpy as jnp
        import numpy as np
        DIM = 128
        EXPERT_DIM = 64
        N_EXPERTS = 16
        TOPK = 2
        SHARED_HIDDEN = EXPERT_DIM * TOPK
        B, T = (4, 128)

        def _moe_forward(x, router_w, router_bias, up_proj, gate_proj, down_proj, sh_gate, sh_up, sh_down):
            Bb, Tt, D = x.shape
            flat = x.reshape(Bb * Tt, D)
            N = flat.shape[0]
            logits = flat @ router_w.T
            topk_scores, topk_idx = jax.lax.top_k(logits + router_bias, TOPK)
            topk_scores = jax.nn.softmax(topk_scores, axis=-1)
            combine = jnp.zeros((N, N_EXPERTS), flat.dtype)
            combine = combine.at[jnp.arange(N)[:, None], topk_idx].add(topk_scores)
            up_all = jnp.einsum('nd,kde->nke', flat, up_proj)
            gate_all = jnp.einsum('nd,kde->nke', flat, gate_proj)
            hidden = jax.nn.silu(gate_all) * up_all
            down_all = jnp.einsum('nke,ked->nkd', hidden, down_proj)
            out = jnp.einsum('nk,nkd->nd', combine, down_all)
            sh_hidden = jax.nn.silu(flat @ sh_gate.T) * (flat @ sh_up.T)
            out = out + sh_hidden @ sh_down.T
            return out.reshape(Bb, Tt, D)
        return _moe_forward(x, router_w, router_bias, up_proj, gate_proj, down_proj, sh_gate, sh_up, sh_down)
    x = _layernorm(x + _L0_attn_ref(x, L0_attn_Wq, L0_attn_bq, L0_attn_Wk, L0_attn_bk, L0_attn_Wv, L0_attn_bv, L0_attn_Wu, L0_attn_bu, L0_attn_Wo, L0_attn_bo, L0_attn_scale), axis=-1)
    x = _layernorm(x + _L0_xattn_ref(x, ctx_1024, ctx_1024, fside_BxSxS2_0, mask_BxSxS2_ik1, L0_xattn_wq_k, L0_xattn_wq_b, L0_xattn_wk_k, L0_xattn_wk_b, L0_xattn_wv_k, L0_xattn_wv_b, L0_xattn_wo_k, L0_xattn_wo_b), axis=-1)
    x = _layernorm(x + _L0_ffn_ref(x, L0_ffn_router_w, L0_ffn_router_bias, L0_ffn_up_proj, L0_ffn_gate_proj, L0_ffn_down_proj, L0_ffn_sh_gate, L0_ffn_sh_up, L0_ffn_sh_down), axis=-1)
    return x

_drawn_inputs = setup_inputs


def setup_inputs(seed=0):
    import zlib

    import numpy as np

    out = dict(_drawn_inputs(seed))
    spreads = {'L0_attn_bq': (0.0, 0.677),
     'L0_attn_bk': (0.0, 0.332),
     'L0_attn_bv': (0.0, 0.357),
     'L0_attn_bu': (0.0, 0.618),
     'L0_attn_bo': (0.0, 0.1),
     'L0_attn_scale': (1.0, 0.6),
     'L0_xattn_wq_b': (0.0, 0.69),
     'L0_xattn_wk_b': (0.0, 0.8),
     'L0_xattn_wv_b': (0.0, 0.1),
     'L0_xattn_wo_b': (0.0, 0.1),
     'L0_ffn_router_bias': (0.0, 0.8)}
    factors = {'L0_attn_Wk': 2.811,
     'L0_attn_Wv': 2.772,
     'L0_ffn_router_w': 8.0,
     'L0_ffn_up_proj': 8.0,
     'L0_ffn_gate_proj': 8.0,
     'L0_ffn_down_proj': 8.0,
     'L0_ffn_sh_gate': 8.0,
     'L0_ffn_sh_up': 8.0,
     'L0_ffn_sh_down': 8.0}
    for name, (base, spread) in spreads.items():
        noise = np.random.default_rng([zlib.crc32(name.encode()), seed]).standard_normal(out[name].shape)
        drawn = base * np.exp(spread * noise) if base else spread * noise
        out[name] = jnp.asarray(drawn.astype(out[name].dtype))
    for name, factor in factors.items():
        out[name] = (out[name] * factor).astype(out[name].dtype)
    return out
```

```python
from contextlib import ExitStack

import concourse.bass as bass
from concourse import mybir

F32 = mybir.dt.float32
BF16 = mybir.dt.bfloat16
I32 = mybir.dt.int32
U32 = mybir.dt.uint32
ALU = mybir.AluOpType
ACT = mybir.ActivationFunctionType
X = mybir.AxisListType.X

P = 128
D = 128
GB = 4
T = GB * P
H1, E1 = 8, 16
H2, E2 = 16, 8
NE, FE = 16, 64
NJ = NE * FE // P
NBLK = NJ + 1
MASKED = -1e9
LN_EPS = 1e-5
RMS_EPS = 1e-8
HEADS_OF = [(0, 6), (6, 12), (12, 16)]
NLG = len(HEADS_OF)


def decoder_layer(nc, x, xT, ctxT, gp, mask, wqT, wkT, wuvT, woT, bq, bk, bu, bv, bo, scale,
                  xwq, xbq, xwk, xbk, xwv, xbv, xwo, xbo, routerT, router_b, up, gate, down,
                  sh_gateT, sh_upT, sh_downT, out):
    NB, SK = ctxT.shape[1], ctxT.shape[2]
    NG = NB // GB
    KT = GB * SK

    ctx = ExitStack()
    with ctx:
        def sb(name, shape, dt=F32):
            return ctx.enter_context(nc.sbuf_tensor(name, shape, dt))

        def sem(name):
            return ctx.enter_context(nc.semaphore(name))

        w_qT, w_kT, w_oT = (sb(n, [P, D]) for n in ("w_qT", "w_kT", "w_oT"))
        w_uvT = sb("w_uvT", [P, 2 * D])
        w_xq, w_xk, w_xv, w_xo = (sb(n, [P, D]) for n in ("w_xq", "w_xk", "w_xv", "w_xo"))
        w_routerT = sb("w_routerT", [P, NE])
        w_gate, w_up, w_down = (sb(n, [P, NBLK, P]) for n in ("w_gate", "w_up", "w_down"))
        b_cols = sb("b_cols", [P, 5])
        b_uv = sb("b_uv", [P, 2 * D])
        b_o = sb("b_o", [P, D])
        half_scale = sb("half_scale", [P, D])
        b_xv = sb("b_xv", [P, D])
        b_xo = sb("b_xo", [P, D])
        b_router = sb("b_router", [P, NE])
        ones = sb("ones", [P, D])
        ident = sb("ident", [P, D])
        ident16 = sb("ident16", [P, D], BF16)
        causal = sb("causal", [P, D])
        head_rows1 = sb("head_rows1", [P, H1])
        head_rows2 = sb("head_rows2", [P, H2])
        expert_no = sb("expert_no", [P, NE])
        expert_i = sb("expert_i", [P, NE], I32)
        pick_expert = sb("pick_expert", [3 * NE, NJ, P], BF16)
        half_power = sb("half_power", [P, GB])
        minus_half_power = sb("minus_half_power", [P, GB])

        x_tok = sb("x_tok", [P, GB, D])
        x_T = sb("x_T", [P, T])
        ctx_T = sb("ctx_T", [P, KT])
        gprob = sb("gprob", [P, GB, SK])
        mask_i = sb("mask_i", [P, GB, SK], I32)

        exp_qk = sb("exp_qk", [P, 2, T])
        q1 = sb("q1", [P, T])
        k1 = sb("k1", [P, T])
        q1_heads = sb("q1_heads", [P, 2, H1, P])
        uv = sb("uv", [P, GB, 2 * D])
        tanh_uv = sb("tanh_uv", [P, GB, 2 * D])
        u_scaled = sb("u_scaled", [P, GB, D])
        x_bo = sb("x_bo", [P, GB, D])
        energy = sb("energy", [P, 2, H1, P])
        sq = sb("sq", [P, D])
        sumsq = sb("sumsq", [P, GB])
        rms = sb("rms", [P, GB])
        rms_inv = sb("rms_inv", [P, GB])
        gated = sb("gated", [P, GB, D])
        gated_T = sb("gated_T", [P, T])
        y1 = sb("y1", [P, GB, D])
        x1 = sb("x1", [P, GB, D])
        x1_bo = sb("x1_bo", [P, GB, D])
        x1_T = sb("x1_T", [P, T])
        stats = sb("stats", [P, GB, 6])
        moments = sb("moments", [P, GB, 2])
        var_eps = sb("var_eps", [P, GB])
        rstd = sb("rstd", [P, GB])

        neg = sb("neg", [P, GB, SK])
        q2_T = sb("q2_T", [P, T])
        k2_T = sb("k2_T", [P, KT])
        k2_heads = sb("k2_heads", [P, GB, H2, SK])
        v2 = sb("v2", [SK, GB, D])
        logit = sb("logit", [P, 2, H2, SK])
        shifted = sb("shifted", [P, 2, H2, SK])
        neg_max = sb("neg_max", [P, 2, H2])
        prob_sum = sb("prob_sum", [P, GB, H2])
        prob_inv = sb("prob_inv", [P, GB, H2])
        prob_T = sb("prob_T", [SK, 2, H2, P])
        att2 = sb("att2", [P, GB, D])
        att2_T = sb("att2_T", [P, T])
        y2 = sb("y2", [P, GB, D])
        x2 = sb("x2", [P, GB, D])
        x2_T = sb("x2_T", [P, T])

        score = sb("score", [P, GB, NE])
        top8 = sb("top8", [P, GB, 8])
        top_i = sb("top_i", [P, GB, 8], U32)
        top_f = sb("top_f", [P, GB, 8])
        gap = sb("gap", [P, GB])
        exp_gap = sb("exp_gap", [P, GB])
        wait_column = sb("wait_column", [P, 1])
        one_plus = sb("one_plus", [P, GB])
        w_top = sb("w_top", [P, 2, GB])
        hit = sb("hit", [P, 2, GB, NE])
        comb_2 = sb("comb_2", [P, 2, GB, NE])
        combine = sb("combine", [P, 3, GB, NE])
        comb_parts = sb("comb_parts", [P, GB, 3, NE], BF16)
        comb_T = sb("comb_T", [3 * NE, T], BF16)
        weight_rows = sb("weight_rows", [P, NJ, T])
        tanh_g = sb("tanh_g", [P, 2, T])
        silu_g = sb("silu_g", [P, 2, T])
        hidden = sb("hidden", [P, 2, T])
        hidden_w = sb("hidden_w", [P, 2, T])
        moe_T = sb("moe_T", [P, T])
        y3 = sb("y3", [P, GB, D])
        y_out = sb("y_out", [P, GB, D])
        stats3 = sb("stats3", [P, GB, 6])
        moments3 = sb("moments3", [P, GB, 2])
        var_eps3 = sb("var_eps3", [P, GB])
        rstd3 = sb("rstd3", [P, GB])

        A = [ctx.enter_context(nc.psum_tensor(f"bank_a{n}", [P, T], F32)) for n in range(5)]
        G, U, O = (ctx.enter_context(nc.psum_tensor(n, [P, T], F32)) for n in ("bank_g", "bank_u", "bank_o"))
        A4 = [a[:, :].rearrange("p (b d) -> p b d", b=GB) for a in A]
        G4 = G[:, :].rearrange("p (b d) -> p b d", b=GB)

        weights_in = sem("weights_in")
        consts_pool = sem("consts_pool")
        pick_ready = sem("pick_ready")
        consts_dve = sem("consts_dve")
        q_bias_ready = sem("q_bias_ready")
        waited = sem("waited")
        x_T_in, x_in, ctx_in, gp_in, mask_in = (sem(n) for n in ("x_T_in", "x_in", "ctx_in", "gp_in", "mask_in"))
        out_written = sem("out_written")
        qk1_done, uv_done, k2_done, v2_done = (sem(n) for n in ("qk1_done", "uv_done", "k2_done", "v2_done"))
        energy_done, pv1_done, gT_done, proj1_done = (
            sem(n) for n in ("energy_done", "pv1_done", "gT_done", "proj1_done"))
        x1T_done, q2_done, logits_done, probT_done, pv2_done = (
            sem(n) for n in ("x1T_done", "q2_done", "logits_done", "probT_done", "pv2_done"))
        aT_done, proj2_done, x2T_done = (sem(n) for n in ("aT_done", "proj2_done", "x2T_done"))
        router_done, combT_done, rows_done, gu_done, down_done, moe_back = (
            sem(n) for n in ("router_done", "combT_done", "rows_done", "gu_done", "down_done", "moe_back"))
        exp_qk_ready, tanh_uv_ready, k2_ready, sumsq_ready, gT_ready, x1T_ready, q2_ready = (
            sem(n) for n in ("exp_qk_ready", "tanh_uv_ready", "k2_ready", "sumsq_ready", "gT_ready",
                             "x1T_ready", "q2_ready"))
        exp2_ready, probT_ready, aT_ready, x2T_ready = (
            sem(n) for n in ("exp2_ready", "probT_ready", "aT_ready", "x2T_ready"))
        exp_gap_ready, combT_ready, rows_ready, tanh_g_ready, moeT_ready = (
            sem(n) for n in ("exp_gap_ready", "combT_ready", "rows_ready", "tanh_g_ready", "moeT_ready"))
        qk1_ready, uv_biased, uv_ready, v2_ready, energy_ready = (
            sem(n) for n in ("qk1_ready", "uv_biased", "uv_ready", "v2_ready", "energy_ready"))
        elu_part, rms_eps_added, rms_inv_ready, gated_ready, y1_ready, mom1_ready, x1_ready = (
            sem(n) for n in ("elu_part", "rms_eps_added", "rms_inv_ready", "gated_ready", "y1_ready",
                             "mom1_ready", "x1_ready"))
        neg_ready, logit_ready, max_ready, sum_ready, inv_ready, att2_ready = (
            sem(n) for n in ("neg_ready", "logit_ready", "max_ready", "sum_ready", "inv_ready", "att2_ready"))
        y2_ready, mom2_ready, x2_ready, split_step = (
            sem(n) for n in ("y2_ready", "mom2_ready", "x2_ready", "split_step"))
        route_step, gap_ready, parts_ready, silu_ready, hidden_ready, y3_ready, mom3_ready, out_ready = (
            sem(n) for n in ("route_step", "gap_ready", "parts_ready", "silu_ready", "hidden_ready",
                             "y3_ready", "mom3_ready", "out_ready"))
        q1_heads_ready, u_scaled_ready, x_bo_ready, rms_ready, rstd1_ready, x1_bo_ready = (
            sem(n) for n in ("q1_heads_ready", "u_scaled_ready", "x_bo_ready", "rms_ready", "rstd1_ready",
                             "x1_bo_ready"))
        k2_heads_ready, shifted_ready, prob_ready, rstd2_ready, hidden_w_ready, rstd3_ready = (
            sem(n) for n in ("k2_heads_ready", "shifted_ready", "prob_ready", "rstd2_ready",
                             "hidden_w_ready", "rstd3_ready"))

        def at(i, per, k):
            count = i * per + k
            return max(count, 0) if isinstance(count, int) else count

        def heads_of(ap, n, h, e):
            return ap.unsqueeze(2).broadcast_to([n, h, e])

        loads = [
            (w_qT[:, :], wqT), (w_kT[:, :], wkT), (w_uvT[:, :], wuvT), (w_oT[:, :], woT),
            (w_xq[:, :], xwq), (w_xk[:, :], xwk), (w_xv[:, :], xwv), (w_xo[:, :], xwo),
            (w_routerT[:, :], routerT),
            (w_gate[:, 0:NJ, :].rearrange("p j (t e) -> p (j t) e", e=FE), gate.rearrange("k d e -> d k e")),
            (w_up[:, 0:NJ, :].rearrange("p j (t e) -> p (j t) e", e=FE), up.rearrange("k d e -> d k e")),
            (w_down[:, 0:NJ, :], down.rearrange("(j t) e d -> (t e) j d", t=2)),
            (w_gate[:, NJ, :], sh_gateT), (w_up[:, NJ, :], sh_upT), (w_down[:, NJ, :], sh_downT),
            (b_cols[:, 0:1], bq.unsqueeze(1)), (b_cols[:, 1:2], bk.unsqueeze(1)),
            (b_cols[:, 2:3], xbq.unsqueeze(1)), (b_cols[:, 3:4], xbk.unsqueeze(1)),
            (b_uv[:, 0:D], bu.partition_broadcast(P)), (b_uv[:, D:2 * D], bv.partition_broadcast(P)),
            (b_o[:, :], bo.partition_broadcast(P)), (half_scale[:, :], scale.partition_broadcast(P)),
            (b_xv[:, :], xbv.partition_broadcast(P)), (b_xo[:, :], xbo.partition_broadcast(P)),
            (b_router[:, :], router_b.partition_broadcast(P)),
        ]
        ALL_WEIGHTS = 16 * len(loads)

        block = ctx.enter_context(nc.Block())

        @block.sync
        def _(sp):
            def load_group(i):
                sp.wait_ge(uv_done, at(i, 2, 0))
                sp.dma_start(x_T[:, :], xT[:, bass.ds(i * T, T)]).then_inc(x_T_in, 16)
                sp.wait_ge(x_bo_ready, at(i, 1, 0))
                sp.dma_start(x_tok[:, :, :], x[bass.ds(i * GB, GB)].rearrange("b p d -> p b d"))\
                  .then_inc(x_in, 16)
                sp.wait_ge(v2_done, at(i, 1, 0))
                sp.wait_ge(k2_done, at(i, 1, 0))
                sp.dma_start(ctx_T[:, :], ctxT[:, bass.ds(i * GB, GB), :].rearrange("p b k -> p (b k)"))\
                  .then_inc(ctx_in, 16)
                sp.wait_ge(neg_ready, at(i, 1, 0))
                sp.dma_start(mask_i[:, :, :], mask[bass.ds(i * GB, GB)].rearrange("b p k -> p b k"))\
                  .then_inc(mask_in, 16)

            def load_gprob(i):
                sp.wait_ge(prob_ready, at(i, GB, 0))
                sp.dma_start(gprob[:, :, :], gp[bass.ds(i * GB, GB)].rearrange("b p k -> p b k"))\
                  .then_inc(gp_in, 16)

            def store_group(i):
                sp.wait_ge(out_ready, at(i, GB, GB))
                sp.dma_start(out[bass.ds(i * GB, GB)].rearrange("b p d -> p b d"), y_out[:, :, :])\
                  .then_inc(out_written, 16)

            for dst, src in loads[:3]:
                sp.dma_start(dst, src).then_inc(weights_in, 16)
            load_group(0)
            for dst, src in loads[3:]:
                sp.dma_start(dst, src).then_inc(weights_in, 16)
            load_gprob(0)
            load_group(1)
            load_gprob(1)
            with sp.Fori(1, NG - 1) as i:
                load_group(i + 1)
                store_group(i - 1)
                load_gprob(i + 1)
            store_group(NG - 2)
            store_group(NG - 1)
            sp.wait_ge(out_written, 16 * NG)

        @block.tensor
        def _(pe):
            def router(i):
                pe.wait_ge(x2T_ready, at(i, 1, 1))
                pe.wait_ge(y3_ready, at(i, 1, 0))
                for b in range(GB):
                    mm = pe.matmul(G[:, NE * b:NE * b + NE], x2_T[:, P * b:P * b + P], w_routerT[:, :],
                                   start=True, stop=True)
                mm.then_inc(router_done, 1)

            def combine_transpose(i):
                pe.wait_ge(pick_ready, 3)
                pe.wait_ge(parts_ready, at(i, 1, 1))
                pe.wait_ge(moeT_ready, at(i, 1, 0))
                view = O[:, :].bitcast(BF16)
                for b in range(GB):
                    mm = pe.transpose(view[0:3 * NE, P * b:P * b + P],
                                      comb_parts[:, b, :, :].rearrange("p s e -> p (s e)"), ident16[:, :])
                mm.then_inc(combT_done, 1)

            def combine_rows(i):
                pe.wait_ge(combT_ready, at(i, 1, 1))
                for j in range(NJ):
                    if j >= 2:
                        pe.wait_ge(rows_ready, at(i, NJ, j - 1))
                    elif j == 1:
                        pe.wait_ge(hidden_ready, at(i, NBLK, 0))
                    else:
                        pe.wait_ge(gap_ready, at(i, 1, 1))
                    pe.matmul((G, U)[j % 2][:, :], pick_expert[:, j, :], comb_T[:, :], start=True, stop=True)\
                      .then_inc(rows_done, 1)

            def gate_up(i, j):
                if j == 0:
                    pe.wait_ge(rows_ready, at(i, NJ, NJ))
                else:
                    pe.wait_ge(silu_ready, at(i, NBLK, j))
                pe.matmul(G[:, :], w_gate[:, j, :], x2_T[:, :], start=True, stop=True).then_inc(gu_done, 1)
                if j > 0:
                    pe.wait_ge(hidden_ready, at(i, NBLK, j))
                pe.matmul(U[:, :], w_up[:, j, :], x2_T[:, :], start=True, stop=True).then_inc(gu_done, 1)

            def expert_down(i, j):
                if j < NJ:
                    pe.wait_ge(hidden_w_ready, at(i, NJ, j + 1))
                else:
                    pe.wait_ge(hidden_ready, at(i, NBLK, NBLK))
                h = hidden_w if j < NJ else hidden
                if j == 0:
                    pe.wait_ge(combT_ready, at(i, 1, 1))
                pe.matmul(O[:, :], w_down[:, j, :], h[:, j % 2, :], start=(j == 0), stop=(j == NBLK - 1))\
                  .then_inc(down_done, 1)

            def moe_transpose(i):
                pe.wait_ge(moeT_ready, at(i, 1, 1))
                pe.wait_ge(silu_ready, at(i, NBLK, NBLK))
                for b in range(GB):
                    mm = pe.transpose(G[:, P * b:P * b + P], moe_T[:, P * b:P * b + P], ident[:, :])
                mm.then_inc(moe_back, 1)

            def project_first(i):
                pe.wait_ge(x_T_in, at(i, 16, 16))
                pe.wait_ge(y2_ready, at(i, 1, 0))
                pe.matmul(A[0][:, :], w_qT[:, :], x_T[:, :], start=True, stop=True).then_inc(qk1_done, 1)
                pe.wait_ge(x2T_ready, at(i, 1, 0))
                pe.matmul(A[1][:, :], w_kT[:, :], x_T[:, :], start=True, stop=True).then_inc(qk1_done, 1)
                pe.wait_ge(att2_ready, at(i, 1, 0))
                pe.wait_ge(aT_ready, at(i, 1, 0))
                for c in range(2):
                    for b in range(2 * c, 2 * c + 2):
                        o = 2 * D * (b % 2)
                        mm = pe.matmul(A[2 + c][:, o:o + 2 * D], x_T[:, P * b:P * b + P], w_uvT[:, :],
                                       start=True, stop=True)
                    mm.then_inc(uv_done, 1)

            def context_keys(i):
                pe.wait_ge(ctx_in, at(i, 16, 16))
                pe.wait_ge(probT_ready, at(i, 4 * GB, 0))
                pe.matmul(A[4][:, 0:KT], w_xk[:, :], ctx_T[:, :], start=True, stop=True).then_inc(k2_done, 1)

            def energies(i, b):
                pe.wait_ge(q1_heads_ready, at(i, GB, b + 1))
                for c in range(2):
                    if b == 0:
                        pe.wait_ge(qk1_ready, at(i, 2, c + 1))
                        if c == 0:
                            pe.wait_ge(qk1_ready, at(i, 2, 2))
                    else:
                        pe.wait_ge(energy_ready, at(i, 2 * GB, 2 * (b - 1) + c + 1))
                    pe.matmul(A[c][:, :], k1[:, P * b:P * b + P],
                              q1_heads[:, b % 2, 4 * c:4 * c + 4, :].rearrange("p h n -> p (h n)"),
                              start=True, stop=True).then_inc(energy_done, 1)

            def values_first(i, b):
                pe.wait_ge(energy_ready, at(i, 2 * GB, 2 * b + 2))
                if b == 0:
                    pe.wait_ge(uv_ready, at(i, 1, 1))
                for h in range(H1):
                    o = D * b + E1 * h
                    mm = pe.matmul(A[2][:, o:o + E1], energy[:, b % 2, h, :],
                                   uv[:, b, D + E1 * h:D + E1 * h + E1], start=True, stop=True)
                mm.then_inc(pv1_done, 1)

            def context_values(i):
                pe.wait_ge(uv_biased, at(i, 2, 2))
                for b in range(GB):
                    mm = pe.matmul(A[3][0:SK, P * b:P * b + P], ctx_T[:, SK * b:SK * b + SK], w_xv[:, :],
                                   start=True, stop=True)
                mm.then_inc(v2_done, 1)

            def gated_transpose(i):
                pe.wait_ge(gated_ready, at(i, GB, GB))
                pe.wait_ge(k2_ready, at(i, 1, 1))
                for b in range(GB):
                    mm = pe.transpose(A[4][:, P * b:P * b + P], gated[:, b, :], ident[:, :])
                mm.then_inc(gT_done, 1)

            def output_first(i):
                pe.wait_ge(gT_ready, at(i, 1, 1))
                pe.wait_ge(energy_ready, at(i, 2 * GB, 2 * GB))
                for b in range(GB):
                    mm = pe.matmul(A[0][:, P * b:P * b + P], gated_T[:, P * b:P * b + P], w_oT[:, :],
                                   start=True, stop=True)
                mm.then_inc(proj1_done, 1)

            def x1_transpose(i):
                pe.wait_ge(x1_ready, at(i, GB, GB))
                for b in range(GB):
                    mm = pe.transpose(A[1][:, P * b:P * b + P], x1[:, b, :], ident[:, :])
                mm.then_inc(x1T_done, 1)

            def queries_second(i):
                pe.wait_ge(x1T_ready, at(i, 1, 1))
                pe.wait_ge(gated_ready, at(i, GB, GB))
                pe.matmul(A[2][:, :], w_xq[:, :], x1_T[:, :], start=True, stop=True).then_inc(q2_done, 1)

            def logits(i, b):
                if b == 0:
                    pe.wait_ge(q2_ready, at(i, 1, 1))
                    pe.wait_ge(y1_ready, at(i, 1, 1))
                pe.wait_ge(k2_heads_ready, at(i, GB, b + 1))
                for g, (h0, h1) in enumerate(HEADS_OF):
                    n = NLG * b + g
                    if n >= 2:
                        pe.wait_ge(logit_ready, at(i, NLG * GB, n - 1))
                    pe.matmul(A[n % 2][:, 0:SK * (h1 - h0)], q2_T[:, P * b:P * b + P],
                              k2_heads[:, b, h0:h1, :].rearrange("p h k -> p (h k)"),
                              start=True, stop=True).then_inc(logits_done, 1)

            def values_second(i, b):
                pe.wait_ge(prob_ready, at(i, GB, b + 1))

                def transposes(c):
                    n = 4 * b + c
                    if n == 0:
                        pe.wait_ge(v2_ready, at(i, 1, 1))
                    elif n == 1:
                        pe.wait_ge(gT_ready, at(i, 1, 1))
                    else:
                        pe.wait_ge(probT_ready, at(i, 4 * GB, n - 1))
                    for h in range(4 * c, 4 * c + 4):
                        mm = pe.transpose(A[3 + n % 2][0:SK, P * (h % 4):P * (h % 4) + P],
                                          shifted[:, b % 2, h, :], ident[:, :])
                    mm.then_inc(probT_done, 1)

                def products(c):
                    pe.wait_ge(probT_ready, at(i, 4 * GB, 4 * b + c + 1))
                    if b == 0 and c == 0:
                        pe.wait_ge(q2_ready, at(i, 1, 1))
                        pe.wait_ge(v2_ready, at(i, 1, 1))
                    for h in range(4 * c, 4 * c + 4):
                        o = D * b + E2 * h
                        mm = pe.matmul(A[2][:, o:o + E2], prob_T[:, b % 2, h, :],
                                       v2[:, b, E2 * h:E2 * h + E2], start=True, stop=True)
                    mm.then_inc(pv2_done, 1)

                transposes(0)
                transposes(1)
                products(0)
                transposes(2)
                products(1)
                transposes(3)
                products(2)
                products(3)

            def att2_transpose(i):
                pe.wait_ge(att2_ready, at(i, 1, 1))
                pe.wait_ge(probT_ready, at(i, 4 * GB, 4 * GB))
                for b in range(GB):
                    mm = pe.transpose(A[3][:, P * b:P * b + P], att2[:, b, :], ident[:, :])
                mm.then_inc(aT_done, 1)

            def output_second(i):
                pe.wait_ge(aT_ready, at(i, 1, 1))
                pe.wait_ge(logit_ready, at(i, NLG * GB, NLG * GB))
                for b in range(GB):
                    mm = pe.matmul(A[0][:, P * b:P * b + P], att2_T[:, P * b:P * b + P], w_xo[:, :],
                                   start=True, stop=True)
                mm.then_inc(proj2_done, 1)

            def x2_transpose(i):
                pe.wait_ge(x2_ready, at(i, GB, GB))
                for b in range(GB):
                    mm = pe.transpose(A[1][:, P * b:P * b + P], x2[:, b, :], ident[:, :])
                mm.then_inc(x2T_done, 1)

            def turn(i, attend, route):
                m = i - 1
                if route:
                    router(m)
                if attend:
                    project_first(i)
                    context_keys(i)
                if route:
                    combine_transpose(m)
                    combine_rows(m)
                if attend:
                    energies(i, 0)
                if route:
                    gate_up(m, 0)
                if attend:
                    energies(i, 1)
                    values_first(i, 0)
                if route:
                    gate_up(m, 1)
                    expert_down(m, 0)
                if attend:
                    energies(i, 2)
                    values_first(i, 1)
                if route:
                    gate_up(m, 2)
                    expert_down(m, 1)
                if attend:
                    energies(i, 3)
                    values_first(i, 2)
                if route:
                    gate_up(m, 3)
                    expert_down(m, 2)
                if attend:
                    values_first(i, 3)
                    context_values(i)
                if route:
                    gate_up(m, 4)
                    expert_down(m, 3)
                if attend:
                    gated_transpose(i)
                if route:
                    gate_up(m, 5)
                if attend:
                    output_first(i)
                if route:
                    expert_down(m, 4)
                    gate_up(m, 6)
                if attend:
                    x1_transpose(i)
                if route:
                    expert_down(m, 5)
                if attend:
                    queries_second(i)
                if route:
                    gate_up(m, 7)
                if attend:
                    logits(i, 0)
                if route:
                    expert_down(m, 6)
                if attend:
                    logits(i, 1)
                if route:
                    gate_up(m, 8)
                    expert_down(m, 7)
                if attend:
                    values_second(i, 0)
                    logits(i, 2)
                if route:
                    expert_down(m, 8)
                if attend:
                    values_second(i, 1)
                    logits(i, 3)
                if route:
                    moe_transpose(m)
                if attend:
                    values_second(i, 2)
                    values_second(i, 3)
                    att2_transpose(i)
                    output_second(i)
                    x2_transpose(i)

            pe.wait_ge(weights_in, ALL_WEIGHTS)
            pe.wait_ge(consts_pool, 12)
            pe.wait_ge(pick_ready, 3)
            turn(0, True, False)
            turn(1, True, True)
            with pe.Fori(2, NG) as i:
                turn(i, True, True)
            turn(NG, False, True)

        @block.scalar
        def _(act):
            def q_bias():
                act.wait_ge(weights_in, ALL_WEIGHTS)
                act.mul(b_cols[:, 4:5], b_cols[:, 2:3], E2 ** -0.5).then_inc(q_bias_ready, 1)
                act.wait_ge(q_bias_ready, 1)

            def exp_first(i):
                act.wait_ge(qk1_ready, at(i, 2, 0))
                for c in range(2):
                    act.wait_ge(qk1_done, at(i, 2, c + 1))
                    act.activation(exp_qk[:, c, :], A[c][:, :], ACT.Exp, bias=b_cols[:, c:c + 1])\
                       .then_inc(exp_qk_ready, 1)

            def keys_second(i):
                act.wait_ge(k2_done, at(i, 1, 1))
                act.wait_ge(k2_heads_ready, at(i, GB, 0))
                act.activation(k2_T[:, :], A[4][:, 0:KT], ACT.Identity, bias=b_cols[:, 3:4])\
                   .then_inc(k2_ready, 1)

            def tanh_first(i):
                for c in range(2):
                    act.wait_ge(uv_biased, at(i, 2, c + 1))
                    act.activation(tanh_uv[:, 2 * c:2 * c + 2, :], uv[:, 2 * c:2 * c + 2, :], ACT.Tanh, scale=0.5)\
                       .then_inc(tanh_uv_ready, 1)

            def squares(i):
                act.wait_ge(pv1_done, at(i, GB, GB))
                for b in range(GB):
                    if b:
                        act.wait_ge(sumsq_ready, at(i, GB, b))
                    act.activation(sq[:, :], A4[2][:, b, :], ACT.Square, scale=D ** -0.5, accum_out=sumsq[:, b:b + 1])\
                       .then_inc(sumsq_ready, 1)

            def copy(i, done, bank, dst, ready):
                act.wait_ge(done, at(i, 1, 1))
                act.activation(dst[:, :], bank[:, :], ACT.Copy).then_inc(ready, 1)

            def queries(i):
                act.wait_ge(q2_done, at(i, 1, 1))
                act.activation(q2_T[:, :], A[2][:, :], ACT.Identity, bias=b_cols[:, 4:5], scale=E2 ** -0.5)\
                   .then_inc(q2_ready, 1)

            def exp_second(i, b):
                act.wait_ge(shifted_ready, at(i, GB, b + 1))
                act.activation(logit[:, b % 2, :, :], shifted[:, b % 2, :, :], ACT.Exp).then_inc(exp2_ready, 1)

            def copy_probs(i, b):
                for c in range(4):
                    act.wait_ge(probT_done, at(i, 4 * GB, 4 * b + c + 1))
                    act.wait_ge(pv2_done, at(i, 4 * GB, 4 * (b - 2) + c + 1))
                    act.activation(prob_T[:, b % 2, 4 * c:4 * c + 4, :].rearrange("k h p -> k (h p)"),
                                   A[3 + c % 2][0:SK, :], ACT.Copy).then_inc(probT_ready, 1)

            def exp_gap_of(i):
                act.wait_ge(gap_ready, at(i, 1, 1))
                act.activation(exp_gap[:, :], gap[:, :], ACT.Exp).then_inc(exp_gap_ready, 1)

            def combine_rows(i):
                act.wait_ge(combT_done, at(i, 1, 1))
                act.activation(comb_T[:, :], O[:, :].bitcast(BF16)[0:3 * NE, 0:T], ACT.Copy)\
                   .then_inc(combT_ready, 1)
                for j in range(NJ):
                    act.wait_ge(rows_done, at(i, NJ, j + 1))
                    act.activation(weight_rows[:, j, :], (G, U)[j % 2][:, :], ACT.Copy).then_inc(rows_ready, 1)

            def tanh_gate(i, j):
                act.wait_ge(gu_done, at(i, 2 * NBLK, 2 * j + 1))
                act.wait_ge(silu_ready, at(i, NBLK, j - 1 if j >= 2 else 0))
                act.activation(tanh_g[:, j % 2, :], G[:, :], ACT.Tanh, scale=0.5).then_inc(tanh_g_ready, 1)

            def moe_out(i):
                act.wait_ge(down_done, at(i, NBLK, NBLK))
                act.activation(moe_T[:, :], O[:, :], ACT.Copy, scale=0.5).then_inc(moeT_ready, 1)

            def turn(i, attend, route):
                m = i - 1
                if route:
                    exp_gap_of(m)
                if attend:
                    exp_first(i)
                    tanh_first(i)
                    keys_second(i)
                if route:
                    combine_rows(m)
                    tanh_gate(m, 0)
                    tanh_gate(m, 1)
                    tanh_gate(m, 2)
                    tanh_gate(m, 3)
                if attend:
                    squares(i)
                if route:
                    tanh_gate(m, 4)
                if attend:
                    copy(i, gT_done, A[4], gated_T, gT_ready)
                if route:
                    tanh_gate(m, 5)
                    tanh_gate(m, 6)
                if attend:
                    copy(i, x1T_done, A[1], x1_T, x1T_ready)
                    queries(i)
                if route:
                    tanh_gate(m, 7)
                if attend:
                    exp_second(i, 0)
                if route:
                    tanh_gate(m, 8)
                if attend:
                    exp_second(i, 1)
                    copy_probs(i, 0)
                if route:
                    moe_out(m)
                if attend:
                    exp_second(i, 2)
                    copy_probs(i, 1)
                    exp_second(i, 3)
                    copy_probs(i, 2)
                    copy_probs(i, 3)
                    copy(i, aT_done, A[3], att2_T, aT_ready)
                    act.wait_ge(gu_done, at(i, 2 * NBLK, 0))
                    copy(i, x2T_done, A[1], x2_T, x2T_ready)

            q_bias()
            turn(0, True, False)
            turn(1, True, True)
            with act.Fori(2, NG) as i:
                turn(i, True, True)
            turn(NG, False, True)

        @block.vector
        def _(dve):
            def wait_carrier():
                dve.tensor_copy(wait_column[:, :], ones[:, 0:1]).then_inc(waited, 1)

            def route(i):
                dve.wait_ge(router_done, at(i, 1, 1))
                gs = G[:, 0:GB * NE].rearrange("p (b e) -> p b e", b=GB)
                dve.tensor_tensor(score[:, :, :], gs, b_router[:, :].unsqueeze(1).broadcast_to([P, GB, NE]),
                                  ALU.add).then_inc(route_step, 1)
                dve.wait_ge(route_step, at(i, 10, 1))
                wait_carrier()
                for b in range(GB):
                    mx = dve.max(top8[:, b, :], score[:, b, :])
                mx.then_inc(route_step, 1)
                dve.wait_ge(route_step, at(i, 10, 2))
                dve.tensor_tensor(gap[:, :], top8[:, :, 1], top8[:, :, 0], ALU.subtract).then_inc(gap_ready, 1)
                for b in range(GB):
                    mx = dve.max_index(top_i[:, b, :], top8[:, b, :], score[:, b, :])
                mx.then_inc(route_step, 1)
                dve.wait_ge(route_step, at(i, 10, 3))
                dve.tensor_copy(top_f[:, :, :], top_i[:, :, :]).then_inc(route_step, 1)
                dve.wait_ge(route_step, at(i, 10, 4))
                experts = expert_no[:, :].unsqueeze(1).broadcast_to([P, GB, NE])
                for r in range(2):
                    hits = dve.tensor_tensor(hit[:, r, :, :], experts, heads_of(top_f[:, :, r], P, GB, NE),
                                             ALU.is_equal)
                hits.then_inc(route_step, 1)
                dve.wait_ge(exp_gap_ready, at(i, 1, 1))
                dve.tensor_scalar(one_plus[:, :], exp_gap[:, :], 1.0, None, ALU.add).then_inc(route_step, 1)
                dve.wait_ge(route_step, at(i, 10, 6))
                dve.reciprocal(w_top[:, 0, :], one_plus[:, :]).then_inc(route_step, 1)
                dve.wait_ge(route_step, at(i, 10, 7))
                dve.tensor_tensor(w_top[:, 1, :], exp_gap[:, :], w_top[:, 0, :], ALU.mult).then_inc(route_step, 1)
                dve.wait_ge(route_step, at(i, 10, 8))
                for r in range(2):
                    w = dve.tensor_tensor(comb_2[:, r, :, :], hit[:, r, :, :],
                                          heads_of(w_top[:, r, :], P, GB, NE), ALU.mult)
                w.then_inc(route_step, 1)
                dve.wait_ge(route_step, at(i, 10, 9))
                dve.tensor_tensor(combine[:, 0, :, :], comb_2[:, 0, :, :], comb_2[:, 1, :, :], ALU.add)\
                   .then_inc(route_step, 1)
                dve.wait_ge(route_step, at(i, 10, 10))

            def combine_split(i):
                dve.wait_ge(combT_done, at(i, 1, 0))
                for s in range(2):
                    dve.tensor_copy(comb_parts[:, :, s, :], combine[:, s, :, :]).then_inc(split_step, 1)
                    dve.wait_ge(split_step, at(i, 4, 2 * s + 1))
                    dve.tensor_tensor(combine[:, s + 1, :, :], combine[:, s, :, :], comb_parts[:, :, s, :],
                                      ALU.subtract).then_inc(split_step, 1)
                    dve.wait_ge(split_step, at(i, 4, 2 * s + 2))
                dve.tensor_copy(comb_parts[:, :, 2, :], combine[:, 2, :, :]).then_inc(parts_ready, 1)

            def elu(i):
                dve.wait_ge(q1_heads_ready, at(i, GB, 0))
                dve.wait_ge(energy_done, at(i, 2 * GB, 0))
                for c, z in enumerate((q1, k1)):
                    dve.wait_ge(exp_qk_ready, at(i, 2, c + 1))
                    dve.tensor_scalar(exp_qk[:, c, :], exp_qk[:, c, :], 1.0, -1.0, ALU.min, ALU.add)\
                       .then_inc(elu_part, 1)
                    dve.wait_ge(elu_part, at(i, 2, c + 1))
                    dve.scalar_tensor_tensor(out=z[:, :], in0=A[c][:, :], scalar=b_cols[:, c:c + 1],
                                             in1=exp_qk[:, c, :], op0=ALU.add, op1=ALU.max)\
                       .then_inc(qk1_ready, 1)

            def add_uv_bias(i):
                dve.wait_ge(u_scaled_ready, at(i, 1, 0))
                dve.wait_ge(pv1_done, at(i, GB, 0))
                for c in range(2):
                    dve.wait_ge(uv_done, at(i, 2, c + 1))
                    dve.tensor_tensor(uv[:, 2 * c:2 * c + 2, :],
                                      A[2 + c][:, :].rearrange("p (b n) -> p b n", b=2),
                                      b_uv[:, :].unsqueeze(1).broadcast_to([P, 2, 2 * D]),
                                      ALU.add).then_inc(uv_biased, 1)

            def silu_uv(i):
                dve.wait_ge(tanh_uv_ready, at(i, 2, 2))
                uvf = uv[:, :, :].rearrange("p b n -> p (b n)")
                dve.scalar_tensor_tensor(out=uvf, in0=tanh_uv[:, :, :].rearrange("p b n -> p (b n)"), scalar=1.0,
                                         in1=uvf, op0=ALU.add, op1=ALU.mult).then_inc(uv_ready, 1)

            def mask_energy(i, b):
                for c in range(2):
                    dve.wait_ge(energy_done, at(i, 2 * GB, 2 * b + c + 1))
                    dve.wait_ge(pv1_done, at(i, GB, b - 1))
                    dve.tensor_tensor(energy[:, b % 2, 4 * c:4 * c + 4, :],
                                      A[c][:, :].rearrange("p (h n) -> p h n", h=4),
                                      causal[:, :].unsqueeze(1).broadcast_to([P, 4, P]), ALU.mult)\
                       .then_inc(energy_ready, 1)

            def values_bias(i):
                dve.wait_ge(v2_done, at(i, 1, 1))
                dve.wait_ge(pv2_done, at(i, 4 * GB, 0))
                dve.tensor_tensor(v2[:, :, :], A4[3][0:SK], b_xv[0:SK, :].unsqueeze(1).broadcast_to([SK, GB, D]),
                                  ALU.add).then_inc(v2_ready, 1)

            def mask_term(i):
                dve.wait_ge(mask_in, at(i, 16, 16))
                dve.tensor_scalar(neg[:, :, :], mask_i[:, :, :], 1.0, -MASKED, ALU.subtract, ALU.mult)\
                   .then_inc(neg_ready, 1)
                dve.wait_ge(neg_ready, at(i, 1, 1))

            def gate_first(i):
                dve.wait_ge(rms_ready, at(i, 1, 1))
                dve.tensor_scalar(rms[:, :], rms[:, :], 2 * RMS_EPS, None, ALU.add).then_inc(rms_eps_added, 1)
                dve.wait_ge(rms_eps_added, at(i, 1, 1))
                dve.reciprocal(rms_inv[:, :], rms[:, :]).then_inc(rms_inv_ready, 1)
                dve.wait_ge(rms_inv_ready, at(i, 1, 1))
                dve.wait_ge(u_scaled_ready, at(i, 1, 1))
                for b in range(GB):
                    dve.scalar_tensor_tensor(out=gated[:, b, :], in0=A4[2][:, b, :], scalar=rms_inv[:, b:b + 1],
                                             in1=u_scaled[:, b, :], op0=ALU.mult, op1=ALU.mult)\
                       .then_inc(gated_ready, 1)

            def layernorm(i, done, bank4, residual_ready, residual, y, y_ready, st, mo, mom_ready, ve,
                          rstd_ready, rs, dst, dst_ready):
                dve.wait_ge(done, at(i, 1, 1))
                dve.wait_ge(residual_ready, at(i, 1, 1))
                dve.tensor_tensor(y[:, :, :], bank4, residual[:, :, :], ALU.add).then_inc(y_ready, 1)
                dve.wait_ge(y_ready, at(i, 1, 1))
                for b in range(GB):
                    dve.bn_stats(st[:, b, :], y[:, b, :]).then_inc(mom_ready, 1)
                dve.wait_ge(mom_ready, at(i, 2 * GB + 1, GB))
                wait_carrier()
                for b in range(GB):
                    dve.bn_aggr(mo[:, b, :], st[:, b, :]).then_inc(mom_ready, 1)
                dve.wait_ge(mom_ready, at(i, 2 * GB + 1, 2 * GB))
                dve.tensor_scalar(ve[:, :], mo[:, :, 1], LN_EPS, None, ALU.add).then_inc(mom_ready, 1)
                dve.wait_ge(rstd_ready, at(i, 1, 1))
                for b in range(GB):
                    dve.tensor_scalar(dst[:, b, :], y[:, b, :], mo[:, b, 0:1], rs[:, b:b + 1],
                                      ALU.subtract, ALU.mult).then_inc(dst_ready, 1)

            def norm_first(i):
                dve.wait_ge(x1T_done, at(i, 1, 0))
                dve.wait_ge(x1_bo_ready, at(i, 1, 0))
                layernorm(i, proj1_done, A4[0], x_bo_ready, x_bo, y1, y1_ready, stats, moments, mom1_ready,
                          var_eps, rstd1_ready, rstd, x1, x1_ready)

            def norm_second(i):
                dve.wait_ge(x2T_done, at(i, 1, 0))
                layernorm(i, proj2_done, A4[0], x1_bo_ready, x1_bo, y2, y2_ready, stats, moments, mom2_ready,
                          var_eps, rstd2_ready, rstd, x2, x2_ready)

            def norm_third(i):
                dve.wait_ge(out_written, at(i, 16, 0))
                layernorm(i, moe_back, G4, x2T_ready, x2, y3, y3_ready, stats3, moments3, mom3_ready,
                          var_eps3, rstd3_ready, rstd3, y_out, out_ready)

            def add_mask(i, b):
                dve.wait_ge(prob_ready, at(i, GB, b - 1))
                for g, (h0, h1) in enumerate(HEADS_OF):
                    n = NLG * b + g
                    dve.wait_ge(logits_done, at(i, NLG * GB, n + 1))
                    dve.tensor_tensor(logit[:, b % 2, h0:h1, :],
                                      A[n % 2][:, 0:SK * (h1 - h0)].rearrange("p (h k) -> p h k", k=SK),
                                      neg[:, b, :].unsqueeze(1).broadcast_to([P, h1 - h0, SK]),
                                      ALU.add).then_inc(logit_ready, 1)
                dve.wait_ge(logit_ready, at(i, NLG * GB, NLG * (b + 1)))
                dve.tensor_reduce(neg_max[:, b % 2, :], logit[:, b % 2, :, :], X, ALU.max, negate=True)\
                   .then_inc(max_ready, 1)

            def sum_probs(i, b):
                dve.wait_ge(exp2_ready, at(i, GB, b + 1))
                dve.tensor_reduce(prob_sum[:, b, :], logit[:, b % 2, :, :], X, ALU.add).then_inc(sum_ready, 1)

            def normalize(i):
                dve.wait_ge(sum_ready, at(i, GB, GB))
                dve.reciprocal(prob_inv[:, :, :], prob_sum[:, :, :]).then_inc(inv_ready, 1)
                dve.wait_ge(inv_ready, at(i, 1, 1))
                dve.wait_ge(pv2_done, at(i, 4 * GB, 4 * GB))
                dve.tensor_tensor(att2[:, :, :].rearrange("p b (h e) -> p (b h) e", e=E2),
                                  A[2][:, :].rearrange("p (n e) -> p n e", e=E2),
                                  heads_of(prob_inv[:, :, :].rearrange("p b h -> p (b h)"), P, GB * H2, E2),
                                  ALU.mult).then_inc(att2_ready, 1)

            def hidden_rows(i, j):
                dve.wait_ge(tanh_g_ready, at(i, NBLK, j + 1))
                dve.scalar_tensor_tensor(out=silu_g[:, j % 2, :], in0=tanh_g[:, j % 2, :], scalar=1.0,
                                         in1=G[:, :], op0=ALU.add, op1=ALU.mult).then_inc(silu_ready, 1)
                dve.wait_ge(silu_ready, at(i, NBLK, j + 1))
                dve.wait_ge(gu_done, at(i, 2 * NBLK, 2 * j + 2))
                if j >= 2:
                    dve.wait_ge(hidden_w_ready, at(i, NJ, j - 1))
                else:
                    dve.wait_ge(down_done, at(i, NBLK, 0))
                dve.tensor_tensor(hidden[:, j % 2, :], silu_g[:, j % 2, :], U[:, :], ALU.mult)\
                   .then_inc(hidden_ready, 1)

            def turn(i, attend, experts):
                m = i - 1
                if experts:
                    route(m)
                    combine_split(m)
                if attend:
                    elu(i)
                    add_uv_bias(i)
                    silu_uv(i)
                    mask_energy(i, 0)
                if experts:
                    hidden_rows(m, 0)
                if attend:
                    mask_energy(i, 1)
                if experts:
                    hidden_rows(m, 1)
                if attend:
                    mask_energy(i, 2)
                if experts:
                    hidden_rows(m, 2)
                if attend:
                    mask_energy(i, 3)
                if experts:
                    hidden_rows(m, 3)
                if attend:
                    values_bias(i)
                    mask_term(i)
                    gate_first(i)
                if experts:
                    hidden_rows(m, 4)
                    hidden_rows(m, 5)
                if attend:
                    norm_first(i)
                if experts:
                    hidden_rows(m, 6)
                    hidden_rows(m, 7)
                if attend:
                    add_mask(i, 0)
                    add_mask(i, 1)
                if experts:
                    hidden_rows(m, 8)
                if attend:
                    sum_probs(i, 0)
                    add_mask(i, 2)
                    sum_probs(i, 1)
                    add_mask(i, 3)
                if experts:
                    norm_third(m)
                if attend:
                    sum_probs(i, 2)
                    sum_probs(i, 3)
                    normalize(i)
                    norm_second(i)

            dve.wait_ge(weights_in, ALL_WEIGHTS)
            dve.wait_ge(consts_pool, 12)
            dve.tensor_scalar(half_scale[:, :], half_scale[:, :], 0.5, None, ALU.mult).then_inc(consts_dve, 1)
            dve.tensor_copy(expert_no[:, :], expert_i[:, :]).then_inc(consts_dve, 1)
            dve.wait_ge(consts_dve, 2)
            turn(0, True, False)
            turn(1, True, True)
            with dve.Fori(2, NG) as i:
                turn(i, True, True)
            turn(NG, False, True)

        @block.gpsimd
        def _(pool):
            def constants():
                pool.memset(ones[:, :], 1.0).then_inc(consts_pool, 1)
                pool.memset(half_power[:, :], 0.5).then_inc(consts_pool, 1)
                pool.memset(minus_half_power[:, :], -0.5).then_inc(consts_pool, 1)
                pool.memset(pick_expert[:, :, :], 0.0).then_inc(consts_pool, 1)
                pool.iota(expert_i[:, :], pattern=[[1, NE]], base=0, channel_multiplier=0).then_inc(consts_pool, 1)
                pool.wait_ge(consts_pool, 5)
                for dst in (ident, ident16):
                    pool.affine_select(out=dst[:, :], in_=ones[:, :], compare_op=ALU.is_equal, fill=0.0, base=0,
                                       pattern=[[-1, D]], channel_multiplier=1).then_inc(consts_pool, 1)
                pool.affine_select(out=causal[:, :], in_=ones[:, :], compare_op=ALU.is_ge, fill=0.0, base=0,
                                   pattern=[[1, D]], channel_multiplier=-1).then_inc(consts_pool, 1)
                for dst, h, e in ((head_rows1, H1, E1), (head_rows2, H2, E2)):
                    pool.affine_select(out=dst[:, :], in_=ones[:, 0:h], compare_op=ALU.is_ge, fill=0.0, base=0,
                                       pattern=[[-e, h]], channel_multiplier=1).then_inc(consts_pool, 1)
                pool.wait_ge(consts_pool, 10)
                for dst, h, e in ((head_rows1, H1, E1), (head_rows2, H2, E2)):
                    pool.affine_select(out=dst[:, :], in_=dst[:, :], compare_op=ALU.is_ge, fill=0.0, base=e - 1,
                                       pattern=[[e, h]], channel_multiplier=-1).then_inc(consts_pool, 1)
                for s in range(3):
                    pool.affine_select(
                        out=pick_expert[:, :, :].rearrange("p j (t f) -> p j t f", f=FE),
                        in_=pick_expert[:, :, :].rearrange("p j (t f) -> p j t f", f=FE),
                        compare_op=ALU.not_equal, fill=1.0, base=-NE * s,
                        pattern=[[-2, NJ], [-1, 2], [0, FE]], channel_multiplier=1).then_inc(pick_ready, 1)
                    pool.wait_ge(pick_ready, s + 1)

            def query_heads(i, b):
                if b == 0:
                    pool.wait_ge(qk1_ready, at(i, 2, 1))
                pool.wait_ge(energy_done, at(i, 2 * GB, 2 * (b - 1)))
                pool.tensor_tensor(q1_heads[:, b % 2, :, :],
                                   q1[:, P * b:P * b + P].unsqueeze(1).broadcast_to([P, H1, P]),
                                   heads_of(head_rows1[:, :], P, H1, P), ALU.mult).then_inc(q1_heads_ready, 1)

            def gate_scale(i):
                pool.wait_ge(uv_ready, at(i, 1, 1))
                pool.wait_ge(gated_ready, at(i, GB, 0))
                pool.tensor_tensor(u_scaled[:, :, :], uv[:, :, 0:D],
                                   half_scale[:, :].unsqueeze(1).broadcast_to([P, GB, D]), ALU.mult)\
                    .then_inc(u_scaled_ready, 1)

            def add_bo(i):
                pool.wait_ge(x_in, at(i, 16, 16))
                pool.wait_ge(y1_ready, at(i, 1, 0))
                pool.tensor_tensor(x_bo[:, :, :], x_tok[:, :, :], b_o[:, :].unsqueeze(1).broadcast_to([P, GB, D]),
                                   ALU.add).then_inc(x_bo_ready, 1)

            def key_heads(i):
                pool.wait_ge(k2_ready, at(i, 1, 1))
                pool.wait_ge(logits_done, at(i, NLG * GB, 0))
                for b in range(GB):
                    pool.tensor_tensor(k2_heads[:, b, :, :],
                                       k2_T[:, SK * b:SK * b + SK].unsqueeze(1).broadcast_to([P, H2, SK]),
                                       heads_of(head_rows2[:, :], P, H2, SK), ALU.mult)\
                        .then_inc(k2_heads_ready, 1)

            def root_first(i):
                pool.wait_ge(sumsq_ready, at(i, GB, GB))
                pool.tensor_tensor(rms[:, :], sumsq[:, :], half_power[:, :], ALU.pow).then_inc(rms_ready, 1)

            def inverse_root(i, mom_ready, ve, rs, ready):
                pool.wait_ge(mom_ready, at(i, 2 * GB + 1, 2 * GB + 1))
                pool.tensor_tensor(rs[:, :], ve[:, :], minus_half_power[:, :], ALU.pow).then_inc(ready, 1)

            def add_xbo(i):
                pool.wait_ge(x1_ready, at(i, GB, GB))
                pool.wait_ge(y2_ready, at(i, 1, 0))
                pool.tensor_tensor(x1_bo[:, :, :], x1[:, :, :], b_xo[:, :].unsqueeze(1).broadcast_to([P, GB, D]),
                                   ALU.add).then_inc(x1_bo_ready, 1)

            def shift(i, b):
                pool.wait_ge(max_ready, at(i, GB, b + 1))
                pool.wait_ge(probT_done, at(i, 4 * GB, 4 * (b - 1)))
                pool.tensor_tensor(shifted[:, b % 2, :, :], logit[:, b % 2, :, :],
                                   heads_of(neg_max[:, b % 2, :], P, H2, SK), ALU.add)\
                    .then_inc(shifted_ready, 1)

            def group_prob(i, b):
                if b == 0:
                    pool.wait_ge(gp_in, at(i, 16, 16))
                pool.wait_ge(exp2_ready, at(i, GB, b + 1))
                pool.wait_ge(sum_ready, at(i, GB, b + 1))
                pool.tensor_tensor(shifted[:, b % 2, :, :], logit[:, b % 2, :, :],
                                   gprob[:, b, :].unsqueeze(1).broadcast_to([P, H2, SK]), ALU.mult)\
                    .then_inc(prob_ready, 1)

            def weight_hidden(i, j):
                pool.wait_ge(hidden_ready, at(i, NBLK, j + 1))
                pool.wait_ge(rows_ready, at(i, NJ, NJ))
                pool.wait_ge(down_done, at(i, NBLK, j - 1 if j >= 2 else 0))
                pool.tensor_tensor(hidden_w[:, j % 2, :], hidden[:, j % 2, :], weight_rows[:, j, :], ALU.mult)\
                    .then_inc(hidden_w_ready, 1)

            def turn(i, attend, experts):
                m = i - 1
                if attend:
                    query_heads(i, 0)
                    query_heads(i, 1)
                    gate_scale(i)
                    add_bo(i)
                if experts:
                    weight_hidden(m, 0)
                if attend:
                    query_heads(i, 2)
                if experts:
                    weight_hidden(m, 1)
                if attend:
                    query_heads(i, 3)
                if experts:
                    weight_hidden(m, 2)
                    weight_hidden(m, 3)
                if attend:
                    root_first(i)
                if experts:
                    weight_hidden(m, 4)
                if attend:
                    key_heads(i)
                if experts:
                    weight_hidden(m, 5)
                if attend:
                    inverse_root(i, mom1_ready, var_eps, rstd, rstd1_ready)
                    add_xbo(i)
                if experts:
                    weight_hidden(m, 6)
                    weight_hidden(m, 7)
                if attend:
                    shift(i, 0)
                    shift(i, 1)
                    group_prob(i, 0)
                    shift(i, 2)
                    group_prob(i, 1)
                    shift(i, 3)
                if experts:
                    inverse_root(m, mom3_ready, var_eps3, rstd3, rstd3_ready)
                if attend:
                    group_prob(i, 2)
                    group_prob(i, 3)
                    inverse_root(i, mom2_ready, var_eps, rstd, rstd2_ready)

            constants()
            pool.wait_ge(weights_in, ALL_WEIGHTS)
            turn(0, True, False)
            turn(1, True, True)
            with pool.Fori(2, NG) as i:
                turn(i, True, True)
            turn(NG, False, True)


def kernel(x, ctx_1024, fside_BxSxS2_0, mask_BxSxS2_ik1, L0_attn_Wq, L0_attn_bq, L0_attn_Wk, L0_attn_bk,
           L0_attn_Wv, L0_attn_bv, L0_attn_Wu, L0_attn_bu, L0_attn_Wo, L0_attn_bo, L0_attn_scale,
           L0_xattn_wq_k, L0_xattn_wq_b, L0_xattn_wk_k, L0_xattn_wk_b, L0_xattn_wv_k, L0_xattn_wv_b,
           L0_xattn_wo_k, L0_xattn_wo_b, L0_ffn_router_w, L0_ffn_router_bias, L0_ffn_up_proj,
           L0_ffn_gate_proj, L0_ffn_down_proj, L0_ffn_sh_gate, L0_ffn_sh_up, L0_ffn_sh_down):
    import numpy as np
    import concourse.bacc as bacc
    from concourse.bass_utils import run_bass_kernel_spmd

    def laid(a, *axes):
        return np.ascontiguousarray(np.transpose(np.asarray(a), axes) if axes else np.asarray(a))

    nb, s, d = x.shape
    arrays = {
        "x": laid(x),
        "xT": laid(x, 2, 0, 1).reshape(d, nb * s),
        "ctxT": laid(ctx_1024, 2, 0, 1),
        "gp": laid(fside_BxSxS2_0),
        "mask": laid(mask_BxSxS2_ik1),
        "wqT": laid(L0_attn_Wq, 1, 0),
        "wkT": laid(L0_attn_Wk, 1, 0),
        "wuvT": np.concatenate([laid(L0_attn_Wu, 1, 0), laid(L0_attn_Wv, 1, 0)], axis=1),
        "woT": laid(L0_attn_Wo, 1, 0),
        "bq": laid(L0_attn_bq), "bk": laid(L0_attn_bk), "bu": laid(L0_attn_bu), "bv": laid(L0_attn_bv),
        "bo": laid(L0_attn_bo), "scale": laid(L0_attn_scale),
        "xwq": laid(L0_xattn_wq_k), "xbq": laid(L0_xattn_wq_b),
        "xwk": laid(L0_xattn_wk_k), "xbk": laid(L0_xattn_wk_b),
        "xwv": laid(L0_xattn_wv_k), "xbv": laid(L0_xattn_wv_b),
        "xwo": laid(L0_xattn_wo_k), "xbo": laid(L0_xattn_wo_b),
        "routerT": laid(L0_ffn_router_w, 1, 0), "router_b": laid(L0_ffn_router_bias),
        "up": laid(L0_ffn_up_proj), "gate": laid(L0_ffn_gate_proj), "down": laid(L0_ffn_down_proj),
        "sh_gateT": laid(L0_ffn_sh_gate, 1, 0), "sh_upT": laid(L0_ffn_sh_up, 1, 0),
        "sh_downT": laid(L0_ffn_sh_down, 1, 0),
    }
    nc = bacc.Bacc("TRN2", target_bir_lowering=False, num_devices=1)
    args = {n: nc.dram_tensor(f"in_{n}", a.shape, mybir.dt.from_np(a.dtype), kind="ExternalInput").ap()
            for n, a in arrays.items()}
    args["out"] = nc.dram_tensor("out_x", (nb, s, d), F32, kind="ExternalOutput").ap()
    decoder_layer(nc, **args)
    r = run_bass_kernel_spmd(nc, [{f"in_{n}": a for n, a in arrays.items()}], core_ids=[0])
    return r.results[0]["out_x"]
```

```python
from contextlib import ExitStack

import concourse.bass as bass
from concourse import mybir

F32 = mybir.dt.float32
BF16 = mybir.dt.bfloat16
I32 = mybir.dt.int32
U32 = mybir.dt.uint32
ALU = mybir.AluOpType
ACT = mybir.ActivationFunctionType
X = mybir.AxisListType.X

P = 128
D = 128
GB = 4
T = GB * P
H1, E1 = 8, 16
H2, E2 = 16, 8
NE, FE = 16, 64
NJ = NE * FE // P
NBLK = NJ + 1
MASKED = -1e9
LN_EPS = 1e-5
RMS_EPS = 1e-8
HEADS_OF = [(0, 6), (6, 12), (12, 16)]
NLG = len(HEADS_OF)
NPT = 4
TH = T // 2
NGU = 2 * NBLK
SHARED = [(what, k, lag) for what, first, end, lag in [
    ("queries", 0, 1, 1), ("att2_T", 0, 1, 2), ("logits", 0, 3, 1), ("projection", 0, 1, 2),
    ("x2_T", 0, 1, 2), ("probs", 0, 1, 1), ("logits", 3, 4, 1), ("probs", 1, 2, 1), ("logits", 4, 5, 1),
    ("probs", 2, 3, 1), ("logits", 5, 6, 1), ("probs", 3, 4, 1), ("logits", 6, 9, 1), ("probs", 4, 7, 1),
    ("logits", 9, 10, 1), ("probs", 7, 8, 1), ("logits", 10, 12, 1), ("probs", 8, 16, 1)
] for k in range(first, end)]
SHARED_PLACE = {(what, k): n for n, (what, k, lag) in enumerate(SHARED)}
assert len(SHARED) % 2 == 0


def decoder_layer(nc, x, xT, ctxT, gp, mask, wqT, wkT, wuvT, woT, bq, bk, bu, bv, bo, scale,
                  xwq, xbq, xwk, xbk, xwv, xbv, xwo, xbo, routerT, router_b, up, gate, down,
                  sh_gateT, sh_upT, sh_downT, out):
    NB, SK = ctxT.shape[1], ctxT.shape[2]
    NG = NB // GB
    KT = GB * SK

    ctx = ExitStack()
    with ctx:
        def sb(name, shape, dt=F32):
            return ctx.enter_context(nc.sbuf_tensor(name, shape, dt))

        def sem(name):
            return ctx.enter_context(nc.semaphore(name))

        w_qT, w_kT, w_oT = (sb(n, [P, D]) for n in ("w_qT", "w_kT", "w_oT"))
        w_uvT = sb("w_uvT", [P, 2 * D])
        w_xq, w_xk, w_xv, w_xo = (sb(n, [P, D]) for n in ("w_xq", "w_xk", "w_xv", "w_xo"))
        w_routerT = sb("w_routerT", [P, NE])
        w_gate, w_up, w_down = (sb(n, [P, NBLK, P]) for n in ("w_gate", "w_up", "w_down"))
        b_cols = sb("b_cols", [P, 5])
        b_uv = sb("b_uv", [P, 2 * D])
        b_o = sb("b_o", [P, D])
        half_scale = sb("half_scale", [P, D])
        b_xv = sb("b_xv", [P, D])
        b_xo = sb("b_xo", [P, D])
        b_router = sb("b_router", [P, NE])
        ones = sb("ones", [P, D])
        ident = sb("ident", [P, D])
        ident16 = sb("ident16", [P, D], BF16)
        causal = sb("causal", [P, D])
        head_rows1 = sb("head_rows1", [P, H1])
        head_rows2 = sb("head_rows2", [P, H2])
        expert_no = sb("expert_no", [P, NE])
        expert_i = sb("expert_i", [P, NE], I32)
        pick_expert = sb("pick_expert", [3 * NE, NJ, P], BF16)
        half_power = sb("half_power", [P, GB])
        minus_half_power = sb("minus_half_power", [P, GB])

        x_tok = sb("x_tok", [P, GB, D])
        x_T = sb("x_T", [P, T])
        ctx_T = sb("ctx_T", [P, KT])
        gprob = sb("gprob", [P, GB, SK])
        mask_i = sb("mask_i", [P, GB, SK], I32)

        exp_qk = sb("exp_qk", [P, 2, T])
        q1 = sb("q1", [P, T])
        k1 = sb("k1", [P, T])
        q1_heads = sb("q1_heads", [P, 2, H1, P])
        uv = sb("uv", [P, GB, 2 * D])
        tanh_uv = sb("tanh_uv", [P, GB, 2 * D])
        u_scaled = sb("u_scaled", [P, GB, D])
        x_bo = sb("x_bo", [P, GB, D])
        energy = sb("energy", [P, 2, H1, P])
        sq = sb("sq", [P, D])
        sumsq = sb("sumsq", [P, GB])
        rms = sb("rms", [P, GB])
        rms_inv = sb("rms_inv", [P, GB])
        gated = sb("gated", [P, GB, D])
        gated_T = sb("gated_T", [P, T])
        y1 = sb("y1", [P, GB, D])
        x1 = sb("x1", [P, GB, D])
        x1_bo = sb("x1_bo", [P, GB, D])
        x1_T = sb("x1_T", [P, T])
        stats = sb("stats", [P, GB, 6])
        moments = sb("moments", [P, GB, 2])
        var_eps = sb("var_eps", [P, GB])
        rstd = sb("rstd", [P, GB])

        neg = sb("neg", [P, GB, SK])
        q2_T = sb("q2_T", [P, T])
        k2_T = sb("k2_T", [P, KT])
        k2_heads = sb("k2_heads", [P, GB, H2, SK])
        v2 = sb("v2", [SK, GB, D])
        logit = sb("logit", [P, 2, H2, SK])
        shifted = sb("shifted", [P, 2, H2, SK])
        neg_max = sb("neg_max", [P, 2, H2])
        prob_sum = sb("prob_sum", [P, GB, H2])
        prob_inv = sb("prob_inv", [P, GB, H2])
        prob_T = sb("prob_T", [SK, 2, H2, P])
        att2 = sb("att2", [P, GB, D])
        att2_T = sb("att2_T", [P, T])
        y2 = sb("y2", [P, GB, D])
        x2 = sb("x2", [P, GB, D])
        x2_T = sb("x2_T", [P, T])

        score = sb("score", [P, GB, NE])
        top8 = sb("top8", [P, GB, 8])
        top_i = sb("top_i", [P, GB, 8], U32)
        top_f = sb("top_f", [P, GB, 8])
        gap = sb("gap", [P, GB])
        exp_gap = sb("exp_gap", [P, GB])
        wait_column = sb("wait_column", [P, 1])
        one_plus = sb("one_plus", [P, GB])
        w_top = sb("w_top", [P, 2, GB])
        hit = sb("hit", [P, 2, GB, NE])
        comb_2 = sb("comb_2", [P, 2, GB, NE])
        combine = sb("combine", [P, 3, GB, NE])
        comb_parts = sb("comb_parts", [P, GB, 3, NE], BF16)
        comb_T = sb("comb_T", [3 * NE, T], BF16)
        weight_rows = sb("weight_rows", [P, NJ, T])
        tanh_g = sb("tanh_g", [P, 2, TH])
        silu_g = sb("silu_g", [P, 2, TH])
        hidden = sb("hidden", [P, 2, T])
        hidden_w = sb("hidden_w", [P, 2, T])
        moe_T = sb("moe_T", [P, T])
        x2_kept = sb("x2_kept", [P, GB, D])
        y3 = sb("y3", [P, GB, D])
        y_out = sb("y_out", [P, GB, D])
        stats3 = sb("stats3", [P, GB, 6])
        moments3 = sb("moments3", [P, GB, 2])
        var_eps3 = sb("var_eps3", [P, GB])
        rstd3 = sb("rstd3", [P, GB])

        def bank(name):
            return ctx.enter_context(nc.psum_tensor(name, [P, T], F32))

        first_a, first_b, first_out = bank("first_a"), bank("first_b"), bank("first_out")
        second_pair = [bank("second_a"), bank("second_b")]
        second_out = bank("second_out")
        experts_gu, experts_out = bank("experts_gu"), bank("experts_out")

        def by_batch(bank):
            return bank[:, :].rearrange("p (b d) -> p b d", b=GB)

        weights_in = sem("weights_in")
        consts_pool = sem("consts_pool")
        pick_ready = sem("pick_ready")
        consts_dve = sem("consts_dve")
        q_bias_ready = sem("q_bias_ready")
        waited = sem("waited")
        x_T_in, x_in, ctx_in, gp_in, mask_in = (sem(n) for n in ("x_T_in", "x_in", "ctx_in", "gp_in", "mask_in"))
        out_written = sem("out_written")
        qk1_done, uv_done, k2_done, v2_done = (sem(n) for n in ("qk1_done", "uv_done", "k2_done", "v2_done"))
        energy_done, pv1_done, gT_done, proj1_done = (
            sem(n) for n in ("energy_done", "pv1_done", "gT_done", "proj1_done"))
        kept_ready = sem("kept_ready")
        x1T_done, q2_done, logits_done, probT_done, pv2_done = (
            sem(n) for n in ("x1T_done", "q2_done", "logits_done", "probT_done", "pv2_done"))
        aT_done, proj2_done, x2T_done = (sem(n) for n in ("aT_done", "proj2_done", "x2T_done"))
        router_done, combT_done, rows_done, gu_done, down_done, moe_back = (
            sem(n) for n in ("router_done", "combT_done", "rows_done", "gu_done", "down_done", "moe_back"))
        exp_qk_ready, tanh_uv_ready, k2_ready, sumsq_ready, gT_ready, x1T_ready, q2_ready = (
            sem(n) for n in ("exp_qk_ready", "tanh_uv_ready", "k2_ready", "sumsq_ready", "gT_ready",
                             "x1T_ready", "q2_ready"))
        exp2_ready, probT_ready, aT_ready, x2T_ready = (
            sem(n) for n in ("exp2_ready", "probT_ready", "aT_ready", "x2T_ready"))
        exp_gap_ready, combT_ready, rows_ready, tanh_g_ready, moeT_ready = (
            sem(n) for n in ("exp_gap_ready", "combT_ready", "rows_ready", "tanh_g_ready", "moeT_ready"))
        qk1_ready, uv_biased, uv_ready, v2_ready, energy_ready = (
            sem(n) for n in ("qk1_ready", "uv_biased", "uv_ready", "v2_ready", "energy_ready"))
        elu_part, rms_eps_added, rms_inv_ready, gated_ready, y1_ready, mom1_ready, x1_ready = (
            sem(n) for n in ("elu_part", "rms_eps_added", "rms_inv_ready", "gated_ready", "y1_ready",
                             "mom1_ready", "x1_ready"))
        neg_ready, logit_ready, max_ready, sum_ready, inv_ready, att2_ready = (
            sem(n) for n in ("neg_ready", "logit_ready", "max_ready", "sum_ready", "inv_ready", "att2_ready"))
        y2_ready, mom2_ready, x2_ready, split_step = (
            sem(n) for n in ("y2_ready", "mom2_ready", "x2_ready", "split_step"))
        route_step, gap_ready, parts_ready, silu_ready, hidden_ready, y3_ready, mom3_ready, out_ready = (
            sem(n) for n in ("route_step", "gap_ready", "parts_ready", "silu_ready", "hidden_ready",
                             "y3_ready", "mom3_ready", "out_ready"))
        q1_heads_ready, u_scaled_ready, x_bo_ready, rms_ready, rstd1_ready, x1_bo_ready = (
            sem(n) for n in ("q1_heads_ready", "u_scaled_ready", "x_bo_ready", "rms_ready", "rstd1_ready",
                             "x1_bo_ready"))
        k2_heads_ready, shifted_ready, prob_ready, rstd2_ready, hidden_w_ready, rstd3_ready = (
            sem(n) for n in ("k2_heads_ready", "shifted_ready", "prob_ready", "rstd2_ready",
                             "hidden_w_ready", "rstd3_ready"))

        def at(i, per, k):
            count = i * per + k
            return max(count, 0) if isinstance(count, int) else count

        def runs(t, lag):
            return not isinstance(t, int) or 0 <= t - lag < NG

        def shared(what, k):
            return second_pair[SHARED_PLACE[what, k] % 2]

        def heads_of(ap, n, h, e):
            return ap.unsqueeze(2).broadcast_to([n, h, e])

        loads = [
            (w_qT[:, :], wqT), (w_kT[:, :], wkT), (w_uvT[:, :], wuvT), (w_oT[:, :], woT),
            (w_xq[:, :], xwq), (w_xk[:, :], xwk), (w_xv[:, :], xwv), (w_xo[:, :], xwo),
            (w_routerT[:, :], routerT),
            (w_gate[:, 0:NJ, :].rearrange("p j (t e) -> p (j t) e", e=FE), gate.rearrange("k d e -> d k e")),
            (w_up[:, 0:NJ, :].rearrange("p j (t e) -> p (j t) e", e=FE), up.rearrange("k d e -> d k e")),
            (w_down[:, 0:NJ, :], down.rearrange("(j t) e d -> (t e) j d", t=2)),
            (w_gate[:, NJ, :], sh_gateT), (w_up[:, NJ, :], sh_upT), (w_down[:, NJ, :], sh_downT),
            (b_cols[:, 0:1], bq.unsqueeze(1)), (b_cols[:, 1:2], bk.unsqueeze(1)),
            (b_cols[:, 2:3], xbq.unsqueeze(1)), (b_cols[:, 3:4], xbk.unsqueeze(1)),
            (b_uv[:, 0:D], bu.partition_broadcast(P)), (b_uv[:, D:2 * D], bv.partition_broadcast(P)),
            (b_o[:, :], bo.partition_broadcast(P)), (half_scale[:, :], scale.partition_broadcast(P)),
            (b_xv[:, :], xbv.partition_broadcast(P)), (b_xo[:, :], xbo.partition_broadcast(P)),
            (b_router[:, :], router_b.partition_broadcast(P)),
        ]
        ALL_WEIGHTS = 16 * len(loads)

        block = ctx.enter_context(nc.Block())

        @block.sync
        def _(sp):
            def load_x_T(i):
                sp.wait_ge(uv_done, at(i, 2, 0))
                sp.dma_start(x_T[:, :], xT[:, bass.ds(i * T, T)]).then_inc(x_T_in, 16)

            def load_x(i):
                sp.wait_ge(x_bo_ready, at(i, 1, 0))
                sp.dma_start(x_tok[:, :, :], x[bass.ds(i * GB, GB)].rearrange("b p d -> p b d"))\
                  .then_inc(x_in, 16)

            def load_context(i):
                sp.wait_ge(v2_done, at(i, 1, 0))
                sp.wait_ge(k2_done, at(i, 1, 0))
                sp.dma_start(ctx_T[:, :], ctxT[:, bass.ds(i * GB, GB), :].rearrange("p b k -> p (b k)"))\
                  .then_inc(ctx_in, 16)

            def load_mask(i):
                sp.wait_ge(neg_ready, at(i, 1, 0))
                sp.dma_start(mask_i[:, :, :], mask[bass.ds(i * GB, GB)].rearrange("b p k -> p b k"))\
                  .then_inc(mask_in, 16)

            def load_gprob(i):
                sp.wait_ge(prob_ready, at(i, GB, 0))
                sp.dma_start(gprob[:, :, :], gp[bass.ds(i * GB, GB)].rearrange("b p k -> p b k"))\
                  .then_inc(gp_in, 16)

            def store_group(i):
                sp.wait_ge(out_ready, at(i, GB, GB))
                sp.dma_start(out[bass.ds(i * GB, GB)].rearrange("b p d -> p b d"), y_out[:, :, :])\
                  .then_inc(out_written, 16)

            def turn(t, load_next):
                if runs(t, 1):
                    load_gprob(t - 1)
                if runs(t, 0):
                    load_mask(t)
                    load_context(t)
                if load_next:
                    load_x_T(t + 1)
                if runs(t, 3):
                    store_group(t - 3)
                if load_next:
                    load_x(t + 1)

            for dst, src in loads[:3]:
                sp.dma_start(dst, src).then_inc(weights_in, 16)
            load_x_T(0)
            for dst, src in loads[3:]:
                sp.dma_start(dst, src).then_inc(weights_in, 16)
            load_x(0)
            for t in range(4):
                turn(t, True)
            with sp.Fori(4, NG - 1) as t:
                turn(t, True)
            for t in range(NG - 1, NG + 3):
                turn(t, False)
            sp.wait_ge(out_written, 16 * NG)

        @block.tensor
        def _(pe):
            def router(i):
                pe.wait_ge(x2T_ready, at(i, 1, 1))
                pe.wait_ge(y3_ready, at(i, 1, 0))
                for b in range(GB):
                    mm = pe.matmul(experts_gu[:, NE * b:NE * b + NE], x2_T[:, P * b:P * b + P], w_routerT[:, :],
                                   start=True, stop=True)
                mm.then_inc(router_done, 1)

            def combine_transpose(i):
                pe.wait_ge(pick_ready, 3)
                pe.wait_ge(parts_ready, at(i, 1, 1))
                pe.wait_ge(moeT_ready, at(i, 1, 0))
                view = experts_out[:, :].bitcast(BF16)
                for b in range(GB):
                    mm = pe.transpose(view[0:3 * NE, P * b:P * b + P],
                                      comb_parts[:, b, :, :].rearrange("p s e -> p (s e)"), ident16[:, :])
                mm.then_inc(combT_done, 1)

            def combine_rows(i, j0, j1):
                for j in range(j0, j1):
                    if j == 0:
                        pe.wait_ge(combT_ready, at(i, 1, 1))
                        pe.wait_ge(gap_ready, at(i, 1, 1))
                    elif j >= 2:
                        pe.wait_ge(rows_ready, at(i, NJ, j - 1))
                    pe.matmul((experts_gu, experts_out)[j % 2][:, :], pick_expert[:, j, :], comb_T[:, :],
                              start=True, stop=True).then_inc(rows_done, 1)

            def gate_up(i, n):
                if n == 0:
                    pe.wait_ge(rows_ready, at(i, NJ, NJ))
                else:
                    pe.wait_ge(hidden_ready, at(i, NGU, n))
                o = TH * (n % 2)
                pe.matmul(experts_gu[:, 0:TH], w_gate[:, n // 2, :], x2_T[:, o:o + TH], start=True, stop=True)
                pe.matmul(experts_gu[:, TH:T], w_up[:, n // 2, :], x2_T[:, o:o + TH], start=True, stop=True)\
                  .then_inc(gu_done, 1)

            def expert_down(i, j):
                if j < NJ:
                    pe.wait_ge(hidden_w_ready, at(i, NJ, j + 1))
                else:
                    pe.wait_ge(hidden_ready, at(i, NGU, NGU))
                h = hidden_w if j < NJ else hidden
                pe.matmul(experts_out[:, :], w_down[:, j, :], h[:, j % 2, :], start=(j == 0),
                          stop=(j == NBLK - 1)).then_inc(down_done, 1)

            def moe_transpose(i):
                pe.wait_ge(moeT_ready, at(i, 1, 1))
                for b in range(GB):
                    mm = pe.transpose(experts_gu[:, P * b:P * b + P], moe_T[:, P * b:P * b + P], ident[:, :])
                mm.then_inc(moe_back, 1)

            def project_qk(i):
                pe.wait_ge(x_T_in, at(i, 16, 16))
                pe.wait_ge(y1_ready, at(i, 1, 0))
                pe.matmul(first_a[:, :], w_qT[:, :], x_T[:, :], start=True, stop=True).then_inc(qk1_done, 1)
                pe.wait_ge(v2_ready, at(i, 1, 0))
                pe.matmul(first_b[:, :], w_kT[:, :], x_T[:, :], start=True, stop=True).then_inc(qk1_done, 1)

            def project_uv(i, c):
                if c == 0:
                    pe.wait_ge(gated_ready, at(i, GB, 0))
                else:
                    pe.wait_ge(qk1_ready, at(i, 2, 1))
                for b in range(2 * c, 2 * c + 2):
                    o = 2 * D * (b % 2)
                    mm = pe.matmul((first_out, first_a)[c][:, o:o + 2 * D], x_T[:, P * b:P * b + P],
                                   w_uvT[:, :], start=True, stop=True)
                mm.then_inc(uv_done, 1)

            def context_keys(i):
                pe.wait_ge(ctx_in, at(i, 16, 16))
                pe.wait_ge(energy_ready, at(i, 2 * GB, 2 * GB))
                pe.matmul(first_b[:, 0:KT], w_xk[:, :], ctx_T[:, :], start=True, stop=True).then_inc(k2_done, 1)

            def context_values(i):
                pe.wait_ge(x1T_ready, at(i, 1, 1))
                for b in range(GB):
                    mm = pe.matmul(first_b[0:SK, P * b:P * b + P], ctx_T[:, SK * b:SK * b + SK], w_xv[:, :],
                                   start=True, stop=True)
                mm.then_inc(v2_done, 1)

            def energies(i, b, c):
                if c == 0:
                    pe.wait_ge(q1_heads_ready, at(i, GB, b + 1))
                if b == 0 and c == 0:
                    pe.wait_ge(uv_biased, at(i, 2, 2))
                    pe.wait_ge(qk1_ready, at(i, 2, 2))
                elif b > 0:
                    pe.wait_ge(energy_ready, at(i, 2 * GB, 2 * (b - 1) + c + 1))
                pe.matmul((first_a, first_b)[c][:, :], k1[:, P * b:P * b + P],
                          q1_heads[:, b % 2, 4 * c:4 * c + 4, :].rearrange("p h n -> p (h n)"),
                          start=True, stop=True).then_inc(energy_done, 1)

            def values_first(i, b, c):
                pe.wait_ge(energy_ready, at(i, 2 * GB, 2 * b + c + 1))
                if b == 0 and c == 0:
                    pe.wait_ge(uv_ready, at(i, 1, 1))
                for h in range(4 * c, 4 * c + 4):
                    o = D * b + E1 * h
                    mm = pe.matmul(first_out[:, o:o + E1], energy[:, b % 2, h, :],
                                   uv[:, b, D + E1 * h:D + E1 * h + E1], start=True, stop=True)
                mm.then_inc(pv1_done, 1)

            def gated_transpose(i):
                pe.wait_ge(gated_ready, at(i, GB, GB))
                for b in range(GB):
                    mm = pe.transpose(first_a[:, P * b:P * b + P], gated[:, b, :], ident[:, :])
                mm.then_inc(gT_done, 1)

            def output_first(i):
                pe.wait_ge(gT_ready, at(i, 1, 1))
                for b in range(GB):
                    mm = pe.matmul(first_a[:, P * b:P * b + P], gated_T[:, P * b:P * b + P], w_oT[:, :],
                                   start=True, stop=True)
                mm.then_inc(proj1_done, 1)

            def x1_transpose(i):
                pe.wait_ge(x1_ready, at(i, GB, GB))
                pe.wait_ge(k2_ready, at(i, 1, 1))
                for b in range(GB):
                    mm = pe.transpose(first_b[:, P * b:P * b + P], x1[:, b, :], ident[:, :])
                mm.then_inc(x1T_done, 1)

            def queries_second(i):
                pe.wait_ge(x1T_ready, at(i, 1, 1))
                shared_bank_free(i + 1, "queries", 0)
                pe.matmul(shared("queries", 0)[:, :], w_xq[:, :], x1_T[:, :], start=True, stop=True).then_inc(q2_done, 1)

            def shared_bank_free(t, what, k):
                n = SHARED_PLACE[what, k] - 2
                while True:
                    last, number, lag = SHARED[n % len(SHARED)]
                    i = t - lag if n >= 0 else t - 1 - lag
                    if not isinstance(i, int) or 0 <= i < NG:
                        break
                    n -= 2
                    if n < -len(SHARED):
                        return
                if last == "queries":
                    pe.wait_ge(q2_ready, at(i, 1, 1))
                elif last == "logits":
                    pe.wait_ge(logit_ready, at(i, NLG * GB, number + 1))
                elif last == "probs":
                    pe.wait_ge(probT_ready, at(i, NPT * GB, number + 1))
                elif last == "att2_T":
                    pe.wait_ge(aT_ready, at(i, 1, 1))
                elif last == "projection":
                    pe.wait_ge(y2_ready, at(i, 1, 1))
                else:
                    pe.wait_ge(x2T_ready, at(i, 1, 1))

            def logits(i, b, g):
                h0, h1 = HEADS_OF[g]
                if b == 0 and g == 0:
                    pe.wait_ge(q2_ready, at(i, 1, 1))
                if g == 0:
                    pe.wait_ge(k2_heads_ready, at(i, GB, b + 1))
                shared_bank_free(i + 1, "logits", NLG * b + g)
                pe.matmul(shared("logits", NLG * b + g)[:, 0:SK * (h1 - h0)], q2_T[:, P * b:P * b + P],
                          k2_heads[:, b, h0:h1, :].rearrange("p h k -> p (h k)"),
                          start=True, stop=True).then_inc(logits_done, 1)

            def prob_transposes(i, b, c):
                if c == 0:
                    pe.wait_ge(prob_ready, at(i, GB, b + 1))
                shared_bank_free(i + 1, "probs", NPT * b + c)
                for h in range(4 * c, 4 * c + 4):
                    mm = pe.transpose(shared("probs", NPT * b + c)[0:SK, P * (h % 4):P * (h % 4) + P],
                                      shifted[:, b % 2, h, :], ident[:, :])
                mm.then_inc(probT_done, 1)

            def values_second(i, b, c):
                if b == 0 and c == 0:
                    pe.wait_ge(v2_ready, at(i, 1, 1))
                    pe.wait_ge(att2_ready, at(i, 1, 0))
                pe.wait_ge(probT_ready, at(i, NPT * GB, NPT * b + c + 1))
                for h in range(4 * c, 4 * c + 4):
                    o = D * b + E2 * h
                    mm = pe.matmul(second_out[:, o:o + E2], prob_T[:, b % 2, h, :],
                                   v2[:, b, E2 * h:E2 * h + E2], start=True, stop=True)
                mm.then_inc(pv2_done, 1)

            def att2_transpose(i):
                pe.wait_ge(att2_ready, at(i, 1, 1))
                shared_bank_free(i + 2, "att2_T", 0)
                for b in range(GB):
                    mm = pe.transpose(shared("att2_T", 0)[:, P * b:P * b + P], att2[:, b, :], ident[:, :])
                mm.then_inc(aT_done, 1)

            def output_second(i):
                pe.wait_ge(aT_ready, at(i, 1, 1))
                shared_bank_free(i + 2, "projection", 0)
                for b in range(GB):
                    mm = pe.matmul(shared("projection", 0)[:, P * b:P * b + P], att2_T[:, P * b:P * b + P],
                                   w_xo[:, :], start=True, stop=True)
                mm.then_inc(proj2_done, 1)

            def x2_transpose(i):
                pe.wait_ge(x2_ready, at(i, GB, GB))
                shared_bank_free(i + 2, "x2_T", 0)
                for b in range(GB):
                    mm = pe.transpose(shared("x2_T", 0)[:, P * b:P * b + P], x2[:, b, :], ident[:, :])
                mm.then_inc(x2T_done, 1)

            def turn(t):
                i, s, r, m = t, t - 1, t - 2, t - 3
                if runs(t, 1):
                    queries_second(s)
                    context_values(s)
                if runs(t, 3):
                    gate_up(m, 14)
                if runs(t, 2):
                    att2_transpose(r)
                if runs(t, 1):
                    logits(s, 0, 0)
                    logits(s, 0, 1)
                    logits(s, 0, 2)
                if runs(t, 2):
                    output_second(r)
                if runs(t, 3):
                    gate_up(m, 15)
                    expert_down(m, 6)
                if runs(t, 0):
                    project_qk(i)
                if runs(t, 3):
                    gate_up(m, 16)
                if runs(t, 0):
                    project_uv(i, 0)
                if runs(t, 3):
                    expert_down(m, 7)
                if runs(t, 0):
                    project_uv(i, 1)
                if runs(t, 3):
                    gate_up(m, 17)
                if runs(t, 2):
                    x2_transpose(r)
                if runs(t, 0):
                    energies(i, 0, 0)
                    energies(i, 0, 1)
                if runs(t, 3):
                    expert_down(m, 8)
                if runs(t, 1):
                    prob_transposes(s, 0, 0)
                    logits(s, 1, 0)
                    values_second(s, 0, 0)
                    prob_transposes(s, 0, 1)
                if runs(t, 3):
                    moe_transpose(m)
                if runs(t, 0):
                    energies(i, 1, 0)
                if runs(t, 1):
                    values_second(s, 0, 1)
                    logits(s, 1, 1)
                if runs(t, 0):
                    values_first(i, 0, 0)
                if runs(t, 1):
                    prob_transposes(s, 0, 2)
                if runs(t, 0):
                    energies(i, 1, 1)
                if runs(t, 1):
                    values_second(s, 0, 2)
                    logits(s, 1, 2)
                if runs(t, 2):
                    router(r)
                if runs(t, 0):
                    values_first(i, 0, 1)
                if runs(t, 1):
                    prob_transposes(s, 0, 3)
                if runs(t, 0):
                    energies(i, 2, 0)
                if runs(t, 1):
                    values_second(s, 0, 3)
                    logits(s, 2, 0)
                if runs(t, 0):
                    values_first(i, 1, 0)
                if runs(t, 1):
                    logits(s, 2, 1)
                if runs(t, 0):
                    energies(i, 2, 1)
                if runs(t, 2):
                    combine_transpose(r)
                if runs(t, 0):
                    values_first(i, 1, 1)
                if runs(t, 1):
                    logits(s, 2, 2)
                if runs(t, 2):
                    combine_rows(r, 0, 2)
                if runs(t, 1):
                    prob_transposes(s, 1, 0)
                if runs(t, 2):
                    combine_rows(r, 2, 4)
                if runs(t, 1):
                    values_second(s, 1, 0)
                if runs(t, 2):
                    combine_rows(r, 4, 6)
                if runs(t, 1):
                    prob_transposes(s, 1, 1)
                if runs(t, 0):
                    energies(i, 3, 0)
                if runs(t, 2):
                    combine_rows(r, 6, 8)
                if runs(t, 1):
                    values_second(s, 1, 1)
                if runs(t, 2):
                    gate_up(r, 0)
                if runs(t, 1):
                    prob_transposes(s, 1, 2)
                if runs(t, 0):
                    values_first(i, 2, 0)
                if runs(t, 2):
                    gate_up(r, 1)
                if runs(t, 1):
                    values_second(s, 1, 2)
                    logits(s, 3, 0)
                    prob_transposes(s, 1, 3)
                if runs(t, 2):
                    gate_up(r, 2)
                if runs(t, 1):
                    values_second(s, 1, 3)
                    logits(s, 3, 1)
                if runs(t, 0):
                    values_first(i, 2, 1)
                if runs(t, 2):
                    gate_up(r, 3)
                    expert_down(r, 0)
                if runs(t, 1):
                    logits(s, 3, 2)
                    prob_transposes(s, 2, 0)
                if runs(t, 2):
                    gate_up(r, 4)
                if runs(t, 1):
                    values_second(s, 2, 0)
                    prob_transposes(s, 2, 1)
                if runs(t, 0):
                    energies(i, 3, 1)
                if runs(t, 1):
                    values_second(s, 2, 1)
                if runs(t, 2):
                    gate_up(r, 5)
                if runs(t, 0):
                    values_first(i, 3, 0)
                if runs(t, 2):
                    expert_down(r, 1)
                if runs(t, 1):
                    prob_transposes(s, 2, 2)
                if runs(t, 2):
                    gate_up(r, 6)
                if runs(t, 1):
                    values_second(s, 2, 2)
                if runs(t, 2):
                    gate_up(r, 7)
                if runs(t, 1):
                    prob_transposes(s, 2, 3)
                if runs(t, 0):
                    values_first(i, 3, 1)
                if runs(t, 2):
                    expert_down(r, 2)
                if runs(t, 1):
                    values_second(s, 2, 3)
                if runs(t, 2):
                    gate_up(r, 8)
                if runs(t, 0):
                    context_keys(i)
                if runs(t, 2):
                    gate_up(r, 9)
                if runs(t, 1):
                    prob_transposes(s, 3, 0)
                if runs(t, 2):
                    expert_down(r, 3)
                if runs(t, 1):
                    values_second(s, 3, 0)
                if runs(t, 2):
                    gate_up(r, 10)
                if runs(t, 0):
                    gated_transpose(i)
                if runs(t, 1):
                    prob_transposes(s, 3, 1)
                if runs(t, 2):
                    expert_down(r, 4)
                if runs(t, 1):
                    values_second(s, 3, 1)
                if runs(t, 0):
                    output_first(i)
                if runs(t, 2):
                    gate_up(r, 11)
                if runs(t, 1):
                    prob_transposes(s, 3, 2)
                    values_second(s, 3, 2)
                if runs(t, 2):
                    gate_up(r, 12)
                    expert_down(r, 5)
                if runs(t, 1):
                    prob_transposes(s, 3, 3)
                if runs(t, 2):
                    gate_up(r, 13)
                if runs(t, 1):
                    values_second(s, 3, 3)
                if runs(t, 0):
                    x1_transpose(i)

            pe.wait_ge(weights_in, ALL_WEIGHTS)
            pe.wait_ge(consts_pool, 12)
            pe.wait_ge(pick_ready, 3)
            for t in range(4):
                turn(t)
            with pe.Fori(4, NG) as t:
                turn(t)
            for t in range(NG, NG + 3):
                turn(t)

        @block.scalar
        def _(act):
            def q_bias():
                act.wait_ge(weights_in, ALL_WEIGHTS)
                act.mul(b_cols[:, 4:5], b_cols[:, 2:3], E2 ** -0.5).then_inc(q_bias_ready, 1)
                act.wait_ge(q_bias_ready, 1)

            def exp_first(i):
                act.wait_ge(qk1_ready, at(i, 2, 0))
                for c in range(2):
                    act.wait_ge(qk1_done, at(i, 2, c + 1))
                    act.activation(exp_qk[:, c, :], (first_a, first_b)[c][:, :], ACT.Exp, bias=b_cols[:, c:c + 1])\
                       .then_inc(exp_qk_ready, 1)

            def keys_second(i):
                act.wait_ge(k2_done, at(i, 1, 1))
                act.wait_ge(k2_heads_ready, at(i, GB, 0))
                act.activation(k2_T[:, :], first_b[:, 0:KT], ACT.Identity, bias=b_cols[:, 3:4])\
                   .then_inc(k2_ready, 1)

            def tanh_first(i, c):
                act.wait_ge(uv_biased, at(i, 2, c + 1))
                act.activation(tanh_uv[:, 2 * c:2 * c + 2, :], uv[:, 2 * c:2 * c + 2, :], ACT.Tanh, scale=0.5)\
                   .then_inc(tanh_uv_ready, 1)

            def squares(i):
                act.wait_ge(pv1_done, at(i, 2 * GB, 2 * GB))
                for b in range(GB):
                    if b:
                        act.wait_ge(sumsq_ready, at(i, GB, b))
                    act.activation(sq[:, :], by_batch(first_out)[:, b, :], ACT.Square, scale=D ** -0.5, accum_out=sumsq[:, b:b + 1])\
                       .then_inc(sumsq_ready, 1)

            def copy(i, done, bank, dst, ready):
                act.wait_ge(done, at(i, 1, 1))
                act.activation(dst[:, :], bank[:, :], ACT.Copy).then_inc(ready, 1)

            def queries(i):
                act.wait_ge(q2_done, at(i, 1, 1))
                act.activation(q2_T[:, :], shared("queries", 0)[:, :], ACT.Identity, bias=b_cols[:, 4:5], scale=E2 ** -0.5)\
                   .then_inc(q2_ready, 1)

            def exp_second(i, b):
                act.wait_ge(shifted_ready, at(i, GB, b + 1))
                act.activation(logit[:, b % 2, :, :], shifted[:, b % 2, :, :], ACT.Exp).then_inc(exp2_ready, 1)

            def copy_probs(i, b, c):
                act.wait_ge(probT_done, at(i, NPT * GB, NPT * b + c + 1))
                act.wait_ge(pv2_done, at(i, NPT * GB, NPT * (b - 2) + c + 1))
                act.activation(prob_T[:, b % 2, 4 * c:4 * c + 4, :].rearrange("k h p -> k (h p)"),
                               shared("probs", NPT * b + c)[0:SK, :], ACT.Copy).then_inc(probT_ready, 1)

            def exp_gap_of(i):
                act.wait_ge(gap_ready, at(i, 1, 1))
                act.activation(exp_gap[:, :], gap[:, :], ACT.Exp).then_inc(exp_gap_ready, 1)

            def keep_residual(i):
                act.wait_ge(x2_ready, at(i, GB, GB))
                act.wait_ge(y3_ready, at(i, 1, 0))
                act.activation(x2_kept[:, :, :], x2[:, :, :], ACT.Copy).then_inc(kept_ready, 1)

            def copy_combine(i):
                act.wait_ge(combT_done, at(i, 1, 1))
                act.activation(comb_T[:, :], experts_out[:, :].bitcast(BF16)[0:3 * NE, 0:T], ACT.Copy)\
                   .then_inc(combT_ready, 1)

            def copy_rows(i, j0, j1):
                for j in range(j0, j1):
                    act.wait_ge(rows_done, at(i, NJ, j + 1))
                    act.wait_ge(hidden_w_ready, at(i, NJ, 0))
                    act.activation(weight_rows[:, j, :], (experts_gu, experts_out)[j % 2][:, :], ACT.Copy)\
                       .then_inc(rows_ready, 1)

            def tanh_gate(i, n):
                act.wait_ge(gu_done, at(i, NGU, n + 1))
                act.wait_ge(silu_ready, at(i, NGU, n - 1))
                act.activation(tanh_g[:, n % 2, :], experts_gu[:, 0:TH], ACT.Tanh, scale=0.5)\
                   .then_inc(tanh_g_ready, 1)

            def copy_x2(i):
                act.wait_ge(gu_done, at(i, NGU, 0))
                copy(i, x2T_done, shared("x2_T", 0), x2_T, x2T_ready)

            def moe_out(i):
                act.wait_ge(down_done, at(i, NBLK, NBLK))
                act.activation(moe_T[:, :], experts_out[:, :], ACT.Copy, scale=0.5).then_inc(moeT_ready, 1)

            def turn(t):
                i, s, r, m = t, t - 1, t - 2, t - 3
                if runs(t, 1):
                    queries(s)
                if runs(t, 3):
                    tanh_gate(m, 14)
                if runs(t, 2):
                    copy(r, aT_done, shared("att2_T", 0), att2_T, aT_ready)
                if runs(t, 3):
                    tanh_gate(m, 15)
                if runs(t, 0):
                    exp_first(i)
                if runs(t, 3):
                    tanh_gate(m, 16)
                if runs(t, 1):
                    exp_second(s, 0)
                if runs(t, 0):
                    tanh_first(i, 0)
                    tanh_first(i, 1)
                if runs(t, 3):
                    tanh_gate(m, 17)
                if runs(t, 2):
                    copy_x2(r)
                if runs(t, 1):
                    copy_probs(s, 0, 0)
                if runs(t, 3):
                    moe_out(m)
                if runs(t, 1):
                    copy_probs(s, 0, 1)
                    copy_probs(s, 0, 2)
                if runs(t, 2):
                    keep_residual(r)
                if runs(t, 1):
                    copy_probs(s, 0, 3)
                if runs(t, 2):
                    exp_gap_of(r)
                if runs(t, 1):
                    exp_second(s, 1)
                if runs(t, 2):
                    copy_combine(r)
                    copy_rows(r, 0, 2)
                if runs(t, 1):
                    copy_probs(s, 1, 0)
                if runs(t, 2):
                    copy_rows(r, 2, 6)
                if runs(t, 1):
                    copy_probs(s, 1, 1)
                if runs(t, 2):
                    copy_rows(r, 6, 8)
                    tanh_gate(r, 0)
                if runs(t, 1):
                    copy_probs(s, 1, 2)
                if runs(t, 2):
                    tanh_gate(r, 1)
                if runs(t, 1):
                    copy_probs(s, 1, 3)
                if runs(t, 2):
                    tanh_gate(r, 2)
                if runs(t, 1):
                    exp_second(s, 2)
                if runs(t, 2):
                    tanh_gate(r, 3)
                if runs(t, 1):
                    copy_probs(s, 2, 0)
                if runs(t, 2):
                    tanh_gate(r, 4)
                if runs(t, 1):
                    copy_probs(s, 2, 1)
                if runs(t, 2):
                    tanh_gate(r, 5)
                if runs(t, 1):
                    copy_probs(s, 2, 2)
                if runs(t, 2):
                    tanh_gate(r, 6)
                if runs(t, 1):
                    exp_second(s, 3)
                if runs(t, 2):
                    tanh_gate(r, 7)
                if runs(t, 1):
                    copy_probs(s, 2, 3)
                if runs(t, 2):
                    tanh_gate(r, 8)
                if runs(t, 0):
                    squares(i)
                    keys_second(i)
                if runs(t, 2):
                    tanh_gate(r, 9)
                if runs(t, 1):
                    copy_probs(s, 3, 0)
                if runs(t, 2):
                    tanh_gate(r, 10)
                if runs(t, 0):
                    copy(i, gT_done, first_a, gated_T, gT_ready)
                if runs(t, 1):
                    copy_probs(s, 3, 1)
                if runs(t, 2):
                    tanh_gate(r, 11)
                if runs(t, 1):
                    copy_probs(s, 3, 2)
                if runs(t, 2):
                    tanh_gate(r, 12)
                if runs(t, 1):
                    copy_probs(s, 3, 3)
                if runs(t, 2):
                    tanh_gate(r, 13)
                if runs(t, 0):
                    copy(i, x1T_done, first_b, x1_T, x1T_ready)

            q_bias()
            for t in range(4):
                turn(t)
            with act.Fori(4, NG) as t:
                turn(t)
            for t in range(NG, NG + 3):
                turn(t)

        @block.vector
        def _(dve):
            def wait_carrier():
                dve.tensor_copy(wait_column[:, :], ones[:, 0:1]).then_inc(waited, 1)

            def route(i):
                dve.wait_ge(router_done, at(i, 1, 1))
                gs = experts_gu[:, 0:GB * NE].rearrange("p (b e) -> p b e", b=GB)
                dve.tensor_tensor(score[:, :, :], gs, b_router[:, :].unsqueeze(1).broadcast_to([P, GB, NE]),
                                  ALU.add).then_inc(route_step, 1)
                dve.wait_ge(route_step, at(i, 10, 1))
                wait_carrier()
                for b in range(GB):
                    mx = dve.max(top8[:, b, :], score[:, b, :])
                mx.then_inc(route_step, 1)
                dve.wait_ge(route_step, at(i, 10, 2))
                dve.tensor_tensor(gap[:, :], top8[:, :, 1], top8[:, :, 0], ALU.subtract).then_inc(gap_ready, 1)
                for b in range(GB):
                    mx = dve.max_index(top_i[:, b, :], top8[:, b, :], score[:, b, :])
                mx.then_inc(route_step, 1)
                dve.wait_ge(route_step, at(i, 10, 3))
                dve.tensor_copy(top_f[:, :, :], top_i[:, :, :]).then_inc(route_step, 1)
                dve.wait_ge(route_step, at(i, 10, 4))
                experts = expert_no[:, :].unsqueeze(1).broadcast_to([P, GB, NE])
                for r in range(2):
                    hits = dve.tensor_tensor(hit[:, r, :, :], experts, heads_of(top_f[:, :, r], P, GB, NE),
                                             ALU.is_equal)
                hits.then_inc(route_step, 1)
                dve.wait_ge(exp_gap_ready, at(i, 1, 1))
                dve.tensor_scalar(one_plus[:, :], exp_gap[:, :], 1.0, None, ALU.add).then_inc(route_step, 1)
                dve.wait_ge(route_step, at(i, 10, 6))
                dve.reciprocal(w_top[:, 0, :], one_plus[:, :]).then_inc(route_step, 1)
                dve.wait_ge(route_step, at(i, 10, 7))
                dve.tensor_tensor(w_top[:, 1, :], exp_gap[:, :], w_top[:, 0, :], ALU.mult).then_inc(route_step, 1)
                dve.wait_ge(route_step, at(i, 10, 8))
                for r in range(2):
                    w = dve.tensor_tensor(comb_2[:, r, :, :], hit[:, r, :, :],
                                          heads_of(w_top[:, r, :], P, GB, NE), ALU.mult)
                w.then_inc(route_step, 1)
                dve.wait_ge(route_step, at(i, 10, 9))
                dve.tensor_tensor(combine[:, 0, :, :], comb_2[:, 0, :, :], comb_2[:, 1, :, :], ALU.add)\
                   .then_inc(route_step, 1)
                dve.wait_ge(route_step, at(i, 10, 10))

            def combine_split(i):
                dve.wait_ge(combT_done, at(i, 1, 0))
                for s in range(2):
                    dve.tensor_copy(comb_parts[:, :, s, :], combine[:, s, :, :]).then_inc(split_step, 1)
                    dve.wait_ge(split_step, at(i, 4, 2 * s + 1))
                    dve.tensor_tensor(combine[:, s + 1, :, :], combine[:, s, :, :], comb_parts[:, :, s, :],
                                      ALU.subtract).then_inc(split_step, 1)
                    dve.wait_ge(split_step, at(i, 4, 2 * s + 2))
                dve.tensor_copy(comb_parts[:, :, 2, :], combine[:, 2, :, :]).then_inc(parts_ready, 1)

            def elu(i):
                dve.wait_ge(q1_heads_ready, at(i, GB, 0))
                dve.wait_ge(energy_done, at(i, 2 * GB, 0))
                for c, z in ((0, q1), (1, k1)):
                    dve.wait_ge(exp_qk_ready, at(i, 2, c + 1))
                    dve.tensor_scalar(exp_qk[:, c, :], exp_qk[:, c, :], 1.0, -1.0, ALU.min, ALU.add)\
                       .then_inc(elu_part, 1)
                    dve.wait_ge(elu_part, at(i, 2, c + 1))
                    dve.scalar_tensor_tensor(out=z[:, :], in0=(first_a, first_b)[c][:, :], scalar=b_cols[:, c:c + 1],
                                             in1=exp_qk[:, c, :], op0=ALU.add, op1=ALU.max)\
                       .then_inc(qk1_ready, 1)

            def add_uv_bias(i, c):
                if c == 0:
                    dve.wait_ge(u_scaled_ready, at(i, 1, 0))
                    dve.wait_ge(pv1_done, at(i, 2 * GB, 0))
                dve.wait_ge(uv_done, at(i, 2, c + 1))
                dve.tensor_tensor(uv[:, 2 * c:2 * c + 2, :],
                                  (first_out, first_a)[c][:, :].rearrange("p (b n) -> p b n", b=2),
                                  b_uv[:, :].unsqueeze(1).broadcast_to([P, 2, 2 * D]),
                                  ALU.add).then_inc(uv_biased, 1)

            def silu_uv(i):
                dve.wait_ge(tanh_uv_ready, at(i, 2, 2))
                uvf = uv[:, :, :].rearrange("p b n -> p (b n)")
                dve.scalar_tensor_tensor(out=uvf, in0=tanh_uv[:, :, :].rearrange("p b n -> p (b n)"), scalar=1.0,
                                         in1=uvf, op0=ALU.add, op1=ALU.mult).then_inc(uv_ready, 1)

            def mask_energy(i, b, c):
                dve.wait_ge(energy_done, at(i, 2 * GB, 2 * b + c + 1))
                dve.wait_ge(pv1_done, at(i, 2 * GB, 2 * (b - 2) + c + 1))
                dve.tensor_tensor(energy[:, b % 2, 4 * c:4 * c + 4, :],
                                  (first_a, first_b)[c][:, :].rearrange("p (h n) -> p h n", h=4),
                                  causal[:, :].unsqueeze(1).broadcast_to([P, 4, P]), ALU.mult)\
                   .then_inc(energy_ready, 1)

            def values_bias(i):
                dve.wait_ge(v2_done, at(i, 1, 1))
                dve.wait_ge(pv2_done, at(i, NPT * GB, 0))
                dve.tensor_tensor(v2[:, :, :], by_batch(first_b)[0:SK], b_xv[0:SK, :].unsqueeze(1).broadcast_to([SK, GB, D]),
                                  ALU.add).then_inc(v2_ready, 1)

            def mask_term(i):
                dve.wait_ge(mask_in, at(i, 16, 16))
                dve.tensor_scalar(neg[:, :, :], mask_i[:, :, :], 1.0, -MASKED, ALU.subtract, ALU.mult)\
                   .then_inc(neg_ready, 1)
                dve.wait_ge(neg_ready, at(i, 1, 1))

            def gate_first(i):
                dve.wait_ge(rms_ready, at(i, 1, 1))
                dve.tensor_scalar(rms[:, :], rms[:, :], 2 * RMS_EPS, None, ALU.add).then_inc(rms_eps_added, 1)
                dve.wait_ge(rms_eps_added, at(i, 1, 1))
                dve.reciprocal(rms_inv[:, :], rms[:, :]).then_inc(rms_inv_ready, 1)
                dve.wait_ge(rms_inv_ready, at(i, 1, 1))
                dve.wait_ge(u_scaled_ready, at(i, 1, 1))
                for b in range(GB):
                    dve.scalar_tensor_tensor(out=gated[:, b, :], in0=by_batch(first_out)[:, b, :], scalar=rms_inv[:, b:b + 1],
                                             in1=u_scaled[:, b, :], op0=ALU.mult, op1=ALU.mult)\
                       .then_inc(gated_ready, 1)

            def row_moments(i, y_ready, y, st, mo, ve, mom_ready):
                dve.wait_ge(y_ready, at(i, 1, 1))
                for b in range(GB):
                    dve.bn_stats(st[:, b, :], y[:, b, :]).then_inc(mom_ready, 1)
                dve.wait_ge(mom_ready, at(i, 2 * GB + 1, GB))
                wait_carrier()
                for b in range(GB):
                    dve.bn_aggr(mo[:, b, :], st[:, b, :]).then_inc(mom_ready, 1)
                dve.wait_ge(mom_ready, at(i, 2 * GB + 1, 2 * GB))
                dve.tensor_scalar(ve[:, :], mo[:, :, 1], LN_EPS, None, ALU.add).then_inc(mom_ready, 1)

            def normal_rows(i, rstd_ready, y, mo, rs, dst, dst_ready):
                dve.wait_ge(rstd_ready, at(i, 1, 1))
                for b in range(GB):
                    dve.tensor_scalar(dst[:, b, :], y[:, b, :], mo[:, b, 0:1], rs[:, b:b + 1],
                                      ALU.subtract, ALU.mult).then_inc(dst_ready, 1)

            def moments_first(i):
                dve.wait_ge(proj1_done, at(i, 1, 1))
                dve.wait_ge(x_bo_ready, at(i, 1, 1))
                dve.tensor_tensor(y1[:, :, :], by_batch(first_a), x_bo[:, :, :], ALU.add).then_inc(y1_ready, 1)
                row_moments(i, y1_ready, y1, stats, moments, var_eps, mom1_ready)

            def normal_first(i):
                dve.wait_ge(x1T_done, at(i, 1, 0))
                dve.wait_ge(x1_bo_ready, at(i, 1, 0))
                normal_rows(i, rstd1_ready, y1, moments, rstd, x1, x1_ready)

            def moments_second(i):
                dve.wait_ge(proj2_done, at(i, 1, 1))
                dve.wait_ge(x1_bo_ready, at(i, 1, 1))
                dve.tensor_tensor(y2[:, :, :], by_batch(shared("projection", 0)), x1_bo[:, :, :], ALU.add)\
                   .then_inc(y2_ready, 1)
                row_moments(i, y2_ready, y2, stats, moments, var_eps, mom2_ready)

            def normal_second(i):
                dve.wait_ge(x2T_done, at(i, 1, 0))
                dve.wait_ge(kept_ready, at(i, 1, 0))
                normal_rows(i, rstd2_ready, y2, moments, rstd, x2, x2_ready)

            def moments_third(i):
                dve.wait_ge(moe_back, at(i, 1, 1))
                dve.wait_ge(kept_ready, at(i, 1, 1))
                dve.tensor_tensor(y3[:, :, :], by_batch(experts_gu), x2_kept[:, :, :], ALU.add)\
                   .then_inc(y3_ready, 1)
                row_moments(i, y3_ready, y3, stats3, moments3, var_eps3, mom3_ready)

            def normal_third(i):
                dve.wait_ge(out_written, at(i, 16, 0))
                normal_rows(i, rstd3_ready, y3, moments3, rstd3, y_out, out_ready)

            def add_mask(i, b, g):
                h0, h1 = HEADS_OF[g]
                n = NLG * b + g
                if g == 0:
                    dve.wait_ge(prob_ready, at(i, GB, b - 1))
                    dve.wait_ge(sum_ready, at(i, GB, b - 1))
                dve.wait_ge(logits_done, at(i, NLG * GB, n + 1))
                dve.tensor_tensor(logit[:, b % 2, h0:h1, :],
                                  shared("logits", n)[:, 0:SK * (h1 - h0)].rearrange("p (h k) -> p h k", k=SK),
                                  neg[:, b, :].unsqueeze(1).broadcast_to([P, h1 - h0, SK]),
                                  ALU.add).then_inc(logit_ready, 1)

            def negated_max(i, b):
                dve.wait_ge(logit_ready, at(i, NLG * GB, NLG * (b + 1)))
                dve.tensor_reduce(neg_max[:, b % 2, :], logit[:, b % 2, :, :], X, ALU.max, negate=True)\
                   .then_inc(max_ready, 1)

            def sum_probs(i, b):
                dve.wait_ge(exp2_ready, at(i, GB, b + 1))
                dve.tensor_reduce(prob_sum[:, b, :], logit[:, b % 2, :, :], X, ALU.add).then_inc(sum_ready, 1)

            def normalize(i):
                dve.wait_ge(sum_ready, at(i, GB, GB))
                dve.reciprocal(prob_inv[:, :, :], prob_sum[:, :, :]).then_inc(inv_ready, 1)
                dve.wait_ge(inv_ready, at(i, 1, 1))
                dve.wait_ge(pv2_done, at(i, NPT * GB, NPT * GB))
                dve.tensor_tensor(att2[:, :, :].rearrange("p b (h e) -> p (b h) e", e=E2),
                                  second_out[:, :].rearrange("p (n e) -> p n e", e=E2),
                                  heads_of(prob_inv[:, :, :].rearrange("p b h -> p (b h)"), P, GB * H2, E2),
                                  ALU.mult).then_inc(att2_ready, 1)

            def hidden_rows(i, n):
                j, o = n // 2, TH * (n % 2)
                dve.wait_ge(tanh_g_ready, at(i, NGU, n + 1))
                dve.scalar_tensor_tensor(out=silu_g[:, n % 2, :], in0=tanh_g[:, n % 2, :], scalar=1.0,
                                         in1=experts_gu[:, 0:TH], op0=ALU.add, op1=ALU.mult)\
                   .then_inc(silu_ready, 1)
                dve.wait_ge(silu_ready, at(i, NGU, n + 1))
                if j < 2:
                    dve.wait_ge(down_done, at(i, NBLK, 0))
                else:
                    dve.wait_ge(hidden_w_ready, at(i, NJ, j - 1))
                dve.tensor_tensor(hidden[:, j % 2, o:o + TH], silu_g[:, n % 2, :], experts_gu[:, TH:T], ALU.mult)\
                   .then_inc(hidden_ready, 1)

            def turn(t):
                i, s, r, m = t, t - 1, t - 2, t - 3
                if runs(t, 2):
                    normalize(r)
                if runs(t, 1):
                    values_bias(s)
                if runs(t, 3):
                    hidden_rows(m, 14)
                if runs(t, 1):
                    add_mask(s, 0, 0)
                    add_mask(s, 0, 1)
                    add_mask(s, 0, 2)
                    negated_max(s, 0)
                if runs(t, 3):
                    hidden_rows(m, 15)
                if runs(t, 2):
                    moments_second(r)
                if runs(t, 3):
                    hidden_rows(m, 16)
                if runs(t, 0):
                    elu(i)
                if runs(t, 2):
                    normal_second(r)
                if runs(t, 0):
                    add_uv_bias(i, 0)
                    add_uv_bias(i, 1)
                if runs(t, 3):
                    hidden_rows(m, 17)
                if runs(t, 0):
                    silu_uv(i)
                    mask_energy(i, 0, 0)
                    mask_energy(i, 0, 1)
                if runs(t, 1):
                    add_mask(s, 1, 0)
                    sum_probs(s, 0)
                if runs(t, 0):
                    mask_energy(i, 1, 0)
                if runs(t, 1):
                    add_mask(s, 1, 1)
                if runs(t, 3):
                    moments_third(m)
                if runs(t, 0):
                    mask_energy(i, 1, 1)
                if runs(t, 1):
                    add_mask(s, 1, 2)
                    negated_max(s, 1)
                if runs(t, 3):
                    normal_third(m)
                if runs(t, 2):
                    route(r)
                if runs(t, 0):
                    mask_energy(i, 2, 0)
                if runs(t, 2):
                    combine_split(r)
                if runs(t, 1):
                    add_mask(s, 2, 0)
                    add_mask(s, 2, 1)
                if runs(t, 0):
                    mask_energy(i, 2, 1)
                if runs(t, 1):
                    add_mask(s, 2, 2)
                    negated_max(s, 2)
                    sum_probs(s, 1)
                if runs(t, 0):
                    mask_energy(i, 3, 0)
                if runs(t, 2):
                    hidden_rows(r, 0)
                    hidden_rows(r, 1)
                if runs(t, 1):
                    add_mask(s, 3, 0)
                if runs(t, 2):
                    hidden_rows(r, 2)
                if runs(t, 1):
                    add_mask(s, 3, 1)
                if runs(t, 2):
                    hidden_rows(r, 3)
                if runs(t, 1):
                    add_mask(s, 3, 2)
                    negated_max(s, 3)
                if runs(t, 2):
                    hidden_rows(r, 4)
                if runs(t, 0):
                    mask_energy(i, 3, 1)
                if runs(t, 2):
                    hidden_rows(r, 5)
                    hidden_rows(r, 6)
                if runs(t, 1):
                    sum_probs(s, 2)
                if runs(t, 2):
                    hidden_rows(r, 7)
                    hidden_rows(r, 8)
                    hidden_rows(r, 9)
                if runs(t, 0):
                    gate_first(i)
                if runs(t, 2):
                    hidden_rows(r, 10)
                if runs(t, 1):
                    sum_probs(s, 3)
                if runs(t, 2):
                    hidden_rows(r, 11)
                if runs(t, 0):
                    mask_term(i)
                    moments_first(i)
                if runs(t, 2):
                    hidden_rows(r, 12)
                if runs(t, 0):
                    normal_first(i)
                if runs(t, 2):
                    hidden_rows(r, 13)

            dve.wait_ge(weights_in, ALL_WEIGHTS)
            dve.wait_ge(consts_pool, 12)
            dve.tensor_scalar(half_scale[:, :], half_scale[:, :], 0.5, None, ALU.mult).then_inc(consts_dve, 1)
            dve.tensor_copy(expert_no[:, :], expert_i[:, :]).then_inc(consts_dve, 1)
            dve.wait_ge(consts_dve, 2)
            for t in range(4):
                turn(t)
            with dve.Fori(4, NG) as t:
                turn(t)
            for t in range(NG, NG + 3):
                turn(t)

        @block.gpsimd
        def _(pool):
            def constants():
                pool.memset(ones[:, :], 1.0).then_inc(consts_pool, 1)
                pool.memset(half_power[:, :], 0.5).then_inc(consts_pool, 1)
                pool.memset(minus_half_power[:, :], -0.5).then_inc(consts_pool, 1)
                pool.memset(pick_expert[:, :, :], 0.0).then_inc(consts_pool, 1)
                pool.iota(expert_i[:, :], pattern=[[1, NE]], base=0, channel_multiplier=0).then_inc(consts_pool, 1)
                pool.wait_ge(consts_pool, 5)
                for dst in (ident, ident16):
                    pool.affine_select(out=dst[:, :], in_=ones[:, :], compare_op=ALU.is_equal, fill=0.0, base=0,
                                       pattern=[[-1, D]], channel_multiplier=1).then_inc(consts_pool, 1)
                pool.affine_select(out=causal[:, :], in_=ones[:, :], compare_op=ALU.is_ge, fill=0.0, base=0,
                                   pattern=[[1, D]], channel_multiplier=-1).then_inc(consts_pool, 1)
                for dst, h, e in ((head_rows1, H1, E1), (head_rows2, H2, E2)):
                    pool.affine_select(out=dst[:, :], in_=ones[:, 0:h], compare_op=ALU.is_ge, fill=0.0, base=0,
                                       pattern=[[-e, h]], channel_multiplier=1).then_inc(consts_pool, 1)
                pool.wait_ge(consts_pool, 10)
                for dst, h, e in ((head_rows1, H1, E1), (head_rows2, H2, E2)):
                    pool.affine_select(out=dst[:, :], in_=dst[:, :], compare_op=ALU.is_ge, fill=0.0, base=e - 1,
                                       pattern=[[e, h]], channel_multiplier=-1).then_inc(consts_pool, 1)
                for s in range(3):
                    pool.affine_select(
                        out=pick_expert[:, :, :].rearrange("p j (t f) -> p j t f", f=FE),
                        in_=pick_expert[:, :, :].rearrange("p j (t f) -> p j t f", f=FE),
                        compare_op=ALU.not_equal, fill=1.0, base=-NE * s,
                        pattern=[[-2, NJ], [-1, 2], [0, FE]], channel_multiplier=1).then_inc(pick_ready, 1)
                    pool.wait_ge(pick_ready, s + 1)

            def query_heads(i, b):
                if b == 0:
                    pool.wait_ge(qk1_ready, at(i, 2, 1))
                pool.wait_ge(energy_done, at(i, 2 * GB, 2 * (b - 1)))
                pool.tensor_tensor(q1_heads[:, b % 2, :, :],
                                   q1[:, P * b:P * b + P].unsqueeze(1).broadcast_to([P, H1, P]),
                                   heads_of(head_rows1[:, :], P, H1, P), ALU.mult).then_inc(q1_heads_ready, 1)

            def gate_scale(i):
                pool.wait_ge(uv_ready, at(i, 1, 1))
                pool.wait_ge(gated_ready, at(i, GB, 0))
                pool.tensor_tensor(u_scaled[:, :, :], uv[:, :, 0:D],
                                   half_scale[:, :].unsqueeze(1).broadcast_to([P, GB, D]), ALU.mult)\
                    .then_inc(u_scaled_ready, 1)

            def add_bo(i):
                pool.wait_ge(x_in, at(i, 16, 16))
                pool.wait_ge(y1_ready, at(i, 1, 0))
                pool.tensor_tensor(x_bo[:, :, :], x_tok[:, :, :], b_o[:, :].unsqueeze(1).broadcast_to([P, GB, D]),
                                   ALU.add).then_inc(x_bo_ready, 1)

            def key_heads(i, b):
                pool.wait_ge(k2_ready, at(i, 1, 1))
                pool.wait_ge(logits_done, at(i, NLG * GB, 0))
                pool.tensor_tensor(k2_heads[:, b, :, :],
                                   k2_T[:, SK * b:SK * b + SK].unsqueeze(1).broadcast_to([P, H2, SK]),
                                   heads_of(head_rows2[:, :], P, H2, SK), ALU.mult)\
                    .then_inc(k2_heads_ready, 1)

            def root_first(i):
                pool.wait_ge(sumsq_ready, at(i, GB, GB))
                pool.tensor_tensor(rms[:, :], sumsq[:, :], half_power[:, :], ALU.pow).then_inc(rms_ready, 1)

            def inverse_root(i, mom_ready, ve, rs, ready):
                pool.wait_ge(mom_ready, at(i, 2 * GB + 1, 2 * GB + 1))
                pool.tensor_tensor(rs[:, :], ve[:, :], minus_half_power[:, :], ALU.pow).then_inc(ready, 1)

            def add_xbo(i):
                pool.wait_ge(x1_ready, at(i, GB, GB))
                pool.wait_ge(y2_ready, at(i, 1, 0))
                pool.tensor_tensor(x1_bo[:, :, :], x1[:, :, :], b_xo[:, :].unsqueeze(1).broadcast_to([P, GB, D]),
                                   ALU.add).then_inc(x1_bo_ready, 1)

            def shift(i, b):
                pool.wait_ge(max_ready, at(i, GB, b + 1))
                pool.wait_ge(probT_done, at(i, 4 * GB, 4 * (b - 1)))
                pool.tensor_tensor(shifted[:, b % 2, :, :], logit[:, b % 2, :, :],
                                   heads_of(neg_max[:, b % 2, :], P, H2, SK), ALU.add)\
                    .then_inc(shifted_ready, 1)

            def group_prob(i, b):
                if b == 0:
                    pool.wait_ge(gp_in, at(i, 16, 16))
                pool.wait_ge(exp2_ready, at(i, GB, b + 1))
                pool.tensor_tensor(shifted[:, b % 2, :, :], logit[:, b % 2, :, :],
                                   gprob[:, b, :].unsqueeze(1).broadcast_to([P, H2, SK]), ALU.mult)\
                    .then_inc(prob_ready, 1)

            def weight_hidden(i, j):
                pool.wait_ge(hidden_ready, at(i, NGU, 2 * j + 2))
                pool.wait_ge(rows_ready, at(i, NJ, NJ))
                pool.wait_ge(down_done, at(i, NBLK, j - 1 if j >= 2 else 0))
                pool.tensor_tensor(hidden_w[:, j % 2, :], hidden[:, j % 2, :], weight_rows[:, j, :], ALU.mult)\
                    .then_inc(hidden_w_ready, 1)

            def turn(t):
                i, s, r, m = t, t - 1, t - 2, t - 3
                if runs(t, 3):
                    weight_hidden(m, 6)
                if runs(t, 1):
                    shift(s, 0)
                if runs(t, 3):
                    weight_hidden(m, 7)
                if runs(t, 2):
                    inverse_root(r, mom2_ready, var_eps, rstd, rstd2_ready)
                if runs(t, 0):
                    query_heads(i, 0)
                if runs(t, 1):
                    add_xbo(s)
                    group_prob(s, 0)
                if runs(t, 0):
                    query_heads(i, 1)
                    gate_scale(i)
                    add_bo(i)
                if runs(t, 3):
                    inverse_root(m, mom3_ready, var_eps3, rstd3, rstd3_ready)
                if runs(t, 0):
                    query_heads(i, 2)
                if runs(t, 1):
                    shift(s, 1)
                    group_prob(s, 1)
                if runs(t, 0):
                    query_heads(i, 3)
                if runs(t, 1):
                    shift(s, 2)
                if runs(t, 2):
                    weight_hidden(r, 0)
                if runs(t, 1):
                    group_prob(s, 2)
                if runs(t, 2):
                    weight_hidden(r, 1)
                if runs(t, 1):
                    shift(s, 3)
                if runs(t, 2):
                    weight_hidden(r, 2)
                if runs(t, 1):
                    group_prob(s, 3)
                if runs(t, 2):
                    weight_hidden(r, 3)
                if runs(t, 0):
                    root_first(i)
                if runs(t, 2):
                    weight_hidden(r, 4)
                if runs(t, 0):
                    key_heads(i, 0)
                    key_heads(i, 1)
                if runs(t, 2):
                    weight_hidden(r, 5)
                if runs(t, 0):
                    inverse_root(i, mom1_ready, var_eps, rstd, rstd1_ready)
                    key_heads(i, 2)
                    key_heads(i, 3)

            constants()
            pool.wait_ge(weights_in, ALL_WEIGHTS)
            for t in range(4):
                turn(t)
            with pool.Fori(4, NG) as t:
                turn(t)
            for t in range(NG, NG + 3):
                turn(t)


def kernel(x, ctx_1024, fside_BxSxS2_0, mask_BxSxS2_ik1, L0_attn_Wq, L0_attn_bq, L0_attn_Wk, L0_attn_bk,
           L0_attn_Wv, L0_attn_bv, L0_attn_Wu, L0_attn_bu, L0_attn_Wo, L0_attn_bo, L0_attn_scale,
           L0_xattn_wq_k, L0_xattn_wq_b, L0_xattn_wk_k, L0_xattn_wk_b, L0_xattn_wv_k, L0_xattn_wv_b,
           L0_xattn_wo_k, L0_xattn_wo_b, L0_ffn_router_w, L0_ffn_router_bias, L0_ffn_up_proj,
           L0_ffn_gate_proj, L0_ffn_down_proj, L0_ffn_sh_gate, L0_ffn_sh_up, L0_ffn_sh_down):
    import numpy as np
    import concourse.bacc as bacc
    from concourse.bass_utils import run_bass_kernel_spmd

    def laid(a, *axes):
        return np.ascontiguousarray(np.transpose(np.asarray(a), axes) if axes else np.asarray(a))

    nb, s, d = x.shape
    arrays = {
        "x": laid(x),
        "xT": laid(x, 2, 0, 1).reshape(d, nb * s),
        "ctxT": laid(ctx_1024, 2, 0, 1),
        "gp": laid(fside_BxSxS2_0),
        "mask": laid(mask_BxSxS2_ik1),
        "wqT": laid(L0_attn_Wq, 1, 0),
        "wkT": laid(L0_attn_Wk, 1, 0),
        "wuvT": np.concatenate([laid(L0_attn_Wu, 1, 0), laid(L0_attn_Wv, 1, 0)], axis=1),
        "woT": laid(L0_attn_Wo, 1, 0),
        "bq": laid(L0_attn_bq), "bk": laid(L0_attn_bk), "bu": laid(L0_attn_bu), "bv": laid(L0_attn_bv),
        "bo": laid(L0_attn_bo), "scale": laid(L0_attn_scale),
        "xwq": laid(L0_xattn_wq_k), "xbq": laid(L0_xattn_wq_b),
        "xwk": laid(L0_xattn_wk_k), "xbk": laid(L0_xattn_wk_b),
        "xwv": laid(L0_xattn_wv_k), "xbv": laid(L0_xattn_wv_b),
        "xwo": laid(L0_xattn_wo_k), "xbo": laid(L0_xattn_wo_b),
        "routerT": laid(L0_ffn_router_w, 1, 0), "router_b": laid(L0_ffn_router_bias),
        "up": laid(L0_ffn_up_proj), "gate": laid(L0_ffn_gate_proj), "down": laid(L0_ffn_down_proj),
        "sh_gateT": laid(L0_ffn_sh_gate, 1, 0), "sh_upT": laid(L0_ffn_sh_up, 1, 0),
        "sh_downT": laid(L0_ffn_sh_down, 1, 0),
    }
    nc = bacc.Bacc("TRN2", target_bir_lowering=False, num_devices=1)
    args = {n: nc.dram_tensor(f"in_{n}", a.shape, mybir.dt.from_np(a.dtype), kind="ExternalInput").ap()
            for n, a in arrays.items()}
    args["out"] = nc.dram_tensor("out_x", (nb, s, d), F32, kind="ExternalOutput").ap()
    decoder_layer(nc, **args)
    r = run_bass_kernel_spmd(nc, [{f"in_{n}": a for n, a in arrays.items()}], core_ids=[0])
    return r.results[0]["out_x"]
```

```python
from contextlib import ExitStack

import concourse.bass as bass
from concourse import mybir

F32 = mybir.dt.float32
F32R = mybir.dt.float32r
BF16 = mybir.dt.bfloat16
I32 = mybir.dt.int32
U32 = mybir.dt.uint32
ALU = mybir.AluOpType
ACT = mybir.ActivationFunctionType
X = mybir.AxisListType.X

P = 128
D = 128
GB = 2
T = GB * P
H1, E1 = 8, 16
H2, E2 = 16, 8
NE, FE = 16, 64
NJ = NE * FE // P
NBLK = NJ + 1
MASKED = -1e9
LN_EPS = 1e-5
RMS_EPS = 1e-8
HEADS_OF = [(0, 6), (6, 12), (12, 16)]
NLG = len(HEADS_OF)
CHUNKS_OF = [(0, 4), (4, 8), (8, 10)]
NPT = len(CHUNKS_OF)
NROWS = NJ // 2
SHARED = [(what, k, lag) for what, first, end, lag in [
    ("probs", 5, 6, 2), ("queries", 0, 1, 1), ("logits", 0, 3, 1), ("att2_T", 0, 1, 2),
    ("logits", 3, 4, 1), ("projection", 0, 1, 2), ("logits", 4, 6, 1), ("x2_T", 0, 1, 2),
    ("probs", 0, 5, 1)
] for k in range(first, end)]
SHARED_PLACE = {(what, k): n for n, (what, k, lag) in enumerate(SHARED)}
assert len(SHARED) % 2 == 0


def decoder_layer(nc, x, xT, ctxT, gp, mask, wqT, wkT, wuvT, woT, bq, bk, bu, bv, bo, scale,
                  xwq, xbq, xwk, xbk, xwv, xbv, xwo, xbo, routerT, router_b, up, gate, down,
                  sh_gateT, sh_upT, sh_downT, v_scratch, out):
    NB, SK = ctxT.shape[1], ctxT.shape[2]
    NG = NB // GB
    KT = GB * SK
    NC = -(-H2 * SK // P)
    LAST = H2 * SK - (NC - 1) * P

    ctx = ExitStack()
    with ctx:
        def sb(name, shape, dt=F32):
            return ctx.enter_context(nc.sbuf_tensor(name, shape, dt))

        def sem(name):
            return ctx.enter_context(nc.semaphore(name))

        w_qT, w_kT, w_oT = (sb(n, [P, D]) for n in ("w_qT", "w_kT", "w_oT"))
        w_uvT = sb("w_uvT", [P, 2 * D])
        w_xq, w_xk, w_xv, w_xo = (sb(n, [P, D]) for n in ("w_xq", "w_xk", "w_xv", "w_xo"))
        w_routerT = sb("w_routerT", [P, NE])
        w_gate, w_up, w_down = (sb(n, [P, NBLK, P]) for n in ("w_gate", "w_up", "w_down"))
        w_q_parts, w_k_parts = (sb(n, [P, 2, D], F32R) for n in ("w_q_parts", "w_k_parts"))
        w_uv_parts = sb("w_uv_parts", [P, 2, 2 * D], F32R)
        w_gate_parts, w_up_parts = (sb(n, [P, 2, NBLK, P], F32R) for n in ("w_gate_parts", "w_up_parts"))
        b_cols = sb("b_cols", [P, 5])
        b_uv = sb("b_uv", [P, 2 * D])
        b_o = sb("b_o", [P, D])
        half_scale = sb("half_scale", [P, D])
        b_xv = sb("b_xv", [P, D])
        b_xo = sb("b_xo", [P, D])
        b_router = sb("b_router", [P, NE])
        ones = sb("ones", [P, D])
        ident = sb("ident", [P, D])
        ident16 = sb("ident16", [P, D], BF16)
        causal = sb("causal", [P, D])
        head_rows1 = sb("head_rows1", [P, H1])
        head_rows2 = sb("head_rows2", [P, H2])
        expert_no = sb("expert_no", [P, NE])
        expert_i = sb("expert_i", [P, NE], I32)
        pick_expert = sb("pick_expert", [3 * NE, NJ, P], BF16)
        half_power = sb("half_power", [P, GB])
        minus_half_power = sb("minus_half_power", [P, GB])

        x_tok = sb("x_tok", [P, GB, D])
        x_T = sb("x_T", [P, T])
        x_parts = sb("x_parts", [P, 2, T], F32R)
        ctx_T = sb("ctx_T", [P, KT])
        gprob = sb("gprob", [P, GB, SK])
        mask_i = sb("mask_i", [P, GB, SK], I32)

        exp_qk = sb("exp_qk", [P, 2, T])
        q1 = sb("q1", [P, T])
        k1 = sb("k1", [P, T])
        q1_heads = sb("q1_heads", [P, 2, H1, P])
        uv = sb("uv", [P, GB, 2 * D])
        tanh_uv = sb("tanh_uv", [P, GB, 2 * D])
        u_scaled = sb("u_scaled", [P, GB, D])
        x_bo = sb("x_bo", [P, GB, D])
        energy = sb("energy", [P, 2, H1, P])
        sq = sb("sq", [P, D])
        sumsq = sb("sumsq", [P, GB])
        rms = sb("rms", [P, GB])
        rms_inv = sb("rms_inv", [P, GB])
        gated = sb("gated", [P, GB, D])
        gated_T = sb("gated_T", [P, T])
        y1 = sb("y1", [P, GB, D])
        x1 = sb("x1", [P, GB, D])
        x1_bo = sb("x1_bo", [P, GB, D])
        x1_T = sb("x1_T", [P, T])
        stats1 = sb("stats1", [P, GB, 6])
        moments1 = sb("moments1", [P, GB, 2])
        var_eps1 = sb("var_eps1", [P, GB])
        rstd1 = sb("rstd1", [P, GB])
        stats2 = sb("stats2", [P, GB, 6])
        moments2 = sb("moments2", [P, GB, 2])
        var_eps2 = sb("var_eps2", [P, GB])
        rstd2 = sb("rstd2", [P, GB])

        neg = sb("neg", [P, GB, SK])
        q2_T = sb("q2_T", [P, T])
        k2_T = sb("k2_T", [P, KT])
        k2_heads = sb("k2_heads", [P, GB, H2, SK])
        v2 = sb("v2", [SK, GB, D])
        logit = sb("logit", [P, 2, H2, SK])
        shifted = sb("shifted", [P, 2, NC * P])
        neg_max = sb("neg_max", [P, 2, H2])
        prob_sum = sb("prob_sum", [P, GB, H2])
        prob_inv = sb("prob_inv", [P, GB, H2])
        prob_T = sb("prob_T", [P, 2, NC, P])
        v_rows = sb("v_rows", [P, GB, NC, E2])
        v_blocks = sb("v_blocks", [P, GB, NC, D])
        chunk_heads = sb("chunk_heads", [P, NC, H2])
        att2 = sb("att2", [P, GB, D])
        att2_T = sb("att2_T", [P, T])
        y2 = sb("y2", [P, GB, D])
        x2 = sb("x2", [P, GB, D])
        x2_T = sb("x2_T", [P, T])
        x2_parts = sb("x2_parts", [P, 2, T], F32R)

        score = sb("score", [P, GB, NE])
        top8 = sb("top8", [P, GB, 8])
        top_i = sb("top_i", [P, GB, 8], U32)
        top_f = sb("top_f", [P, GB, 8])
        gap = sb("gap", [P, GB])
        exp_gap = sb("exp_gap", [P, GB])
        wait_column = sb("wait_column", [P, 1])
        one_plus = sb("one_plus", [P, GB])
        w_top = sb("w_top", [P, 2, GB])
        hit = sb("hit", [P, 2, GB, NE])
        comb_2 = sb("comb_2", [P, 2, GB, NE])
        combine = sb("combine", [P, 3, GB, NE])
        comb_parts = sb("comb_parts", [P, GB, 3, NE], BF16)
        comb_T = sb("comb_T", [3 * NE, T], BF16)
        weight_rows = sb("weight_rows", [P, NJ, T])
        tanh_g = sb("tanh_g", [P, 2, T])
        silu_g = sb("silu_g", [P, 2, T])
        hidden = sb("hidden", [P, 2, T])
        hidden_w = sb("hidden_w", [P, 2, T])
        moe_T = sb("moe_T", [P, T])
        x2_kept = sb("x2_kept", [P, GB, D])
        y3 = sb("y3", [P, GB, D])
        y_out = sb("y_out", [P, GB, D])
        stats3 = sb("stats3", [P, GB, 6])
        moments3 = sb("moments3", [P, GB, 2])
        var_eps3 = sb("var_eps3", [P, GB])
        rstd3 = sb("rstd3", [P, GB])

        def bank(name):
            return ctx.enter_context(nc.psum_tensor(name, [P, 2 * T], F32))

        first_a, first_b = bank("first_a"), bank("first_b")
        second_pair = [bank("second_a"), bank("second_b")]
        second_out = bank("second_out")
        experts_pair = [bank("experts_a"), bank("experts_b")]
        experts_out = bank("experts_out")

        def by_batch(bank):
            return bank[:, 0:T].rearrange("p (b d) -> p b d", b=GB)

        weights1_in, weights2_in, weights3_in = sem("weights1_in"), sem("weights2_in"), sem("weights3_in")
        consts_pool = sem("consts_pool")
        pick_ready = sem("pick_ready")
        consts_dve = sem("consts_dve")
        q_bias_ready = sem("q_bias_ready")
        waited = sem("waited")
        x_T_in, x_in, ctx_in, gp_in, mask_in = (sem(n) for n in ("x_T_in", "x_in", "ctx_in", "gp_in", "mask_in"))
        out_written = sem("out_written")
        x_hi_ready, x_lo_ready, x2_hi_ready, x2_lo_ready = (
            sem(n) for n in ("x_hi_ready", "x_lo_ready", "x2_hi_ready", "x2_lo_ready"))
        weights_hi_ready, weights_lo_ready = sem("weights_hi_ready"), sem("weights_lo_ready")
        v_stored, v_rows_in, v_blocks_ready, fill_ready, chunk_heads_ready = (
            sem(n) for n in ("v_stored", "v_rows_in", "v_blocks_ready", "fill_ready", "chunk_heads_ready"))
        VLOADS = 2 * GB
        qk1_done, uv_done, k2_done, v2_done = (sem(n) for n in ("qk1_done", "uv_done", "k2_done", "v2_done"))
        energy_done, pv1_done, gT_done, proj1_done = (
            sem(n) for n in ("energy_done", "pv1_done", "gT_done", "proj1_done"))
        kept_ready = sem("kept_ready")
        x1T_done, q2_done, logits_done, probT_done, pv2_done = (
            sem(n) for n in ("x1T_done", "q2_done", "logits_done", "probT_done", "pv2_done"))
        aT_done, proj2_done, x2T_done = (sem(n) for n in ("aT_done", "proj2_done", "x2T_done"))
        router_done, combT_done, rows_done, gu_done, down_done, moe_back = (
            sem(n) for n in ("router_done", "combT_done", "rows_done", "gu_done", "down_done", "moe_back"))
        exp_qk_ready, tanh_uv_ready, k2_ready, sumsq_ready, gT_ready, x1T_ready, q2_ready = (
            sem(n) for n in ("exp_qk_ready", "tanh_uv_ready", "k2_ready", "sumsq_ready", "gT_ready",
                             "x1T_ready", "q2_ready"))
        exp2_ready, probT_ready, aT_ready, x2T_ready = (
            sem(n) for n in ("exp2_ready", "probT_ready", "aT_ready", "x2T_ready"))
        exp_gap_ready, combT_ready, rows_ready, tanh_g_ready, moeT_ready = (
            sem(n) for n in ("exp_gap_ready", "combT_ready", "rows_ready", "tanh_g_ready", "moeT_ready"))
        qk1_ready, uv_biased, uv_ready, v2_ready, energy_ready = (
            sem(n) for n in ("qk1_ready", "uv_biased", "uv_ready", "v2_ready", "energy_ready"))
        elu_part, rms_eps_added, rms_inv_ready, gated_ready, y1_ready, mom1_ready, x1_ready = (
            sem(n) for n in ("elu_part", "rms_eps_added", "rms_inv_ready", "gated_ready", "y1_ready",
                             "mom1_ready", "x1_ready"))
        neg_ready, logit_ready, max_ready, sum_ready, inv_ready, att2_ready = (
            sem(n) for n in ("neg_ready", "logit_ready", "max_ready", "sum_ready", "inv_ready", "att2_ready"))
        y2_ready, mom2_ready, x2_ready, split_step = (
            sem(n) for n in ("y2_ready", "mom2_ready", "x2_ready", "split_step"))
        route_step, gap_ready, parts_ready, silu_ready, hidden_ready, y3_ready, mom3_ready, out_ready = (
            sem(n) for n in ("route_step", "gap_ready", "parts_ready", "silu_ready", "hidden_ready",
                             "y3_ready", "mom3_ready", "out_ready"))
        q1_heads_ready, u_scaled_ready, x_bo_ready, rms_ready, rstd1_ready, x1_bo_ready = (
            sem(n) for n in ("q1_heads_ready", "u_scaled_ready", "x_bo_ready", "rms_ready", "rstd1_ready",
                             "x1_bo_ready"))
        k2_heads_ready, shifted_ready, prob_ready, rstd2_ready, hidden_w_ready, rstd3_ready = (
            sem(n) for n in ("k2_heads_ready", "shifted_ready", "prob_ready", "rstd2_ready",
                             "hidden_w_ready", "rstd3_ready"))

        def at(i, per, k):
            count = i * per + k
            return max(count, 0) if isinstance(count, int) else count

        def runs(t, lag):
            return not isinstance(t, int) or 0 <= t - lag < NG

        def shared(what, k):
            return second_pair[SHARED_PLACE[what, k] % 2]

        def heads_of(ap, n, h, e):
            return ap.unsqueeze(2).broadcast_to([n, h, e])

        loads1 = [
            (w_qT[:, :], wqT), (w_kT[:, :], wkT),
            (b_cols[:, 0:1], bq.unsqueeze(1)), (b_cols[:, 1:2], bk.unsqueeze(1)), (w_uvT[:, :], wuvT),
            (b_uv[:, 0:D], bu.partition_broadcast(P)), (b_uv[:, D:2 * D], bv.partition_broadcast(P)),
            (half_scale[:, :], scale.partition_broadcast(P)), (w_oT[:, :], woT), (b_o[:, :], bo.partition_broadcast(P)),
            (w_xk[:, :], xwk), (b_cols[:, 3:4], xbk.unsqueeze(1)),
        ]
        loads2 = [
            (w_xq[:, :], xwq), (b_cols[:, 2:3], xbq.unsqueeze(1)), (w_xv[:, :], xwv),
            (b_xv[:, :], xbv.partition_broadcast(P)), (b_xo[:, :], xbo.partition_broadcast(P)), (w_xo[:, :], xwo),
        ]
        loads3 = [
            (w_routerT[:, :], routerT), (b_router[:, :], router_b.partition_broadcast(P)),
            (w_gate[:, 0:NJ, :].rearrange("p j (t e) -> p (j t) e", e=FE), gate.rearrange("k d e -> d k e")),
            (w_up[:, 0:NJ, :].rearrange("p j (t e) -> p (j t) e", e=FE), up.rearrange("k d e -> d k e")),
            (w_down[:, 0:NJ, :], down.rearrange("(j t) e d -> (t e) j d", t=2)),
            (w_gate[:, NJ, :], sh_gateT), (w_up[:, NJ, :], sh_upT), (w_down[:, NJ, :], sh_downT),
        ]
        ALL1, ALL2, ALL3 = 16 * len(loads1), 16 * len(loads2), 16 * len(loads3)

        PART_PAIRS = [(1, 0), (0, 1), (0, 0)]

        def parts_matmul(pe, dst, lhsT_parts, rhs_parts, first=True, last=True):
            for n, (a, b) in enumerate(PART_PAIRS):
                mm = pe.matmul(dst, lhsT_parts(a), rhs_parts(b), start=(first and n == 0), stop=(last and n == 2))
            return mm

        block = ctx.enter_context(nc.Block())

        @block.sync
        def _(sp):
            def load_x_T(i):
                sp.wait_ge(x_lo_ready, at(i, 1, 0))
                sp.dma_start(x_T[:, :], xT[:, bass.ds(i * T, T)]).then_inc(x_T_in, 16)

            def load_x(i):
                sp.wait_ge(x_bo_ready, at(i, 1, 0))
                sp.dma_start(x_tok[:, :, :], x[bass.ds(i * GB, GB)].rearrange("b p d -> p b d"))\
                  .then_inc(x_in, 16)

            def load_context(i):
                sp.wait_ge(v2_done, at(i, 1, 0))
                sp.wait_ge(k2_done, at(i, 1, 0))
                sp.dma_start(ctx_T[:, :], ctxT[:, bass.ds(i * GB, GB), :].rearrange("p b k -> p (b k)"))\
                  .then_inc(ctx_in, 16)

            def load_mask(i):
                sp.wait_ge(neg_ready, at(i, 1, 0))
                sp.dma_start(mask_i[:, :, :], mask[bass.ds(i * GB, GB)].rearrange("b p k -> p b k"))\
                  .then_inc(mask_in, 16)

            def load_gprob(i):
                sp.wait_ge(prob_ready, at(i, GB, 0))
                sp.dma_start(gprob[:, :, :], gp[bass.ds(i * GB, GB)].rearrange("b p k -> p b k"))\
                  .then_inc(gp_in, 16)

            def store_group(i):
                sp.wait_ge(out_ready, at(i, GB, GB))
                sp.dma_start(out[bass.ds(i * GB, GB)].rearrange("b p d -> p b d"), y_out[:, :, :])\
                  .then_inc(out_written, 16)

            def reorder_values(i):
                sp.wait_ge(v2_ready, at(i, 1, 1))
                sp.dma_start(v_scratch.rearrange("b (h k) e -> k b h e", h=H2),
                             v2[:, :, :].rearrange("k b (h e) -> k b h e", e=E2)).then_inc(v_stored, 16)
                sp.wait_ge(v_stored, at(i, 16, 16))
                for b in range(GB):
                    sp.dma_start(v_rows[:, b, 0:NC - 1, :],
                                 v_scratch[b, 0:(NC - 1) * P, :].rearrange("(n p) e -> p n e", p=P))\
                      .then_inc(v_rows_in, 16)
                    sp.dma_start(v_rows[0:LAST, b, NC - 1, :], v_scratch[b, (NC - 1) * P:H2 * SK, :])\
                      .then_inc(v_rows_in, 16)

            def turn(t, load_next):
                if runs(t, 1):
                    load_gprob(t - 1)
                if runs(t, 0):
                    load_mask(t)
                    load_context(t)
                if runs(t, 1):
                    reorder_values(t - 1)
                if load_next:
                    load_x_T(t + 1)
                    load_x(t + 1)
                if runs(t, 3):
                    store_group(t - 3)

            load_x_T(0)
            for dst, src in loads1:
                sp.dma_start(dst, src).then_inc(weights1_in, 16)
            load_x(0)
            load_mask(0)
            load_context(0)
            for dst, src in loads2:
                sp.dma_start(dst, src).then_inc(weights2_in, 16)
            for dst, src in loads3:
                sp.dma_start(dst, src).then_inc(weights3_in, 16)
            load_x_T(1)
            load_x(1)
            sp.wait_ge(fill_ready, 4)
            for t in range(1, 4):
                turn(t, True)
            with sp.Fori(4, NG - 1) as t:
                turn(t, True)
            for t in range(NG - 1, NG + 3):
                turn(t, False)
            sp.wait_ge(v_stored, 16 * NG)
            sp.wait_ge(out_written, 16 * NG)

        @block.tensor
        def _(pe):
            def router(i):
                pe.wait_ge(x2T_ready, at(i, 1, 1))
                pe.wait_ge(hidden_ready, at(i, NBLK, 0))
                for b in range(GB):
                    mm = pe.matmul(experts_pair[0][:, NE * b:NE * b + NE], x2_T[:, P * b:P * b + P],
                                   w_routerT[:, :], start=True, stop=True)
                mm.then_inc(router_done, 1)

            def combine_transpose(i):
                pe.wait_ge(pick_ready, 3)
                pe.wait_ge(parts_ready, at(i, 1, 1))
                pe.wait_ge(moeT_ready, at(i, 1, 0))
                view = experts_out[:, :].bitcast(BF16)
                for b in range(GB):
                    mm = pe.transpose(view[0:3 * NE, P * b:P * b + P],
                                      comb_parts[:, b, :, :].rearrange("p s e -> p (s e)"), ident16[:, :])
                mm.then_inc(combT_done, 1)

            def combine_rows(i, k):
                if k == 0:
                    pe.wait_ge(combT_ready, at(i, 1, 1))
                    pe.wait_ge(y3_ready, at(i, 1, 0))
                elif k == 1:
                    pe.wait_ge(gap_ready, at(i, 1, 1))
                else:
                    pe.wait_ge(rows_ready, at(i, NROWS, k - 1))
                for j in (2 * k, 2 * k + 1):
                    mm = pe.matmul(experts_pair[(k + 1) % 2][:, T * (j % 2):T * (j % 2) + T], pick_expert[:, j, :],
                                   comb_T[:, :], start=True, stop=True)
                mm.then_inc(rows_done, 1)

            def gate_up(i, j):
                if j == 0:
                    pe.wait_ge(x2_lo_ready, at(i, 1, 1))
                    pe.wait_ge(rows_ready, at(i, NROWS, NROWS))
                elif j >= 2:
                    pe.wait_ge(hidden_ready, at(i, NBLK, j - 1))
                dst = experts_pair[j % 2]
                parts_matmul(pe, dst[:, 0:T], lambda a: w_gate_parts[:, a, j, :], lambda b: x2_parts[:, b, :])
                parts_matmul(pe, dst[:, T:2 * T], lambda a: w_up_parts[:, a, j, :], lambda b: x2_parts[:, b, :])\
                    .then_inc(gu_done, 1)

            def expert_down(i, j):
                if j < NJ:
                    pe.wait_ge(hidden_w_ready, at(i, NJ, j + 1))
                else:
                    pe.wait_ge(hidden_ready, at(i, NBLK, NBLK))
                h = hidden_w if j < NJ else hidden
                pe.matmul(experts_out[:, 0:T], w_down[:, j, :], h[:, j % 2, :], start=(j == 0),
                          stop=(j == NBLK - 1)).then_inc(down_done, 1)

            def moe_transpose(i):
                pe.wait_ge(moeT_ready, at(i, 1, 1))
                for b in range(GB):
                    mm = pe.transpose(experts_pair[1][:, P * b:P * b + P], moe_T[:, P * b:P * b + P], ident[:, :])
                mm.then_inc(moe_back, 1)

            def project_qk(i):
                pe.wait_ge(x_lo_ready, at(i, 1, 1))
                pe.wait_ge(y1_ready, at(i, 1, 0))
                parts_matmul(pe, first_a[:, 0:T], lambda a: w_q_parts[:, a, :], lambda b: x_parts[:, b, :])
                parts_matmul(pe, first_a[:, T:2 * T], lambda a: w_k_parts[:, a, :], lambda b: x_parts[:, b, :])\
                    .then_inc(qk1_done, 1)

            def project_uv(i):
                pe.wait_ge(v2_ready, at(i, 1, 0))
                for n in range(GB):
                    mm = parts_matmul(pe, first_b[:, 2 * D * n:2 * D * n + 2 * D],
                                      lambda a: x_parts[:, a, P * n:P * n + P], lambda b: w_uv_parts[:, b, :])
                mm.then_inc(uv_done, 1)

            def context_keys(i):
                pe.wait_ge(ctx_in, at(i, 16, 16))
                pe.wait_ge(energy_ready, at(i, 2 * GB, 2 * GB))
                pe.matmul(first_a[:, 0:KT], w_xk[:, :], ctx_T[:, :], start=True, stop=True).then_inc(k2_done, 1)

            def context_values(i):
                pe.wait_ge(x1T_ready, at(i, 1, 1))
                for b in range(GB):
                    mm = pe.matmul(first_b[0:SK, P * b:P * b + P], ctx_T[:, SK * b:SK * b + SK], w_xv[:, :],
                                   start=True, stop=True)
                mm.then_inc(v2_done, 1)

            def energies(i, b, c):
                if c == 0:
                    pe.wait_ge(q1_heads_ready, at(i, GB, b + 1))
                if b == 0 and c == 0:
                    pe.wait_ge(qk1_ready, at(i, 2, 2))
                else:
                    pe.wait_ge(energy_ready, at(i, 2 * GB, 2 * b + c))
                pe.matmul(first_a[:, :], k1[:, P * b:P * b + P],
                          q1_heads[:, b % 2, 4 * c:4 * c + 4, :].rearrange("p h n -> p (h n)"),
                          start=True, stop=True).then_inc(energy_done, 1)

            def values_first(i, b, c):
                pe.wait_ge(energy_ready, at(i, 2 * GB, 2 * b + c + 1))
                if b == 0 and c == 0:
                    pe.wait_ge(uv_ready, at(i, 1, 1))
                for h in range(4 * c, 4 * c + 4):
                    o = D * b + E1 * h
                    mm = pe.matmul(first_b[:, o:o + E1], energy[:, b % 2, h, :],
                                   uv[:, b, D + E1 * h:D + E1 * h + E1], start=True, stop=True)
                mm.then_inc(pv1_done, 1)

            def gated_transpose(i):
                pe.wait_ge(k2_ready, at(i, 1, 1))
                pe.wait_ge(gated_ready, at(i, GB, GB))
                for b in range(GB):
                    mm = pe.transpose(first_a[:, P * b:P * b + P], gated[:, b, :], ident[:, :])
                mm.then_inc(gT_done, 1)

            def output_first(i):
                pe.wait_ge(gT_ready, at(i, 1, 1))
                for b in range(GB):
                    mm = pe.matmul(first_a[:, P * b:P * b + P], gated_T[:, P * b:P * b + P], w_oT[:, :],
                                   start=True, stop=True)
                mm.then_inc(proj1_done, 1)

            def x1_transpose(i):
                pe.wait_ge(x1_ready, at(i, GB, GB))
                for b in range(GB):
                    mm = pe.transpose(first_b[:, P * b:P * b + P], x1[:, b, :], ident[:, :])
                mm.then_inc(x1T_done, 1)

            def queries_second(i):
                pe.wait_ge(x1T_ready, at(i, 1, 1))
                shared_bank_free(i, "queries", 0)
                pe.matmul(shared("queries", 0)[:, 0:T], w_xq[:, :], x1_T[:, :], start=True, stop=True)\
                  .then_inc(q2_done, 1)

            def shared_bank_free(group, what, k):
                n = SHARED_PLACE[what, k] - 2
                t = group + SHARED[n + 2][2]
                while True:
                    last, number, lag = SHARED[n % len(SHARED)]
                    i = t - lag if n >= 0 else t - 1 - lag
                    if not isinstance(i, int) or 0 <= i < NG:
                        break
                    n -= 2
                    if n < -len(SHARED):
                        return
                if last == "queries":
                    pe.wait_ge(q2_ready, at(i, 1, 1))
                elif last == "logits":
                    pe.wait_ge(logit_ready, at(i, NLG * GB, number + 1))
                elif last == "probs":
                    pe.wait_ge(probT_ready, at(i, NPT * GB, number + 1))
                elif last == "att2_T":
                    pe.wait_ge(aT_ready, at(i, 1, 1))
                elif last == "projection":
                    pe.wait_ge(y2_ready, at(i, 1, 1))
                else:
                    pe.wait_ge(x2T_ready, at(i, 1, 1))

            def logits(i, b, g):
                h0, h1 = HEADS_OF[g]
                if b == 0 and g == 0:
                    pe.wait_ge(q2_ready, at(i, 1, 1))
                if g == 0:
                    pe.wait_ge(k2_heads_ready, at(i, GB, b + 1))
                shared_bank_free(i, "logits", NLG * b + g)
                pe.matmul(shared("logits", NLG * b + g)[:, 0:SK * (h1 - h0)], q2_T[:, P * b:P * b + P],
                          k2_heads[:, b, h0:h1, :].rearrange("p h k -> p (h k)"),
                          start=True, stop=True).then_inc(logits_done, 1)

            def prob_transposes(i, b, c):
                if b == 0 and c == 0:
                    pe.wait_ge(fill_ready, 4)
                if c == 0:
                    pe.wait_ge(prob_ready, at(i, GB, b + 1))
                shared_bank_free(i, "probs", NPT * b + c)
                for n in range(*CHUNKS_OF[c]):
                    mm = pe.transpose(shared("probs", NPT * b + c)[:, P * (n % 4):P * (n % 4) + P],
                                      shifted[:, b % 2, P * n:P * n + P], ident[:, :])
                mm.then_inc(probT_done, 1)

            def values_second(i, b, c):
                if c == 0:
                    pe.wait_ge(v_blocks_ready, at(i, GB, b + 1))
                if b == 0 and c == 0:
                    pe.wait_ge(att2_ready, at(i, 1, 0))
                pe.wait_ge(probT_ready, at(i, NPT * GB, NPT * b + c + 1))
                for n in range(*CHUNKS_OF[c]):
                    mm = pe.matmul(second_out[:, D * b:D * b + D], prob_T[:, b % 2, n, :], v_blocks[:, b, n, :],
                                   start=(n == 0), stop=(n == NC - 1))
                mm.then_inc(pv2_done, 1)

            def att2_transpose(i):
                pe.wait_ge(att2_ready, at(i, 1, 1))
                shared_bank_free(i, "att2_T", 0)
                for b in range(GB):
                    mm = pe.transpose(shared("att2_T", 0)[:, P * b:P * b + P], att2[:, b, :], ident[:, :])
                mm.then_inc(aT_done, 1)

            def output_second(i):
                pe.wait_ge(aT_ready, at(i, 1, 1))
                shared_bank_free(i, "projection", 0)
                for b in range(GB):
                    mm = pe.matmul(shared("projection", 0)[:, P * b:P * b + P], att2_T[:, P * b:P * b + P],
                                   w_xo[:, :], start=True, stop=True)
                mm.then_inc(proj2_done, 1)

            def x2_transpose(i):
                pe.wait_ge(x2_ready, at(i, GB, GB))
                shared_bank_free(i, "x2_T", 0)
                for b in range(GB):
                    mm = pe.transpose(shared("x2_T", 0)[:, P * b:P * b + P], x2[:, b, :], ident[:, :])
                mm.then_inc(x2T_done, 1)

            def turn(t):
                i, s, r, m = t, t - 1, t - 2, t - 3
                if runs(t, 3):
                    gate_up(m, 0)
                    gate_up(m, 1)
                if runs(t, 2):
                    prob_transposes(r, 1, 2)
                    values_second(r, 1, 1)
                    values_second(r, 1, 2)
                if runs(t, 3):
                    gate_up(m, 2)
                    expert_down(m, 0)
                if runs(t, 1):
                    x1_transpose(s)
                if runs(t, 3):
                    gate_up(m, 3)
                if runs(t, 1):
                    queries_second(s)
                    context_values(s)
                if runs(t, 3):
                    gate_up(m, 4)
                if runs(t, 1):
                    logits(s, 0, 0)
                if runs(t, 3):
                    expert_down(m, 1)
                if runs(t, 1):
                    logits(s, 0, 1)
                    logits(s, 0, 2)
                if runs(t, 3):
                    gate_up(m, 5)
                if runs(t, 0):
                    project_qk(i)
                if runs(t, 2):
                    att2_transpose(r)
                if runs(t, 3):
                    expert_down(m, 2)
                if runs(t, 1):
                    logits(s, 1, 0)
                if runs(t, 2):
                    output_second(r)
                if runs(t, 0):
                    project_uv(i)
                if runs(t, 3):
                    gate_up(m, 6)
                    expert_down(m, 3)
                    expert_down(m, 4)
                if runs(t, 1):
                    logits(s, 1, 1)
                if runs(t, 3):
                    gate_up(m, 7)
                if runs(t, 0):
                    energies(i, 0, 0)
                if runs(t, 1):
                    logits(s, 1, 2)
                if runs(t, 3):
                    gate_up(m, 8)
                    expert_down(m, 5)
                if runs(t, 0):
                    energies(i, 0, 1)
                if runs(t, 2):
                    x2_transpose(r)
                if runs(t, 0):
                    values_first(i, 0, 0)
                if runs(t, 3):
                    expert_down(m, 6)
                if runs(t, 0):
                    energies(i, 1, 0)
                    values_first(i, 0, 1)
                if runs(t, 1):
                    prob_transposes(s, 0, 0)
                if runs(t, 0):
                    energies(i, 1, 1)
                if runs(t, 2):
                    router(r)
                if runs(t, 0):
                    values_first(i, 1, 0)
                if runs(t, 3):
                    expert_down(m, 7)
                    expert_down(m, 8)
                if runs(t, 1):
                    prob_transposes(s, 0, 1)
                if runs(t, 0):
                    values_first(i, 1, 1)
                if runs(t, 1):
                    values_second(s, 0, 0)
                if runs(t, 3):
                    moe_transpose(m)
                if runs(t, 1):
                    prob_transposes(s, 0, 2)
                if runs(t, 0):
                    context_keys(i)
                if runs(t, 2):
                    combine_transpose(r)
                if runs(t, 1):
                    values_second(s, 0, 1)
                if runs(t, 2):
                    combine_rows(r, 0)
                    combine_rows(r, 1)
                if runs(t, 1):
                    values_second(s, 0, 2)
                    prob_transposes(s, 1, 0)
                if runs(t, 2):
                    combine_rows(r, 2)
                    combine_rows(r, 3)
                if runs(t, 1):
                    prob_transposes(s, 1, 1)
                if runs(t, 0):
                    gated_transpose(i)
                if runs(t, 1):
                    values_second(s, 1, 0)
                if runs(t, 0):
                    output_first(i)

            pe.wait_ge(weights1_in, ALL1)
            pe.wait_ge(consts_pool, 12)
            pe.wait_ge(pick_ready, 3)
            pe.wait_ge(weights_lo_ready, 3)
            turn(0)
            pe.wait_ge(weights2_in, ALL2)
            turn(1)
            pe.wait_ge(weights3_in, ALL3)
            pe.wait_ge(weights_lo_ready, 5)
            turn(2)
            turn(3)
            with pe.Fori(4, NG) as t:
                turn(t)
            for t in range(NG, NG + 3):
                turn(t)

        @block.scalar
        def _(act):
            def q_bias():
                act.wait_ge(weights2_in, ALL2)
                act.mul(b_cols[:, 4:5], b_cols[:, 2:3], E2 ** -0.5).then_inc(q_bias_ready, 1)
                act.wait_ge(q_bias_ready, 1)

            def exp_first(i):
                act.wait_ge(qk1_ready, at(i, 2, 0))
                for c in range(2):
                    act.wait_ge(qk1_done, at(i, 1, 1))
                    act.activation(exp_qk[:, c, :], first_a[:, T * c:T * c + T], ACT.Exp, bias=b_cols[:, c:c + 1])\
                       .then_inc(exp_qk_ready, 1)

            def keys_second(i):
                act.wait_ge(k2_done, at(i, 1, 1))
                act.wait_ge(k2_heads_ready, at(i, GB, 0))
                act.activation(k2_T[:, :], first_a[:, 0:KT], ACT.Identity, bias=b_cols[:, 3:4])\
                   .then_inc(k2_ready, 1)

            def tanh_first(i):
                act.wait_ge(uv_biased, at(i, 1, 1))
                act.activation(tanh_uv[:, :, :], uv[:, :, :], ACT.Tanh, scale=0.5)\
                   .then_inc(tanh_uv_ready, 1)

            def squares(i):
                act.wait_ge(pv1_done, at(i, 2 * GB, 2 * GB))
                for b in range(GB):
                    if b:
                        act.wait_ge(sumsq_ready, at(i, GB, b))
                    act.activation(sq[:, :], by_batch(first_b)[:, b, :], ACT.Square, scale=D ** -0.5,
                                   accum_out=sumsq[:, b:b + 1])\
                       .then_inc(sumsq_ready, 1)

            def copy(i, done, bank, dst, ready):
                act.wait_ge(done, at(i, 1, 1))
                act.activation(dst[:, :], bank[:, 0:T], ACT.Copy).then_inc(ready, 1)

            def queries(i):
                act.wait_ge(q2_done, at(i, 1, 1))
                act.activation(q2_T[:, :], shared("queries", 0)[:, 0:T], ACT.Identity,
                               bias=b_cols[:, 4:5], scale=E2 ** -0.5)\
                   .then_inc(q2_ready, 1)

            def exp_second(i, b):
                act.wait_ge(shifted_ready, at(i, GB, b + 1))
                act.activation(logit[:, b % 2, :, :].rearrange("p h k -> p (h k)"), shifted[:, b % 2, 0:H2 * SK],
                               ACT.Exp).then_inc(exp2_ready, 1)

            def copy_probs(i, b, c):
                act.wait_ge(probT_done, at(i, NPT * GB, NPT * b + c + 1))
                act.wait_ge(pv2_done, at(i, NPT * GB, NPT * (b - 2) + c + 1))
                n0, n1 = CHUNKS_OF[c]
                act.activation(prob_T[:, b % 2, n0:n1, :].rearrange("k n p -> k (n p)"),
                               shared("probs", NPT * b + c)[:, 0:P * (n1 - n0)], ACT.Copy).then_inc(probT_ready, 1)

            def exp_gap_of(i):
                act.wait_ge(gap_ready, at(i, 1, 1))
                act.activation(exp_gap[:, :], gap[:, :], ACT.Exp).then_inc(exp_gap_ready, 1)

            def keep_residual(i):
                act.wait_ge(x2_ready, at(i, GB, GB))
                act.wait_ge(y3_ready, at(i, 1, 0))
                act.activation(x2_kept[:, :, :], x2[:, :, :], ACT.Copy).then_inc(kept_ready, 1)

            def copy_combine(i):
                act.wait_ge(combT_done, at(i, 1, 1))
                act.activation(comb_T[:, :], experts_out[:, :].bitcast(BF16)[0:3 * NE, 0:T], ACT.Copy)\
                   .then_inc(combT_ready, 1)

            def copy_rows(i, k):
                act.wait_ge(rows_done, at(i, NROWS, k + 1))
                act.wait_ge(hidden_w_ready, at(i, NJ, 0))
                act.activation(weight_rows[:, 2 * k:2 * k + 2, :].rearrange("p j t -> p (j t)"),
                               experts_pair[(k + 1) % 2][:, :], ACT.Copy).then_inc(rows_ready, 1)

            def tanh_gate(i, j):
                act.wait_ge(gu_done, at(i, NBLK, j + 1))
                act.wait_ge(silu_ready, at(i, NBLK, j - 1))
                act.activation(tanh_g[:, j % 2, :], experts_pair[j % 2][:, 0:T], ACT.Tanh, scale=0.5)\
                   .then_inc(tanh_g_ready, 1)

            def copy_att2(i):
                copy(i, aT_done, shared("att2_T", 0), att2_T, aT_ready)

            def copy_gated(i):
                copy(i, gT_done, first_a, gated_T, gT_ready)

            def copy_x1(i):
                copy(i, x1T_done, first_b, x1_T, x1T_ready)

            def copy_x2(i):
                act.wait_ge(router_done, at(i, 1, 0))
                act.wait_ge(x2_lo_ready, at(i, 1, 0))
                copy(i, x2T_done, shared("x2_T", 0), x2_T, x2T_ready)

            def x2_high(i):
                act.wait_ge(gu_done, at(i, NBLK, 0))
                act.wait_ge(x2T_ready, at(i, 1, 1))
                act.activation(x2_parts[:, 0, :], x2_T[:, :], ACT.Copy).then_inc(x2_hi_ready, 1)

            def x_high(i):
                act.wait_ge(x_T_in, at(i, 16, 16))
                act.wait_ge(qk1_done, at(i, 1, 0))
                act.wait_ge(uv_done, at(i, 1, 0))
                act.activation(x_parts[:, 0, :], x_T[:, :], ACT.Copy).then_inc(x_hi_ready, 1)

            def moe_out(i):
                act.wait_ge(down_done, at(i, NBLK, NBLK))
                act.activation(moe_T[:, :], experts_out[:, 0:T], ACT.Copy, scale=0.5).then_inc(moeT_ready, 1)

            def turn(t):
                i, s, r, m = t, t - 1, t - 2, t - 3
                if runs(t, 1):
                    keys_second(s)
                if runs(t, 3):
                    copy_combine(m)
                    keep_residual(m)
                    copy_rows(m, 0)
                    copy_rows(m, 1)
                if runs(t, 2):
                    copy_probs(r, 1, 0)
                if runs(t, 3):
                    copy_rows(m, 2)
                    copy_rows(m, 3)
                if runs(t, 1):
                    copy_gated(s)
                if runs(t, 2):
                    copy_probs(r, 1, 1)
                if runs(t, 3):
                    tanh_gate(m, 0)
                if runs(t, 0):
                    x_high(i)
                if runs(t, 3):
                    tanh_gate(m, 1)
                if runs(t, 2):
                    copy_probs(r, 1, 2)
                if runs(t, 3):
                    tanh_gate(m, 2)
                if runs(t, 1):
                    copy_x1(s)
                if runs(t, 3):
                    tanh_gate(m, 3)
                if runs(t, 1):
                    queries(s)
                if runs(t, 3):
                    tanh_gate(m, 4)
                    tanh_gate(m, 5)
                if runs(t, 0):
                    exp_first(i)
                if runs(t, 2):
                    copy_att2(r)
                if runs(t, 0):
                    tanh_first(i)
                if runs(t, 3):
                    tanh_gate(m, 6)
                if runs(t, 1):
                    exp_second(s, 0)
                if runs(t, 3):
                    tanh_gate(m, 7)
                    tanh_gate(m, 8)
                if runs(t, 2):
                    copy_x2(r)
                if runs(t, 1):
                    copy_probs(s, 0, 0)
                if runs(t, 2):
                    exp_gap_of(r)
                if runs(t, 3):
                    moe_out(m)
                if runs(t, 1):
                    exp_second(s, 1)
                    copy_probs(s, 0, 1)
                if runs(t, 0):
                    squares(i)
                if runs(t, 2):
                    x2_high(r)
                if runs(t, 1):
                    copy_probs(s, 0, 2)

            act.wait_ge(weights1_in, ALL1)
            turn(0)
            q_bias()
            turn(1)
            act.wait_ge(weights3_in, ALL3)
            turn(2)
            turn(3)
            with act.Fori(4, NG) as t:
                turn(t)
            for t in range(NG, NG + 3):
                turn(t)

        @block.vector
        def _(dve):
            def wait_carrier():
                dve.tensor_copy(wait_column[:, :], ones[:, 0:1]).then_inc(waited, 1)

            def route(i):
                dve.wait_ge(router_done, at(i, 1, 1))
                gs = experts_pair[0][:, 0:GB * NE].rearrange("p (b e) -> p b e", b=GB)
                dve.tensor_tensor(score[:, :, :], gs, b_router[:, :].unsqueeze(1).broadcast_to([P, GB, NE]),
                                  ALU.add).then_inc(route_step, 1)
                dve.wait_ge(route_step, at(i, 10, 1))
                wait_carrier()
                for b in range(GB):
                    mx = dve.max(top8[:, b, :], score[:, b, :])
                mx.then_inc(route_step, 1)
                dve.wait_ge(route_step, at(i, 10, 2))
                dve.tensor_tensor(gap[:, :], top8[:, :, 1], top8[:, :, 0], ALU.subtract).then_inc(gap_ready, 1)
                for b in range(GB):
                    mx = dve.max_index(top_i[:, b, :], top8[:, b, :], score[:, b, :])
                mx.then_inc(route_step, 1)
                dve.wait_ge(route_step, at(i, 10, 3))
                dve.tensor_copy(top_f[:, :, :], top_i[:, :, :]).then_inc(route_step, 1)
                dve.wait_ge(route_step, at(i, 10, 4))
                experts = expert_no[:, :].unsqueeze(1).broadcast_to([P, GB, NE])
                for r in range(2):
                    hits = dve.tensor_tensor(hit[:, r, :, :], experts, heads_of(top_f[:, :, r], P, GB, NE),
                                             ALU.is_equal)
                hits.then_inc(route_step, 1)
                dve.wait_ge(exp_gap_ready, at(i, 1, 1))
                dve.tensor_scalar(one_plus[:, :], exp_gap[:, :], 1.0, None, ALU.add).then_inc(route_step, 1)
                dve.wait_ge(route_step, at(i, 10, 6))
                dve.reciprocal(w_top[:, 0, :], one_plus[:, :]).then_inc(route_step, 1)
                dve.wait_ge(route_step, at(i, 10, 7))
                dve.tensor_tensor(w_top[:, 1, :], exp_gap[:, :], w_top[:, 0, :], ALU.mult).then_inc(route_step, 1)
                dve.wait_ge(route_step, at(i, 10, 8))
                for r in range(2):
                    w = dve.tensor_tensor(comb_2[:, r, :, :], hit[:, r, :, :],
                                          heads_of(w_top[:, r, :], P, GB, NE), ALU.mult)
                w.then_inc(route_step, 1)
                dve.wait_ge(route_step, at(i, 10, 9))
                dve.tensor_tensor(combine[:, 0, :, :], comb_2[:, 0, :, :], comb_2[:, 1, :, :], ALU.add)\
                   .then_inc(route_step, 1)
                dve.wait_ge(route_step, at(i, 10, 10))

            def combine_split(i):
                dve.wait_ge(combT_done, at(i, 1, 0))
                for s in range(2):
                    dve.tensor_copy(comb_parts[:, :, s, :], combine[:, s, :, :]).then_inc(split_step, 1)
                    dve.wait_ge(split_step, at(i, 4, 2 * s + 1))
                    dve.tensor_tensor(combine[:, s + 1, :, :], combine[:, s, :, :], comb_parts[:, :, s, :],
                                      ALU.subtract).then_inc(split_step, 1)
                    dve.wait_ge(split_step, at(i, 4, 2 * s + 2))
                dve.tensor_copy(comb_parts[:, :, 2, :], combine[:, 2, :, :]).then_inc(parts_ready, 1)

            def low_part(dst, whole, high):
                return dve.tensor_tensor(dst, whole, high.bitcast(F32), ALU.subtract)

            def x2_low(i):
                dve.wait_ge(x2_hi_ready, at(i, 1, 1))
                low_part(x2_parts[:, 1, :], x2_T[:, :], x2_parts[:, 0, :]).then_inc(x2_lo_ready, 1)

            def x_low(i):
                dve.wait_ge(x_hi_ready, at(i, 1, 1))
                low_part(x_parts[:, 1, :], x_T[:, :], x_parts[:, 0, :]).then_inc(x_lo_ready, 1)

            def split_weights(pairs, high_ready, low_ready, before):
                for whole, parts in pairs:
                    dve.tensor_copy(parts[:, 0], whole).then_inc(high_ready, 1)
                dve.wait_ge(high_ready, before + len(pairs))
                for whole, parts in pairs:
                    low_part(parts[:, 1], whole, parts[:, 0]).then_inc(low_ready, 1)

            def elu(i):
                dve.wait_ge(q1_heads_ready, at(i, GB, 0))
                dve.wait_ge(energy_done, at(i, 2 * GB, 0))
                dve.wait_ge(exp_qk_ready, at(i, 2, 2))
                for c, z in ((0, q1), (1, k1)):
                    dve.tensor_scalar(exp_qk[:, c, :], exp_qk[:, c, :], 1.0, -1.0, ALU.min, ALU.add)\
                       .then_inc(elu_part, 1)
                    dve.wait_ge(elu_part, at(i, 2, c + 1))
                    dve.scalar_tensor_tensor(out=z[:, :], in0=first_a[:, T * c:T * c + T], scalar=b_cols[:, c:c + 1],
                                             in1=exp_qk[:, c, :], op0=ALU.add, op1=ALU.max)\
                       .then_inc(qk1_ready, 1)

            def add_uv_bias(i):
                dve.wait_ge(u_scaled_ready, at(i, 1, 0))
                dve.wait_ge(pv1_done, at(i, 2 * GB, 0))
                dve.wait_ge(uv_done, at(i, 1, 1))
                dve.tensor_tensor(uv[:, :, :], first_b[:, :].rearrange("p (b n) -> p b n", b=GB),
                                  b_uv[:, :].unsqueeze(1).broadcast_to([P, GB, 2 * D]),
                                  ALU.add).then_inc(uv_biased, 1)

            def silu_uv(i):
                dve.wait_ge(tanh_uv_ready, at(i, 1, 1))
                uvf = uv[:, :, :].rearrange("p b n -> p (b n)")
                dve.scalar_tensor_tensor(out=uvf, in0=tanh_uv[:, :, :].rearrange("p b n -> p (b n)"), scalar=1.0,
                                         in1=uvf, op0=ALU.add, op1=ALU.mult).then_inc(uv_ready, 1)

            def mask_energy(i, b, c):
                dve.wait_ge(energy_done, at(i, 2 * GB, 2 * b + c + 1))
                dve.wait_ge(pv1_done, at(i, 2 * GB, 2 * (b - 2) + c + 1))
                dve.tensor_tensor(energy[:, b % 2, 4 * c:4 * c + 4, :],
                                  first_a[:, :].rearrange("p (h n) -> p h n", h=4),
                                  causal[:, :].unsqueeze(1).broadcast_to([P, 4, P]), ALU.mult)\
                   .then_inc(energy_ready, 1)

            def values_bias(i):
                dve.wait_ge(v2_done, at(i, 1, 1))
                dve.wait_ge(v_stored, at(i, 16, 0))
                dve.tensor_tensor(v2[:, :, :], by_batch(first_b)[0:SK],
                                  b_xv[0:SK, :].unsqueeze(1).broadcast_to([SK, GB, D]),
                                  ALU.add).then_inc(v2_ready, 1)

            def spread_values(i, b):
                dve.wait_ge(v_rows_in, at(i, 16 * VLOADS, 16 * VLOADS))
                dve.wait_ge(pv2_done, at(i, NPT * GB, NPT * (b + 1 - GB)))
                dve.tensor_tensor(v_blocks[:, b, :, :].rearrange("p n (h e) -> p n h e", e=E2),
                                  v_rows[:, b, :, :].unsqueeze(2).broadcast_to([P, NC, H2, E2]),
                                  chunk_heads[:, :, :].unsqueeze(3).broadcast_to([P, NC, H2, E2]), ALU.mult)\
                   .then_inc(v_blocks_ready, 1)

            def mask_term(i):
                dve.wait_ge(mask_in, at(i, 16, 16))
                dve.tensor_scalar(neg[:, :, :], mask_i[:, :, :], 1.0, -MASKED, ALU.subtract, ALU.mult)\
                   .then_inc(neg_ready, 1)
                dve.wait_ge(neg_ready, at(i, 1, 1))

            def gate_first(i):
                dve.wait_ge(rms_ready, at(i, 1, 1))
                dve.tensor_scalar(rms[:, :], rms[:, :], 2 * RMS_EPS, None, ALU.add).then_inc(rms_eps_added, 1)
                dve.wait_ge(rms_eps_added, at(i, 1, 1))
                dve.reciprocal(rms_inv[:, :], rms[:, :]).then_inc(rms_inv_ready, 1)
                dve.wait_ge(rms_inv_ready, at(i, 1, 1))
                dve.wait_ge(u_scaled_ready, at(i, 1, 1))
                for b in range(GB):
                    dve.scalar_tensor_tensor(out=gated[:, b, :], in0=by_batch(first_b)[:, b, :],
                                             scalar=rms_inv[:, b:b + 1],
                                             in1=u_scaled[:, b, :], op0=ALU.mult, op1=ALU.mult)\
                       .then_inc(gated_ready, 1)

            def row_moments(i, y_ready, y, st, mo, ve, mom_ready):
                dve.wait_ge(y_ready, at(i, 1, 1))
                for b in range(GB):
                    dve.bn_stats(st[:, b, :], y[:, b, :]).then_inc(mom_ready, 1)
                dve.wait_ge(mom_ready, at(i, 2 * GB + 1, GB))
                wait_carrier()
                for b in range(GB):
                    dve.bn_aggr(mo[:, b, :], st[:, b, :]).then_inc(mom_ready, 1)
                dve.wait_ge(mom_ready, at(i, 2 * GB + 1, 2 * GB))
                dve.tensor_scalar(ve[:, :], mo[:, :, 1], LN_EPS, None, ALU.add).then_inc(mom_ready, 1)

            def normal_rows(i, rstd_ready, y, mo, rs, dst, dst_ready):
                dve.wait_ge(rstd_ready, at(i, 1, 1))
                for b in range(GB):
                    dve.tensor_scalar(dst[:, b, :], y[:, b, :], mo[:, b, 0:1], rs[:, b:b + 1],
                                      ALU.subtract, ALU.mult).then_inc(dst_ready, 1)

            def moments_first(i):
                dve.wait_ge(proj1_done, at(i, 1, 1))
                dve.wait_ge(x_bo_ready, at(i, 1, 1))
                dve.tensor_tensor(y1[:, :, :], by_batch(first_a), x_bo[:, :, :], ALU.add).then_inc(y1_ready, 1)
                row_moments(i, y1_ready, y1, stats1, moments1, var_eps1, mom1_ready)

            def normal_first(i):
                dve.wait_ge(x1T_done, at(i, 1, 0))
                dve.wait_ge(x1_bo_ready, at(i, 1, 0))
                normal_rows(i, rstd1_ready, y1, moments1, rstd1, x1, x1_ready)

            def moments_second(i):
                dve.wait_ge(proj2_done, at(i, 1, 1))
                dve.wait_ge(x1_bo_ready, at(i, 1, 1))
                dve.tensor_tensor(y2[:, :, :], by_batch(shared("projection", 0)), x1_bo[:, :, :], ALU.add)\
                   .then_inc(y2_ready, 1)
                row_moments(i, y2_ready, y2, stats2, moments2, var_eps2, mom2_ready)

            def normal_second(i):
                dve.wait_ge(x2T_done, at(i, 1, 0))
                dve.wait_ge(kept_ready, at(i, 1, 0))
                normal_rows(i, rstd2_ready, y2, moments2, rstd2, x2, x2_ready)

            def moments_third(i):
                dve.wait_ge(moe_back, at(i, 1, 1))
                dve.wait_ge(kept_ready, at(i, 1, 1))
                dve.tensor_tensor(y3[:, :, :], by_batch(experts_pair[1]), x2_kept[:, :, :], ALU.add)\
                   .then_inc(y3_ready, 1)
                row_moments(i, y3_ready, y3, stats3, moments3, var_eps3, mom3_ready)

            def normal_third(i):
                dve.wait_ge(out_written, at(i, 16, 0))
                normal_rows(i, rstd3_ready, y3, moments3, rstd3, y_out, out_ready)

            def add_mask(i, b, g):
                h0, h1 = HEADS_OF[g]
                n = NLG * b + g
                if g == 0:
                    dve.wait_ge(prob_ready, at(i, GB, b - 1))
                    dve.wait_ge(sum_ready, at(i, GB, b - 1))
                dve.wait_ge(logits_done, at(i, NLG * GB, n + 1))
                dve.tensor_tensor(logit[:, b % 2, h0:h1, :],
                                  shared("logits", n)[:, 0:SK * (h1 - h0)].rearrange("p (h k) -> p h k", k=SK),
                                  neg[:, b, :].unsqueeze(1).broadcast_to([P, h1 - h0, SK]),
                                  ALU.add).then_inc(logit_ready, 1)

            def negated_max(i, b):
                dve.wait_ge(logit_ready, at(i, NLG * GB, NLG * (b + 1)))
                dve.tensor_reduce(neg_max[:, b % 2, :], logit[:, b % 2, :, :], X, ALU.max, negate=True)\
                   .then_inc(max_ready, 1)

            def sum_probs(i, b):
                dve.wait_ge(exp2_ready, at(i, GB, b + 1))
                dve.tensor_reduce(prob_sum[:, b, :], logit[:, b % 2, :, :], X, ALU.add).then_inc(sum_ready, 1)

            def normalize(i):
                dve.wait_ge(sum_ready, at(i, GB, GB))
                dve.reciprocal(prob_inv[:, :, :], prob_sum[:, :, :]).then_inc(inv_ready, 1)
                dve.wait_ge(inv_ready, at(i, 1, 1))
                dve.wait_ge(pv2_done, at(i, NPT * GB, NPT * GB))
                dve.tensor_tensor(att2[:, :, :].rearrange("p b (h e) -> p (b h) e", e=E2),
                                  second_out[:, 0:T].rearrange("p (n e) -> p n e", e=E2),
                                  heads_of(prob_inv[:, :, :].rearrange("p b h -> p (b h)"), P, GB * H2, E2),
                                  ALU.mult).then_inc(att2_ready, 1)

            def hidden_rows(i, j):
                dve.wait_ge(tanh_g_ready, at(i, NBLK, j + 1))
                dve.scalar_tensor_tensor(out=silu_g[:, j % 2, :], in0=tanh_g[:, j % 2, :], scalar=1.0,
                                         in1=experts_pair[j % 2][:, 0:T], op0=ALU.add, op1=ALU.mult)\
                   .then_inc(silu_ready, 1)
                dve.wait_ge(silu_ready, at(i, NBLK, j + 1))
                if j < 2:
                    dve.wait_ge(down_done, at(i, NBLK, 0))
                else:
                    dve.wait_ge(hidden_w_ready, at(i, NJ, j - 1))
                dve.tensor_tensor(hidden[:, j % 2, :], silu_g[:, j % 2, :], experts_pair[j % 2][:, T:2 * T],
                                  ALU.mult).then_inc(hidden_ready, 1)

            def turn(t):
                i, s, r, m = t, t - 1, t - 2, t - 3
                if runs(t, 1):
                    moments_first(s)
                if runs(t, 3):
                    hidden_rows(m, 0)
                    hidden_rows(m, 1)
                if runs(t, 1):
                    normal_first(s)
                if runs(t, 2):
                    sum_probs(r, 1)
                if runs(t, 3):
                    hidden_rows(m, 2)
                if runs(t, 0):
                    x_low(i)
                if runs(t, 3):
                    hidden_rows(m, 3)
                if runs(t, 1):
                    values_bias(s)
                if runs(t, 2):
                    normalize(r)
                if runs(t, 1):
                    add_mask(s, 0, 0)
                if runs(t, 3):
                    hidden_rows(m, 4)
                if runs(t, 1):
                    add_mask(s, 0, 1)
                    add_mask(s, 0, 2)
                    negated_max(s, 0)
                if runs(t, 3):
                    hidden_rows(m, 5)
                if runs(t, 0):
                    elu(i)
                    add_uv_bias(i)
                if runs(t, 1):
                    add_mask(s, 1, 0)
                if runs(t, 2):
                    moments_second(r)
                if runs(t, 0):
                    silu_uv(i)
                if runs(t, 3):
                    hidden_rows(m, 6)
                if runs(t, 1):
                    add_mask(s, 1, 1)
                if runs(t, 0):
                    mask_energy(i, 0, 0)
                if runs(t, 2):
                    normal_second(r)
                if runs(t, 1):
                    add_mask(s, 1, 2)
                if runs(t, 3):
                    hidden_rows(m, 7)
                if runs(t, 0):
                    mask_energy(i, 0, 1)
                if runs(t, 1):
                    negated_max(s, 1)
                if runs(t, 0):
                    mask_term(i)
                    mask_energy(i, 1, 0)
                if runs(t, 3):
                    hidden_rows(m, 8)
                if runs(t, 1):
                    spread_values(s, 0)
                if runs(t, 0):
                    mask_energy(i, 1, 1)
                if runs(t, 2):
                    route(r)
                    combine_split(r)
                if runs(t, 3):
                    moments_third(m)
                if runs(t, 1):
                    spread_values(s, 1)
                if runs(t, 0):
                    gate_first(i)
                if runs(t, 2):
                    x2_low(r)
                if runs(t, 1):
                    sum_probs(s, 0)
                if runs(t, 3):
                    normal_third(m)

            dve.wait_ge(weights1_in, ALL1)
            dve.wait_ge(consts_pool, 12)
            dve.tensor_scalar(half_scale[:, :], half_scale[:, :], 0.5, None, ALU.mult).then_inc(consts_dve, 1)
            dve.tensor_copy(expert_no[:, :], expert_i[:, :]).then_inc(consts_dve, 1)
            dve.wait_ge(consts_dve, 2)
            split_weights([(w_qT[:, :], w_q_parts), (w_kT[:, :], w_k_parts), (w_uvT[:, :], w_uv_parts)],
                          weights_hi_ready, weights_lo_ready, 0)
            dve.wait_ge(chunk_heads_ready, 3)
            turn(0)
            dve.wait_ge(weights2_in, ALL2)
            dve.wait_ge(weights3_in, ALL3)
            split_weights([(w_gate[:, :, :], w_gate_parts), (w_up[:, :, :], w_up_parts)],
                          weights_hi_ready, weights_lo_ready, 3)
            turn(1)
            turn(2)
            turn(3)
            with dve.Fori(4, NG) as t:
                turn(t)
            for t in range(NG, NG + 3):
                turn(t)

        @block.gpsimd
        def _(pool):
            def constants():
                pool.memset(ones[:, :], 1.0).then_inc(consts_pool, 1)
                pool.memset(half_power[:, :], 0.5).then_inc(consts_pool, 1)
                pool.memset(minus_half_power[:, :], -0.5).then_inc(consts_pool, 1)
                pool.memset(pick_expert[:, :, :], 0.0).then_inc(consts_pool, 1)
                pool.iota(expert_i[:, :], pattern=[[1, NE]], base=0, channel_multiplier=0).then_inc(consts_pool, 1)
                pool.wait_ge(consts_pool, 5)
                for dst in (ident, ident16):
                    pool.affine_select(out=dst[:, :], in_=ones[:, :], compare_op=ALU.is_equal, fill=0.0, base=0,
                                       pattern=[[-1, D]], channel_multiplier=1).then_inc(consts_pool, 1)
                pool.affine_select(out=causal[:, :], in_=ones[:, :], compare_op=ALU.is_ge, fill=0.0, base=0,
                                   pattern=[[1, D]], channel_multiplier=-1).then_inc(consts_pool, 1)
                for dst, h, e in ((head_rows1, H1, E1), (head_rows2, H2, E2)):
                    pool.affine_select(out=dst[:, :], in_=ones[:, 0:h], compare_op=ALU.is_ge, fill=0.0, base=0,
                                       pattern=[[-e, h]], channel_multiplier=1).then_inc(consts_pool, 1)
                pool.wait_ge(consts_pool, 10)
                for dst, h, e in ((head_rows1, H1, E1), (head_rows2, H2, E2)):
                    pool.affine_select(out=dst[:, :], in_=dst[:, :], compare_op=ALU.is_ge, fill=0.0, base=e - 1,
                                       pattern=[[e, h]], channel_multiplier=-1).then_inc(consts_pool, 1)
                for b in range(2):
                    pool.memset(shifted[:, b, H2 * SK:NC * P], 0.0).then_inc(fill_ready, 1)
                for b in range(GB):
                    pool.memset(v_rows[:, b, NC - 1, :], 0.0).then_inc(fill_ready, 1)
                pool.memset(chunk_heads[:, :, :], 1.0).then_inc(chunk_heads_ready, 1)
                pool.wait_ge(chunk_heads_ready, 1)
                pool.affine_select(out=chunk_heads[:, :, :], in_=chunk_heads[:, :, :], compare_op=ALU.is_ge, fill=0.0,
                                   base=0, pattern=[[P, NC], [-SK, H2]], channel_multiplier=1)\
                    .then_inc(chunk_heads_ready, 1)
                pool.wait_ge(chunk_heads_ready, 2)
                pool.affine_select(out=chunk_heads[:, :, :], in_=chunk_heads[:, :, :], compare_op=ALU.is_ge, fill=0.0,
                                   base=SK - 1, pattern=[[-P, NC], [SK, H2]], channel_multiplier=-1)\
                    .then_inc(chunk_heads_ready, 1)
                for s in range(3):
                    pool.affine_select(
                        out=pick_expert[:, :, :].rearrange("p j (t f) -> p j t f", f=FE),
                        in_=pick_expert[:, :, :].rearrange("p j (t f) -> p j t f", f=FE),
                        compare_op=ALU.not_equal, fill=1.0, base=-NE * s,
                        pattern=[[-2, NJ], [-1, 2], [0, FE]], channel_multiplier=1).then_inc(pick_ready, 1)
                    pool.wait_ge(pick_ready, s + 1)

            def query_heads(i, b):
                if b == 0:
                    pool.wait_ge(qk1_ready, at(i, 2, 1))
                pool.wait_ge(energy_done, at(i, 2 * GB, 2 * (b - 1)))
                pool.tensor_tensor(q1_heads[:, b % 2, :, :],
                                   q1[:, P * b:P * b + P].unsqueeze(1).broadcast_to([P, H1, P]),
                                   heads_of(head_rows1[:, :], P, H1, P), ALU.mult).then_inc(q1_heads_ready, 1)

            def gate_scale(i):
                pool.wait_ge(uv_ready, at(i, 1, 1))
                pool.wait_ge(gated_ready, at(i, GB, 0))
                pool.tensor_tensor(u_scaled[:, :, :], uv[:, :, 0:D],
                                   half_scale[:, :].unsqueeze(1).broadcast_to([P, GB, D]), ALU.mult)\
                    .then_inc(u_scaled_ready, 1)

            def add_bo(i):
                pool.wait_ge(x_in, at(i, 16, 16))
                pool.wait_ge(y1_ready, at(i, 1, 0))
                pool.tensor_tensor(x_bo[:, :, :], x_tok[:, :, :], b_o[:, :].unsqueeze(1).broadcast_to([P, GB, D]),
                                   ALU.add).then_inc(x_bo_ready, 1)

            def key_heads(i, b):
                pool.wait_ge(k2_ready, at(i, 1, 1))
                pool.wait_ge(logits_done, at(i, NLG * GB, 0))
                pool.tensor_tensor(k2_heads[:, b, :, :],
                                   k2_T[:, SK * b:SK * b + SK].unsqueeze(1).broadcast_to([P, H2, SK]),
                                   heads_of(head_rows2[:, :], P, H2, SK), ALU.mult)\
                    .then_inc(k2_heads_ready, 1)

            def root_first(i):
                pool.wait_ge(sumsq_ready, at(i, GB, GB))
                pool.tensor_tensor(rms[:, :], sumsq[:, :], half_power[:, :], ALU.pow).then_inc(rms_ready, 1)

            def inverse_root(i, mom_ready, ve, rs, ready):
                pool.wait_ge(mom_ready, at(i, 2 * GB + 1, 2 * GB + 1))
                pool.tensor_tensor(rs[:, :], ve[:, :], minus_half_power[:, :], ALU.pow).then_inc(ready, 1)

            def root_norm1(i):
                inverse_root(i, mom1_ready, var_eps1, rstd1, rstd1_ready)

            def root_norm2(i):
                inverse_root(i, mom2_ready, var_eps2, rstd2, rstd2_ready)

            def root_norm3(i):
                inverse_root(i, mom3_ready, var_eps3, rstd3, rstd3_ready)

            def add_xbo(i):
                pool.wait_ge(x1_ready, at(i, GB, GB))
                pool.wait_ge(y2_ready, at(i, 1, 0))
                pool.tensor_tensor(x1_bo[:, :, :], x1[:, :, :], b_xo[:, :].unsqueeze(1).broadcast_to([P, GB, D]),
                                   ALU.add).then_inc(x1_bo_ready, 1)

            def shift(i, b):
                pool.wait_ge(max_ready, at(i, GB, b + 1))
                pool.wait_ge(probT_done, at(i, NPT * GB, NPT * (b - 1)))
                pool.tensor_tensor(shifted[:, b % 2, 0:H2 * SK].rearrange("p (h k) -> p h k", k=SK),
                                   logit[:, b % 2, :, :],
                                   heads_of(neg_max[:, b % 2, :], P, H2, SK), ALU.add)\
                    .then_inc(shifted_ready, 1)

            def group_prob(i, b):
                if b == 0:
                    pool.wait_ge(gp_in, at(i, 16, 16))
                pool.wait_ge(exp2_ready, at(i, GB, b + 1))
                pool.tensor_tensor(shifted[:, b % 2, 0:H2 * SK].rearrange("p (h k) -> p h k", k=SK),
                                   logit[:, b % 2, :, :],
                                   gprob[:, b, :].unsqueeze(1).broadcast_to([P, H2, SK]), ALU.mult)\
                    .then_inc(prob_ready, 1)

            def weight_hidden(i, j):
                pool.wait_ge(hidden_ready, at(i, NBLK, j + 1))
                pool.wait_ge(rows_ready, at(i, NROWS, NROWS))
                pool.wait_ge(down_done, at(i, NBLK, j - 1 if j >= 2 else 0))
                pool.tensor_tensor(hidden_w[:, j % 2, :], hidden[:, j % 2, :], weight_rows[:, j, :], ALU.mult)\
                    .then_inc(hidden_w_ready, 1)

            def turn(t):
                i, s, r, m = t, t - 1, t - 2, t - 3
                if runs(t, 1):
                    shift(s, 0)
                if runs(t, 0):
                    query_heads(i, 0)
                if runs(t, 2):
                    root_norm2(r)
                if runs(t, 3):
                    weight_hidden(m, 5)
                if runs(t, 0):
                    query_heads(i, 1)
                if runs(t, 3):
                    weight_hidden(m, 6)
                if runs(t, 1):
                    group_prob(s, 0)
                if runs(t, 0):
                    gate_scale(i)
                if runs(t, 3):
                    weight_hidden(m, 7)
                if runs(t, 1):
                    shift(s, 1)
                    group_prob(s, 1)
                if runs(t, 0):
                    root_first(i)
                    add_bo(i)
                if runs(t, 3):
                    root_norm3(m)
                if runs(t, 0):
                    key_heads(i, 0)
                if runs(t, 1):
                    add_xbo(s)
                if runs(t, 0):
                    root_norm1(i)
                if runs(t, 2):
                    weight_hidden(r, 0)
                    weight_hidden(r, 1)
                    weight_hidden(r, 2)
                if runs(t, 0):
                    key_heads(i, 1)
                if runs(t, 2):
                    weight_hidden(r, 3)
                    weight_hidden(r, 4)

            constants()
            pool.wait_ge(weights1_in, ALL1)
            turn(0)
            pool.wait_ge(weights2_in, ALL2)
            turn(1)
            pool.wait_ge(weights3_in, ALL3)
            turn(2)
            turn(3)
            with pool.Fori(4, NG) as t:
                turn(t)
            for t in range(NG, NG + 3):
                turn(t)


def kernel(x, ctx_1024, fside_BxSxS2_0, mask_BxSxS2_ik1, L0_attn_Wq, L0_attn_bq, L0_attn_Wk, L0_attn_bk,
           L0_attn_Wv, L0_attn_bv, L0_attn_Wu, L0_attn_bu, L0_attn_Wo, L0_attn_bo, L0_attn_scale,
           L0_xattn_wq_k, L0_xattn_wq_b, L0_xattn_wk_k, L0_xattn_wk_b, L0_xattn_wv_k, L0_xattn_wv_b,
           L0_xattn_wo_k, L0_xattn_wo_b, L0_ffn_router_w, L0_ffn_router_bias, L0_ffn_up_proj,
           L0_ffn_gate_proj, L0_ffn_down_proj, L0_ffn_sh_gate, L0_ffn_sh_up, L0_ffn_sh_down):
    import numpy as np
    import concourse.bacc as bacc
    from concourse.bass_utils import run_bass_kernel_spmd

    def laid(a, *axes):
        return np.ascontiguousarray(np.transpose(np.asarray(a), axes) if axes else np.asarray(a))

    nb, s, d = x.shape
    arrays = {
        "x": laid(x),
        "xT": laid(x, 2, 0, 1).reshape(d, nb * s),
        "ctxT": laid(ctx_1024, 2, 0, 1),
        "gp": laid(fside_BxSxS2_0),
        "mask": laid(mask_BxSxS2_ik1),
        "wqT": laid(L0_attn_Wq, 1, 0),
        "wkT": laid(L0_attn_Wk, 1, 0),
        "wuvT": np.concatenate([laid(L0_attn_Wu, 1, 0), laid(L0_attn_Wv, 1, 0)], axis=1),
        "woT": laid(L0_attn_Wo, 1, 0),
        "bq": laid(L0_attn_bq), "bk": laid(L0_attn_bk), "bu": laid(L0_attn_bu), "bv": laid(L0_attn_bv),
        "bo": laid(L0_attn_bo), "scale": laid(L0_attn_scale),
        "xwq": laid(L0_xattn_wq_k), "xbq": laid(L0_xattn_wq_b),
        "xwk": laid(L0_xattn_wk_k), "xbk": laid(L0_xattn_wk_b),
        "xwv": laid(L0_xattn_wv_k), "xbv": laid(L0_xattn_wv_b),
        "xwo": laid(L0_xattn_wo_k), "xbo": laid(L0_xattn_wo_b),
        "routerT": laid(L0_ffn_router_w, 1, 0), "router_b": laid(L0_ffn_router_bias),
        "up": laid(L0_ffn_up_proj), "gate": laid(L0_ffn_gate_proj), "down": laid(L0_ffn_down_proj),
        "sh_gateT": laid(L0_ffn_sh_gate, 1, 0), "sh_upT": laid(L0_ffn_sh_up, 1, 0),
        "sh_downT": laid(L0_ffn_sh_down, 1, 0),
    }
    nc = bacc.Bacc("TRN2", target_bir_lowering=False, num_devices=1)
    args = {n: nc.dram_tensor(f"in_{n}", a.shape, mybir.dt.from_np(a.dtype), kind="ExternalInput").ap()
            for n, a in arrays.items()}
    args["v_scratch"] = nc.dram_tensor("v_scratch", (GB, H2 * ctx_1024.shape[1], E2), F32).ap()
    args["out"] = nc.dram_tensor("out_x", (nb, s, d), F32, kind="ExternalOutput").ap()
    decoder_layer(nc, **args)
    r = run_bass_kernel_spmd(nc, [{f"in_{n}": a for n, a in arrays.items()}], core_ids=[0])
    return r.results[0]["out_x"]
```
